# Optimizing a Trainium2 kernel written in Bass

```python
import numpy as np
import jax
import jax.numpy as jnp

def _softmax(x, axis=-1):
    return jax.nn.softmax(x, axis=axis)

def _gelu(x):
    return jax.nn.gelu(x, approximate=True)

def _silu(x):
    return jax.nn.silu(x)

def _sigmoid(x):
    return jax.nn.sigmoid(x)

def _layernorm(x, axis=-1, eps=1e-05):
    m = jnp.mean(x, axis=axis, keepdims=True)
    v = jnp.var(x, axis=axis, keepdims=True)
    return (x - m) / jnp.sqrt(v + eps)

def _scatter_add(tgt, idx, src, axis=0):
    return tgt.at[idx].add(src)

def _segment_sum(src, seg, n):
    return jax.ops.segment_sum(src, seg, n)
kernel_name = 'mk_gnn_resnorm_d4_gnn_r32_f94581'

def setup_inputs(seed: int=0):
    np.random.seed(seed)
    _w = jnp.asarray

    def _rec_inputs():
        import jax
        import jax.numpy as jnp
        _gk = jax.random.key(seed)
        x = -0.000202 + 1 * jax.random.normal(jax.random.fold_in(_gk, 1), (3125, 64), jnp.float32)
        _s = jax.random.randint(jax.random.fold_in(_gk, 2), (50000,), 0, 3125, jnp.int32)
        _d = jax.random.randint(jax.random.fold_in(_gk, 3), (50000,), 0, 3125, jnp.int32)
        _loop = jnp.arange(3125, dtype=jnp.int32)
        src = jnp.concatenate([_s, _d, _loop])
        dst = jnp.concatenate([_d, _s, _loop])
        _o = jnp.argsort(dst, stable=True)
        src = src[_o]
        dst = dst[_o]
        edge_attr_3 = 0.00117183 + 1.0004 * jax.random.normal(jax.random.fold_in(_gk, 12), (103125, 3), jnp.float32)
        return (x, src, dst, edge_attr_3)
    x, src, dst, edge_attr_3 = _rec_inputs()

    def _L0_gnn_setup():
        import jax, jax.numpy as jnp
        import numpy as np
        EPS = 1e-15
        CLIP = 0.98
        N_NODES = 3125
        N_EDGES = 50000
        D_IN = 64
        D_OUT = 64

        def _norm(x):
            return jnp.sqrt(jnp.sum(x * x, axis=1, keepdims=True))

        def _forward(h, W, c, edge_index):
            N = h.shape[0]
            f = h + EPS
            f = f * CLIP / jnp.maximum(CLIP, _norm(f))
            fn = _norm(f)
            p = jnp.tanh(fn) * f / fn
            sqrt_c = jnp.sqrt(c)
            p = p + EPS
            p = p * CLIP / jnp.maximum(CLIP, _norm(p))
            Mp = p @ W
            pn = _norm(p)
            atan_norm = jnp.arctanh(jnp.clip(sqrt_c * pn, -0.9, 0.9))
            t = Mp * atan_norm / pn / sqrt_c
            clip2 = CLIP / sqrt_c
            t = t * clip2 / jnp.maximum(clip2, _norm(t))
            tn = _norm(t)
            hh = jnp.tanh(sqrt_c * tn) / sqrt_c / tn * t
            row, col = (edge_index[0], edge_index[1])
            u = -hh[row]
            v = hh[col]
            c0 = c[0]
            sqrt_c0 = jnp.sqrt(c0)
            nu = jnp.sum(u * u, axis=1)
            nv = jnp.sum(v * v, axis=1)
            duv = jnp.sum(u * v, axis=1)
            coef1 = 1.0 + 2.0 * c0 * duv + c0 * nv
            coef2 = 1.0 - c0 * nu
            den = 1.0 + 2.0 * c0 * duv + c0 * c0 * nu * nv
            ma = (coef1[:, None] * u + coef2[:, None] * v) / den[:, None]
            rn = jnp.sqrt(jnp.sum(ma * ma, axis=1))
            e = -2.0 / sqrt_c0 * jnp.arctanh(jnp.clip(sqrt_c0 * rn, 1e-08, CLIP))
            e_max = jax.ops.segment_max(e, row, num_segments=N)
            e_max = jnp.where(jnp.isfinite(e_max), e_max, 0.0)
            ex = jnp.exp(e - e_max[row])
            denom = jax.ops.segment_sum(ex, row, num_segments=N)
            attention = ex / (denom[row] + 1e-16)
            g = hh + EPS
            g = g * CLIP / jnp.maximum(CLIP, _norm(g))
            gn = _norm(g)
            log_h = jnp.arctanh(jnp.clip(sqrt_c * gn, -0.9, 0.9)) * g / gn
            weighted = sqrt_c0 * attention[:, None] * log_h[col]
            att_log_h = jax.ops.segment_sum(weighted, row, num_segments=N)
            z = jax.nn.elu(att_log_h) + EPS
            clip3 = CLIP / sqrt_c
            z = z * clip3 / jnp.maximum(clip3, _norm(z))
            zn = _norm(z)
            h_prime = jnp.tanh(sqrt_c * zn) * z / sqrt_c / zn
            return h_prime
        key = jax.random.key(seed)
        k1, k2, k3 = jax.random.split(key, 3)
        h = jax.random.normal(k1, (N_NODES, D_IN), dtype=jnp.float32)
        limit = 1.414 * np.sqrt(6.0 / (D_IN + D_OUT))
        W = jax.random.uniform(k2, (D_IN, D_OUT), dtype=jnp.float32, minval=-limit, maxval=limit)
        c = jnp.array([1.0], dtype=jnp.float32)
        edge_index = jax.random.randint(k3, (2, N_EDGES), 0, N_NODES, dtype=jnp.int32)
        return {'h': h, 'W': W, 'c': c, 'edge_index': edge_index}
    _L0_gnn_all = _L0_gnn_setup()
    _L0_gnn_in = {k: v for k, v in _L0_gnn_all.items() if k in ('W', 'c')}
    del _L0_gnn_all

    def _L1_gnn_setup():
        import jax, jax.numpy as jnp
        import numpy as np
        N_NODES = 3125
        D_FEAT = 64
        AVG_DEG = 16
        ALPHA = 0.2
        key = jax.random.key(seed)
        k1, k2, k3 = jax.random.split(key, 3)
        N, D, E = (N_NODES, D_FEAT, N_NODES * AVG_DEG)
        inputs = jax.random.normal(k1, (N, D), dtype=jnp.float32)
        src = jnp.repeat(jnp.arange(N, dtype=jnp.int32), AVG_DEG)
        dst = jax.random.randint(k2, (E,), 0, N, dtype=jnp.int32)
        edge_index = jnp.stack([src, dst], axis=0)
        W = jnp.ones((D,), dtype=jnp.float32)
        stdv = 1.0 / np.sqrt(2.0 * D)
        a = jax.random.uniform(k3, (2 * D,), dtype=jnp.float32, minval=-stdv, maxval=stdv)
        return {'inputs': inputs, 'W': W, 'a': a, 'edge_index': edge_index}
    _L1_gnn_all = _L1_gnn_setup()
    _L1_gnn_in = {k: v for k, v in _L1_gnn_all.items() if k in ('W', 'a')}
    del _L1_gnn_all

    def _L2_gnn_setup():
        import jax, jax.numpy as jnp
        import numpy as np
        M = 50000
        E = 25000
        C_IN = 64
        C_OUT = 64
        DIM = 3
        RADIUS = 1.0
        EPS = 1e-05

        def layer_norm(x, g, b):
            mu = jnp.mean(x, axis=-1, keepdims=True)
            var = jnp.mean((x - mu) ** 2, axis=-1, keepdims=True)
            return (x - mu) * jax.lax.rsqrt(var + EPS) * g + b
        key = jax.random.key(seed)
        ks = jax.random.split(key, 12)
        inv = 1.0 / np.sqrt(C_OUT)
        return {'source': jax.random.randint(ks[0], (E,), 0, M), 'target': jax.random.randint(ks[1], (E,), 0, M), 'features': jax.random.normal(ks[2], (M, C_IN), dtype=jnp.float32), 'hood_coords': jax.random.normal(ks[3], (E, DIM), dtype=jnp.float32), 'Wd1': jax.random.normal(ks[4], (DIM, C_OUT), dtype=jnp.float32) / np.sqrt(DIM), 'bd1': jnp.zeros((C_OUT,), jnp.float32), 'g1': jnp.ones((C_OUT,), jnp.float32), 'b1': jnp.zeros((C_OUT,), jnp.float32), 'Wd2': jax.random.normal(ks[5], (C_OUT, C_OUT), dtype=jnp.float32) * inv, 'bd2': jnp.zeros((C_OUT,), jnp.float32), 'g2': jnp.ones((C_OUT,), jnp.float32), 'b2': jnp.zeros((C_OUT,), jnp.float32), 'W1': jax.random.normal(ks[6], (C_IN, C_OUT), dtype=jnp.float32) / np.sqrt(C_IN), 'W2': jax.random.normal(ks[7], (C_IN, C_OUT), dtype=jnp.float32) / np.sqrt(C_IN), 'W3': jax.random.normal(ks[8], (C_IN, C_OUT), dtype=jnp.float32) / np.sqrt(C_IN)}
    _L2_gnn_all = _L2_gnn_setup()
    _L2_gnn_in = {k: v for k, v in _L2_gnn_all.items() if k in ('Wd1', 'bd1', 'g1', 'b1', 'Wd2', 'bd2', 'g2', 'b2', 'W1', 'W2', 'W3')}
    del _L2_gnn_all

    def _L3_gnn_setup():
        import jax, jax.numpy as jnp
        import numpy as np
        N_NODES = 3125
        N_EDGES = 50000
        IN_C, HID_C, OUT_C = (64, 128, 64)
        EPS = 1e-12

        def _sage_conv(x, edge_index, W_l, W_r, b, normalize):
            src, dst = (edge_index[0], edge_index[1])
            n = x.shape[0]
            agg = jax.ops.segment_sum(x[src], dst, num_segments=n)
            cnt = jax.ops.segment_sum(jnp.ones((src.shape[0],), x.dtype), dst, num_segments=n)
            mean = agg / jnp.maximum(cnt, 1.0)[:, None]
            out = mean @ W_l + x @ W_r + b
            if normalize:
                norm = jnp.linalg.norm(out, axis=-1, keepdims=True)
                out = out / jnp.maximum(norm, EPS)
            return out
        key = jax.random.key(seed)
        ks = jax.random.split(key, 8)
        s = 0.05
        return {'x': jax.random.normal(ks[0], (N_NODES, IN_C), dtype=jnp.float32), 'edge_index': jax.random.randint(ks[1], (2, N_EDGES), 0, N_NODES, dtype=jnp.int64), 'W1_l': jax.random.normal(ks[2], (IN_C, HID_C), dtype=jnp.float32) * s, 'W1_r': jax.random.normal(ks[3], (IN_C, HID_C), dtype=jnp.float32) * s, 'b1': jnp.zeros((HID_C,), dtype=jnp.float32), 'W3_l': jax.random.normal(ks[4], (HID_C, OUT_C), dtype=jnp.float32) * s, 'W3_r': jax.random.normal(ks[5], (HID_C, OUT_C), dtype=jnp.float32) * s, 'b3': jnp.zeros((OUT_C,), dtype=jnp.float32)}
    _L3_gnn_all = _L3_gnn_setup()
    _L3_gnn_in = {k: v for k, v in _L3_gnn_all.items() if k in ('W1_l', 'W1_r', 'b1', 'W3_l', 'W3_r', 'b3')}
    del _L3_gnn_all
    return {'x': x, 'src': src, 'dst': dst, 'edge_attr_3': edge_attr_3, 'L0_gnn_W': _L0_gnn_in['W'], 'L0_gnn_c': _L0_gnn_in['c'], 'L1_gnn_W': _L1_gnn_in['W'], 'L1_gnn_a': _L1_gnn_in['a'], 'L2_gnn_Wd1': _L2_gnn_in['Wd1'], 'L2_gnn_bd1': _L2_gnn_in['bd1'], 'L2_gnn_g1': _L2_gnn_in['g1'], 'L2_gnn_b1': _L2_gnn_in['b1'], 'L2_gnn_Wd2': _L2_gnn_in['Wd2'], 'L2_gnn_bd2': _L2_gnn_in['bd2'], 'L2_gnn_g2': _L2_gnn_in['g2'], 'L2_gnn_b2': _L2_gnn_in['b2'], 'L2_gnn_W1': _L2_gnn_in['W1'], 'L2_gnn_W2': _L2_gnn_in['W2'], 'L2_gnn_W3': _L2_gnn_in['W3'], 'L3_gnn_W1_l': _L3_gnn_in['W1_l'], 'L3_gnn_W1_r': _L3_gnn_in['W1_r'], 'L3_gnn_b1': _L3_gnn_in['b1'], 'L3_gnn_W3_l': _L3_gnn_in['W3_l'], 'L3_gnn_W3_r': _L3_gnn_in['W3_r'], 'L3_gnn_b3': _L3_gnn_in['b3']}

def reference(x, src, dst, edge_attr_3, L0_gnn_W, L0_gnn_c, L1_gnn_W, L1_gnn_a, L2_gnn_Wd1, L2_gnn_bd1, L2_gnn_g1, L2_gnn_b1, L2_gnn_Wd2, L2_gnn_bd2, L2_gnn_g2, L2_gnn_b2, L2_gnn_W1, L2_gnn_W2, L2_gnn_W3, L3_gnn_W1_l, L3_gnn_W1_r, L3_gnn_b1, L3_gnn_W3_l, L3_gnn_W3_r, L3_gnn_b3):
    import jax
    import jax.numpy as jnp

    def _L0_gnn_ref(h, W, c, edge_index):
        import jax, jax.numpy as jnp
        import numpy as np
        EPS = 1e-15
        CLIP = 0.98
        N_NODES = 3125
        N_EDGES = 50000
        D_IN = 64
        D_OUT = 64

        def _norm(x):
            return jnp.sqrt(jnp.sum(x * x, axis=1, keepdims=True))

        def _forward(h, W, c, edge_index):
            N = h.shape[0]
            f = h + EPS
            f = f * CLIP / jnp.maximum(CLIP, _norm(f))
            fn = _norm(f)
            p = jnp.tanh(fn) * f / fn
            sqrt_c = jnp.sqrt(c)
            p = p + EPS
            p = p * CLIP / jnp.maximum(CLIP, _norm(p))
            Mp = p @ W
            pn = _norm(p)
            atan_norm = jnp.arctanh(jnp.clip(sqrt_c * pn, -0.9, 0.9))
            t = Mp * atan_norm / pn / sqrt_c
            clip2 = CLIP / sqrt_c
            t = t * clip2 / jnp.maximum(clip2, _norm(t))
            tn = _norm(t)
            hh = jnp.tanh(sqrt_c * tn) / sqrt_c / tn * t
            row, col = (edge_index[0], edge_index[1])
            u = -hh[row]
            v = hh[col]
            c0 = c[0]
            sqrt_c0 = jnp.sqrt(c0)
            nu = jnp.sum(u * u, axis=1)
            nv = jnp.sum(v * v, axis=1)
            duv = jnp.sum(u * v, axis=1)
            coef1 = 1.0 + 2.0 * c0 * duv + c0 * nv
            coef2 = 1.0 - c0 * nu
            den = 1.0 + 2.0 * c0 * duv + c0 * c0 * nu * nv
            ma = (coef1[:, None] * u + coef2[:, None] * v) / den[:, None]
            rn = jnp.sqrt(jnp.sum(ma * ma, axis=1))
            e = -2.0 / sqrt_c0 * jnp.arctanh(jnp.clip(sqrt_c0 * rn, 1e-08, CLIP))
            e_max = jax.ops.segment_max(e, row, num_segments=N)
            e_max = jnp.where(jnp.isfinite(e_max), e_max, 0.0)
            ex = jnp.exp(e - e_max[row])
            denom = jax.ops.segment_sum(ex, row, num_segments=N)
            attention = ex / (denom[row] + 1e-16)
            g = hh + EPS
            g = g * CLIP / jnp.maximum(CLIP, _norm(g))
            gn = _norm(g)
            log_h = jnp.arctanh(jnp.clip(sqrt_c * gn, -0.9, 0.9)) * g / gn
            weighted = sqrt_c0 * attention[:, None] * log_h[col]
            att_log_h = jax.ops.segment_sum(weighted, row, num_segments=N)
            z = jax.nn.elu(att_log_h) + EPS
            clip3 = CLIP / sqrt_c
            z = z * clip3 / jnp.maximum(clip3, _norm(z))
            zn = _norm(z)
            h_prime = jnp.tanh(sqrt_c * zn) * z / sqrt_c / zn
            return h_prime
        return _forward(h, W, c, edge_index)

    def _L1_gnn_ref(inputs, W, a, edge_index):
        import jax, jax.numpy as jnp
        import numpy as np
        N_NODES = 3125
        D_FEAT = 64
        AVG_DEG = 16
        ALPHA = 0.2
        N, D = inputs.shape
        src, dst = (edge_index[0], edge_index[1])
        h = inputs * W
        s_src = h @ a[:D]
        s_dst = h @ a[D:]
        score = s_src[src] + s_dst[dst]
        edge_e = jnp.exp(jax.nn.leaky_relu(score, negative_slope=ALPHA))
        e_rowsum = jax.ops.segment_sum(edge_e, src, num_segments=N)
        h_prime = jax.ops.segment_sum(edge_e[:, None] * h[dst], src, num_segments=N)
        h_prime = h_prime / e_rowsum[:, None]
        return jax.nn.elu(h_prime)

    def _L2_gnn_ref(source, target, features, hood_coords, Wd1, bd1, g1, b1, Wd2, bd2, g2, b2, W1, W2, W3):
        import jax, jax.numpy as jnp
        import numpy as np
        M = 50000
        E = 25000
        C_IN = 64
        C_OUT = 64
        DIM = 3
        RADIUS = 1.0
        EPS = 1e-05

        def layer_norm(x, g, b):
            mu = jnp.mean(x, axis=-1, keepdims=True)
            var = jnp.mean((x - mu) ** 2, axis=-1, keepdims=True)
            return (x - mu) * jax.lax.rsqrt(var + EPS) * g + b
        m = features.shape[0]
        x = hood_coords / RADIUS
        d = jax.nn.gelu(layer_norm(x @ Wd1 + bd1, g1, b1), approximate=False)
        d = jax.nn.gelu(layer_norm(d @ Wd2 + bd2, g2, b2), approximate=False)
        w1 = features @ W1
        w2 = features @ W2
        w3 = features @ W3
        logits = w1[target] - w2[source] + d
        seg_max = jax.ops.segment_max(logits, target, num_segments=m)
        seg_max = jnp.where(jnp.isfinite(seg_max), seg_max, 0.0)
        e = jnp.exp(logits - seg_max[target])
        denom = jax.ops.segment_sum(e, target, num_segments=m)
        a = e / denom[target]
        out = jax.ops.segment_sum(a * (w3[source] + d), target, num_segments=m)
        return out

    def _L3_gnn_ref(x, edge_index, W1_l, W1_r, b1, W3_l, W3_r, b3):
        import jax, jax.numpy as jnp
        import numpy as np
        N_NODES = 3125
        N_EDGES = 50000
        IN_C, HID_C, OUT_C = (64, 128, 64)
        EPS = 1e-12

        def _sage_conv(x, edge_index, W_l, W_r, b, normalize):
            src, dst = (edge_index[0], edge_index[1])
            n = x.shape[0]
            agg = jax.ops.segment_sum(x[src], dst, num_segments=n)
            cnt = jax.ops.segment_sum(jnp.ones((src.shape[0],), x.dtype), dst, num_segments=n)
            mean = agg / jnp.maximum(cnt, 1.0)[:, None]
            out = mean @ W_l + x @ W_r + b
            if normalize:
                norm = jnp.linalg.norm(out, axis=-1, keepdims=True)
                out = out / jnp.maximum(norm, EPS)
            return out
        h = _sage_conv(x, edge_index, W1_l, W1_r, b1, normalize=True)
        h = jax.nn.relu(h)
        out = _sage_conv(h, edge_index, W3_l, W3_r, b3, normalize=False)
        return out
    edge_index = jnp.stack([src, dst])
    x = _layernorm(x + _L0_gnn_ref(x, L0_gnn_W, L0_gnn_c, edge_index), axis=-1)
    x = _layernorm(x + _L1_gnn_ref(x, L1_gnn_W, L1_gnn_a, edge_index), axis=-1)
    x = _layernorm(x + _L2_gnn_ref(src, dst, x, edge_attr_3, L2_gnn_Wd1, L2_gnn_bd1, L2_gnn_g1, L2_gnn_b1, L2_gnn_Wd2, L2_gnn_bd2, L2_gnn_g2, L2_gnn_b2, L2_gnn_W1, L2_gnn_W2, L2_gnn_W3), axis=-1)
    x = _layernorm(x + _L3_gnn_ref(x, edge_index, L3_gnn_W1_l, L3_gnn_W1_r, L3_gnn_b1, L3_gnn_W3_l, L3_gnn_W3_r, L3_gnn_b3), axis=-1)
    return x

_drawn_inputs = setup_inputs


def setup_inputs(seed=0):
    import zlib

    import numpy as np

    out = dict(_drawn_inputs(seed))
    spreads = {'L1_gnn_W': (1.0, 0.2),
     'L2_gnn_bd1': (0.0, 0.1),
     'L2_gnn_g1': (1.0, 0.2),
     'L2_gnn_b1': (0.0, 0.1),
     'L2_gnn_bd2': (0.0, 0.1),
     'L2_gnn_g2': (1.0, 0.2),
     'L2_gnn_b2': (0.0, 0.1),
     'L3_gnn_b1': (0.0, 0.8),
     'L3_gnn_b3': (0.0, 0.1)}
    factors = {'L2_gnn_W1': 64.0, 'L3_gnn_W1_l': 9.211, 'L3_gnn_W1_r': 4.382}
    for name, (base, spread) in spreads.items():
        noise = np.random.default_rng([zlib.crc32(name.encode()), seed]).standard_normal(out[name].shape)
        drawn = base * np.exp(spread * noise) if base else spread * noise
        out[name] = jnp.asarray(drawn.astype(out[name].dtype))
    for name, factor in factors.items():
        out[name] = (out[name] * factor).astype(out[name].dtype)
    return out
```

```python
from contextlib import ExitStack

import concourse.bass as bass
import numpy as np
from concourse import mybir

P = 128
N = 3125
E = 103125
F = 64
NBK = -(-N // P)
NP = NBK * P
PADN = NP - 1
CT = 4
NCH = -(-E // (2 * CT * P))
NT = 2 * CT * NCH
HT = NT // 2
EP = NT * P
NG = -(-NT // P)
NPAIR = NT // 2
CUTS = (1, 3, 4, 5, 7)
LEAST = 9
BANK = 512
SPANS = [(k * BANK, min(BANK, NP - k * BANK)) for k in range(-(-NP // BANK))]
SHIFT = NP // 2
BIG = 1e30
ALU = mybir.AluOpType
ACT = mybir.ActivationFunctionType
AX = mybir.AxisListType
F32 = mybir.dt.float32
F16 = mybir.dt.float16
BF16 = mybir.dt.bfloat16
I32 = mybir.dt.int32


def tools(nc, ctx):
    used = []

    def clear():
        for handle in used:
            nc.gpsimd.sem_clear(handle)
    ctx.callback(clear)

    def sb(name, shape, dt=F32):
        return ctx.enter_context(nc.sbuf_tensor(name, shape, dt))

    def ps(name, shape):
        return ctx.enter_context(nc.psum_tensor(name, shape, F32))

    def sem(name, pool_dma=False):
        if pool_dma:
            return nc.alloc_semaphore(name)
        used.append(ctx.enter_context(nc.semaphore(name)))
        return used[-1]
    return sb, ps, sem


def edge_tables(nc, cx, d, k):
    with ExitStack() as ctx:
        sb, ps, sem = tools(nc, ctx)

        raw = sb("raw_ends", [P, 2, NG, P], I32)
        rawf = sb("raw_ends_f", [P, 2, NG, P], F32)
        cur = sb("dst_cur", [P, NT], I32)
        prev = sb("dst_prev", [P, NT], I32)
        starts = sb("start_flags", [P, NT], BF16)
        below = sb("below", [P, NT], F32)
        cnt = sb("cnt", [P, NBK + 1], F32)
        tot = sb("tot", [1, NBK + 1], F32)
        toti = sb("toti", [1, NBK + 1], I32)
        lo = sb("lo", [1, NBK], I32)
        hi = sb("hi", [1, NBK], I32)
        lof = sb("lof", [1, NBK], F32)
        nf = sb("nf", [1, NBK], F32)
        zf = sb("zf", [1, NBK], F32)
        incl = sb("incl", [1, NBK], F32)
        cutf = sb("cutf", [1, NBK], F32)
        tps = ctx.enter_context(nc.psum_tensor("tps", [P, 2, 4, BANK], F32))
        loaded = sem("ends_loaded")
        dl_loaded = sem("dst_loaded")
        stored = sem("starts_stored")
        ready_f = sem("ends_float")
        turned = sem("ends_turned")
        flags = sem("starts_ready")
        cnt_ready = sem("cnt_ready")
        tot_ready = sem("tot_ready")
        step = sem("table_step")
        full = NT // P
        rest = NT - full * P

        with nc.Block() as block:
            @block.sync
            def _(sp):
                for i, t in enumerate((d["src"], d["dst"])):
                    v = t[1:EP + 1] if i else t[0:EP]
                    sp.dma_start(raw[:, i, 0:full, :],
                                 v[0:full * P * P].rearrange("(g p e) -> p g e", p=P, e=P)).then_inc(loaded, 16)
                    sp.dma_start(raw[0:rest, i, full, :],
                                 v[full * P * P:EP].rearrange("(p e) -> p e", e=P)).then_inc(loaded, 16)
                sp.dma_start(prev[:, :], d["dst"][0:EP].rearrange("(p e) -> p e", e=NT)).then_inc(dl_loaded, 16)
                sp.dma_start(cur[:, :], d["dst"][1:EP + 1].rearrange("(p e) -> p e", e=NT)).then_inc(dl_loaded, 16)
                sp.wait_ge(flags, 1)
                sp.dma_start(d["starts"].rearrange("h (p e) -> (h p) e", e=NT), starts[:, :]).then_inc(stored, 16)
                sp.wait_ge(stored, 16)

            @block.tensor
            def _(pe):
                pe.wait_ge(ready_f, 2)
                for i in range(2):
                    for g in range(NG):
                        n = P if g < full else rest
                        last = nc.tensor.transpose(tps[:, i, g // 4, (g % 4) * P:(g % 4) * P + n],
                                                   rawf[0:n, i, g, :], k["ident"][0:n, 0:n])
                    last.then_inc(turned, 1)
                pe.wait_ge(cnt_ready, 1)
                nc.tensor.matmul(tps[0:1, 0, 3, 0:NBK + 1], k["ones"][:, 0:1], cnt[:, :],
                                 start=True, stop=True).then_inc(tot_ready, 1)

            @block.vector
            def _(dve):
                n = [0]

                def then(ins):
                    n[0] += 1
                    ins.then_inc(step, 1)
                    dve.wait_ge(step, n[0])

                dve.wait_ge(loaded, 64)
                for i in range(2):
                    nc.vector.tensor_copy(rawf[:, i, 0:full, :], raw[:, i, 0:full, :])
                    nc.vector.tensor_copy(rawf[0:rest, i, full, :], raw[0:rest, i, full, :]).then_inc(ready_f, 1)
                dve.wait_ge(dl_loaded, 32)
                nc.vector.tensor_tensor(starts[:, :], cur[:, :], prev[:, :], ALU.not_equal).then_inc(flags, 1)
                for i, t in enumerate((k["src_col"], k["dst_col"])):
                    dve.wait_ge(turned, i + 1)
                    for h in range(2):
                        a, b = h * BANK, min(NT, (h + 1) * BANK)
                        then(nc.vector.tensor_copy(t[:, a:b], tps[:, i, h, 0:b - a]))
                then(nc.vector.tensor_copy(k["src_idx"][:, :], k["src_col"][:, :]))
                for b in range(NBK + 1):
                    then(nc.vector.tensor_scalar(below[:, :], k["dst_col"][:, :], float(b * P), None, ALU.is_lt))
                    then(nc.vector.tensor_reduce(cnt[:, b:b + 1], below[:, :], AX.X, ALU.add))
                nc.vector.memset(zf[:, :], 0.0).then_inc(cnt_ready, 1)
                dve.wait_ge(tot_ready, 1)
                then(nc.vector.tensor_copy(tot[:, :], tps[0:1, 0, 3, 0:NBK + 1]))
                then(nc.vector.tensor_copy(toti[:, :], tot[:, :]))
                then(nc.vector.tensor_scalar(lo[:, :], toti[:, 0:NBK], 8, None, ALU.arith_shift_right))
                then(nc.vector.tensor_copy(lof[:, :], lo[:, :]))
                then(nc.vector.tensor_scalar(lof[:, :], lof[:, :], float(NPAIR - LEAST), None, ALU.min))
                then(nc.vector.tensor_scalar(nf[:, :], tot[:, 1:NBK + 1], 255.0, None, ALU.add))
                then(nc.vector.tensor_copy(hi[:, :], nf[:, :]))
                then(nc.vector.tensor_scalar(hi[:, :], hi[:, :], 8, None, ALU.arith_shift_right))
                then(nc.vector.tensor_copy(nf[:, :], hi[:, :]))
                then(nc.vector.scalar_tensor_tensor(out=nf[:, :], in0=lof[:, :], scalar=float(LEAST), in1=nf[:, :],
                                                    op0=ALU.add, op1=ALU.max))
                def keep(row, value):
                    then(nc.vector.tensor_copy(k["pairs"][:, row, :], value[:, :]))
                keep(0, lof)
                keep(1, nf)
                then(nc.vector.tensor_tensor(nf[:, :], nf[:, :], lof[:, :], ALU.subtract))
                for i, e in enumerate(CUTS):
                    then(nc.vector.tensor_scalar(cutf[:, :], nf[:, :], -1.0, float(e), ALU.add, ALU.mult))
                    then(nc.vector.tensor_copy(lo[:, :], cutf[:, :]))
                    then(nc.vector.tensor_scalar(lo[:, :], lo[:, :], 3, None, ALU.arith_shift_right))
                    then(nc.vector.tensor_copy(cutf[:, :], lo[:, :]))
                    then(nc.vector.scalar_tensor_tensor(out=cutf[:, :], in0=cutf[:, :], scalar=1.0, in1=lof[:, :],
                                                        op0=ALU.add, op1=ALU.add))
                    keep(4 + i, cutf)
                then(nc.vector.tensor_tensor_scan(incl[:, :], nf[:, :], zf[:, :], 0.0, ALU.add, ALU.add))
                then(nc.vector.tensor_tensor(incl[:, :], incl[:, :], nf[:, :], ALU.subtract))
                then(nc.vector.scalar_tensor_tensor(out=incl[:, :], in0=incl[:, :], scalar=2.0, in1=lof[:, :],
                                                    op0=ALU.mult, op1=ALU.subtract))
                keep(2, incl)
                then(nc.vector.tensor_tensor(incl[:, :], incl[:, :], nf[:, :], ALU.add))
                keep(3, incl)
                then(nc.vector.tensor_scalar(k["src_sh"][:, :], k["src_col"][:, :], -float(SHIFT), None, ALU.add))


def constants(nc, k):
    with ExitStack() as ctx:
        _, _, sem = tools(nc, ctx)
        made, io_made = sem("consts_made"), sem("iota_made")
        ioi = ctx.enter_context(nc.sbuf_tensor("iota_i", [P, NP], I32))
        iop = ctx.enter_context(nc.sbuf_tensor("iota_p", [P, P], I32))
        iob = ctx.enter_context(nc.sbuf_tensor("iota_b", [P, NBK], I32))
        with nc.Block() as block:
            @block.gpsimd
            def _(pool):
                G = nc.gpsimd
                G.iota(ioi[:, :], pattern=[[1, NP]], base=-SHIFT, channel_multiplier=0).then_inc(io_made, 1)
                G.iota(iop[:, :], pattern=[[1, P]], base=0, channel_multiplier=0).then_inc(io_made, 1)
                G.iota(iob[:, :], pattern=[[P, NBK]], base=0, channel_multiplier=0).then_inc(io_made, 1)
                for name, v in (("ones", 1.0), ("ident", 0.0), ("upper", 1.0), ("is_pad", 0.0), ("half_sel", -BIG),
                                ("zeros", 0.0)):
                    G.memset(k[name][:, :], v).then_inc(made, 1)
                G.memset(k["ones16"][:, :], 1.0).then_inc(made, 1)
                pool.wait_ge(made, 7)

                def where(name, op, fill, base, pattern, mult):
                    return G.affine_select(out=k[name][:, :], in_=k[name][:, :], compare_op=op, fill=fill, base=base,
                                           pattern=pattern, channel_multiplier=mult)
                where("ident", ALU.not_equal, 1.0, 0, [[-1, P]], 1)
                where("upper", ALU.is_ge, 0.0, 0, [[1, P]], -1)
                where("is_pad", ALU.is_ge, 1.0, N - 1, [[-P, NBK]], -1)
                where("half_sel", ALU.is_ge, 0.0, 0, [[1, P]], -F).then_inc(made, 1)
                pool.wait_ge(made, 8)
                where("half_sel", ALU.is_ge, 0.0, F - 1, [[-1, P]], F)

            @block.vector
            def _(dve):
                dve.wait_ge(io_made, 3)
                nc.vector.tensor_copy(k["iota16"][:, :], ioi[:, :])
                nc.vector.tensor_copy(k["iota_blk"][:, :], iop[:, :])
                nc.vector.tensor_copy(k["blk_first"][:, :], iob[:, :])


EPS = 1e-15
CLIP = 0.98
LN_EPS = 1e-5
M_MIN = 1e-16
M_MAX = CLIP * CLIP / (1 - CLIP * CLIP)
HALF_OFF = 2.5
W65 = F + 1
W66 = F + 2


class Count:

    def __init__(self, eng, sem):
        self.eng, self.sem, self.n, self.at = eng, sem, 0, {}

    def __call__(self, ins, name=None):
        self.mark(ins, name)
        self.eng.wait_ge(self.sem, self.n)

    def mark(self, ins, name=None):
        self.n += 1
        ins.then_inc(self.sem, 1)
        if name:
            self.at[name] = self.n


def over_blocks(eng, body):
    with eng.Fori(0, NBK // 2) as h:
        body(h, 0)
        body(h, 1)
    body(NBK // 2, 0)


def spread(col, w=F):
    return col.unsqueeze(2).to_broadcast([P, NBK, w])


def turn_blocks(pe, nc, k, psum, nodes, width, last_sem):
    for b in range(NBK):
        last = nc.tensor.transpose(psum[0:width, b // 4, (b % 4) * P:(b % 4 + 1) * P], nodes[:, b, 0:width],
                                   k["ident"][:, :])
    last.then_inc(last_sem, 1)


def back_blocks(pe, nc, k, psum, cols, width, last_sem):
    for b in range(NBK):
        last = nc.tensor.transpose(psum[:, b // 7, (b % 7) * width:(b % 7 + 1) * width],
                                   cols[0:width, b * P:(b + 1) * P], k["ident"][0:width, 0:width])
    last.then_inc(last_sem, 1)


def norm_sq(nc, then, out, v, sq, name=None):
    then(nc.vector.tensor_tensor(sq[:, :, :], v, v, ALU.mult))
    then(nc.vector.tensor_reduce(out, sq[:, :, :], AX.X, ALU.add), name)


def limit_norm(nc, then, v, nrm, t, lim, c2=None):
    then(nc.vector.tensor_scalar(t, nrm, lim, None, ALU.max))
    then(nc.vector.reciprocal(t, t))
    then(nc.vector.tensor_scalar(t, t, lim, None, ALU.mult))
    then(nc.vector.tensor_tensor(v, v, spread(t), ALU.mult))


def artanh_small(nc, then, out, y, t1, t2):
    then(nc.vector.tensor_tensor(t1, y, y, ALU.mult))
    then(nc.vector.tensor_scalar(t2, t1, 1 / 7, 1 / 5, ALU.mult, ALU.add))
    then(nc.vector.tensor_tensor(t2, t2, t1, ALU.mult))
    then(nc.vector.tensor_scalar(t2, t2, 1 / 3, None, ALU.add))
    then(nc.vector.tensor_tensor(t2, t2, t1, ALU.mult))
    then(nc.vector.tensor_scalar(t2, t2, 1.0, None, ALU.add))
    then(nc.vector.tensor_tensor(out, t2, y, ALU.mult))


def artanh_pick(nc, then, out, y, lnp, lnm, small, t1):
    then(nc.vector.tensor_tensor(out, lnp, lnm, ALU.subtract))
    then(nc.vector.scalar_tensor_tensor(out=out, in0=out, scalar=0.5, in1=small, op0=ALU.mult, op1=ALU.subtract))
    then(nc.vector.tensor_scalar(t1, y, 0.15, None, ALU.is_ge))
    then(nc.vector.tensor_tensor(out, out, t1, ALU.mult))
    then(nc.vector.tensor_tensor(out, out, small, ALU.add))


def layernorm_stats(nc, then, v, sq, m, var, name):
    then(nc.vector.tensor_reduce(m, v, AX.X, ALU.add))
    then(nc.vector.tensor_scalar(m, m, 1 / F, None, ALU.mult))
    then(nc.vector.tensor_tensor(v, v, spread(m), ALU.subtract))
    then(nc.vector.tensor_tensor(sq[:, :, :], v, v, ALU.mult))
    then(nc.vector.tensor_reduce(var, sq[:, :, :], AX.X, ALU.add))
    then(nc.vector.tensor_scalar(var, var, 1 / F, LN_EPS, ALU.mult, ALU.add), name)


def hyperbolic_nodes(nc, d, k):
    with ExitStack() as ctx:
        sb, ps, sem = tools(nc, ctx)
        v = sb("n_v", [P, NBK, F])
        u = sb("n_u", [P, NBK, F])
        sq = sb("n_sq", [P, NBK, F])
        aug = sb("n_aug", [P, 2, NBK, W66])
        vt = sb("n_vt", [F, NP])
        W = sb("n_W", [F, F])
        col = sb("n_col", [P, 12, NBK])
        ss, nr, t1, t2, th, pn, at, small, lnp, lnm, y, nu = (col[:, i, :] for i in range(12))
        pt = ps("n_pt", [P, 7, BANK])
        loaded, dsem, asem, amid = sem("l0_loaded"), sem("l0_dve"), sem("l0_act"), sem("l0_act_mid")
        turned, evac, prod, aug_turned, aug_evac = (sem(f"l0_{x}") for x in
                                                    ("turned", "evac", "prod", "aug_turned", "aug_evac"))
        x, cc = k["x"], k["cc"]
        c1, rc, irc, c2lim = (cc[:, i:i + 1] for i in range(4))
        with nc.Block() as block:
            @block.sync
            def _(sp):
                sp.dma_start(x[:, :, :], d["x"].rearrange("(b p) f -> p b f", p=P)).then_inc(loaded, 16)
                sp.dma_start(c1, d["c"].unsqueeze(0).to_broadcast([P, 1])).then_inc(loaded, 16)
                sp.dma_start(W[:, :], d["W0"]).then_inc(loaded, 16)

            steps = {}

            @block.vector
            def _(dve):
                then = Count(dve, dsem)
                steps["dve"] = then.at
                a = [0]

                def answered():
                    a[0] += 1
                    dve.wait_ge(asem, a[0])

                dve.wait_ge(loaded, 48)
                then(nc.vector.tensor_scalar(v[:, :, :], x[:, :, :], EPS, None, ALU.add), "c")
                norm_sq(nc, then, ss, v[:, :, :], sq, "f_sq")
                answered()
                answered()
                then(nc.vector.reciprocal(irc, rc))
                then(nc.vector.tensor_scalar(c2lim, irc, CLIP, None, ALU.mult))
                then(nc.vector.tensor_scalar(cc[:, 4:5], irc, -2.0, None, ALU.mult))
                limit_norm(nc, then, v[:, :, :], nr, t1, CLIP)
                norm_sq(nc, then, ss, v[:, :, :], sq, "fn_sq")
                answered()
                then(nc.vector.reciprocal(t1, nr))
                then(nc.vector.tensor_tensor(t1, t1, th, ALU.mult))
                then(nc.vector.tensor_tensor(v[:, :, :], v[:, :, :], spread(t1), ALU.mult))
                then(nc.vector.tensor_scalar(v[:, :, :], v[:, :, :], EPS, None, ALU.add))
                norm_sq(nc, then, ss, v[:, :, :], sq, "p_sq")
                answered()
                limit_norm(nc, then, v[:, :, :], nr, t1, CLIP)
                norm_sq(nc, then, ss, v[:, :, :], sq, "pn_sq")
                answered()
                then(nc.vector.tensor_copy(pn, nr))
                then(nc.vector.tensor_scalar(y, pn, rc, None, ALU.mult))
                then(nc.vector.tensor_scalar(y, y, 0.9, -0.9, ALU.min, ALU.max), "y1")
                artanh_small(nc, then, small, y, t1, t2)
                answered()
                artanh_pick(nc, then, at, y, lnp, lnm, small, t1)
                then(nc.vector.reciprocal(t1, pn))
                then(nc.vector.tensor_tensor(t1, t1, at, ALU.mult))
                then(nc.vector.tensor_scalar(t1, t1, irc, None, ALU.mult))
                dve.wait_ge(prod, 1)
                for g in range(4):
                    lo, hi = 8 * g, min(NBK, 8 * g + 8)
                    then(nc.vector.tensor_tensor(
                        u[:, lo:hi, :], pt[:, g, 0:(hi - lo) * F].rearrange("p (b f) -> p b f", f=F),
                        t1[:, lo:hi].unsqueeze(2).to_broadcast([P, hi - lo, F]), ALU.mult))
                norm_sq(nc, then, ss, u[:, :, :], sq, "t_sq")
                answered()
                limit_norm(nc, then, u[:, :, :], nr, t1, c2lim)
                norm_sq(nc, then, ss, u[:, :, :], sq, "tn_sq")
                answered()
                then(nc.vector.reciprocal(t1, nr))
                then(nc.vector.tensor_tensor(t1, t1, th, ALU.mult))
                then(nc.vector.tensor_scalar(t1, t1, irc, None, ALU.mult))
                then(nc.vector.tensor_tensor(u[:, :, :], u[:, :, :], spread(t1), ALU.mult))
                norm_sq(nc, then, nu, u[:, :, :], sq)
                then(nc.vector.tensor_scalar(t1, nu, c1, -1.0, ALU.mult, ALU.mult))
                then(nc.vector.tensor_scalar(t1, t1, 1.0, None, ALU.add))
                then(nc.vector.reciprocal(aug[:, 0, :, F + 1], t1))
                s_ = aug[:, 0, :, F + 1]
                then(nc.vector.tensor_tensor(aug[:, 0, :, F], nu, s_, ALU.mult))
                then(nc.vector.tensor_tensor(aug[:, 0, :, 0:F], u[:, :, :], spread(s_), ALU.mult))
                then(nc.vector.tensor_scalar(aug[:, 1, :, 0:F], aug[:, 0, :, 0:F], c1, -2.0, ALU.mult, ALU.mult))
                then(nc.vector.tensor_scalar(aug[:, 1, :, F], s_, c1, None, ALU.mult))
                then(nc.vector.tensor_scalar(aug[:, 1, :, F + 1], aug[:, 0, :, F], c1, None, ALU.mult), "aug")
                then(nc.vector.tensor_scalar(v[:, :, :], u[:, :, :], EPS, None, ALU.add))
                norm_sq(nc, then, ss, v[:, :, :], sq, "g_sq")
                answered()
                limit_norm(nc, then, v[:, :, :], nr, t1, CLIP)
                norm_sq(nc, then, ss, v[:, :, :], sq, "gn_sq")
                answered()
                then(nc.vector.tensor_copy(pn, nr))
                then(nc.vector.tensor_scalar(y, pn, rc, None, ALU.mult))
                then(nc.vector.tensor_scalar(y, y, 0.9, -0.9, ALU.min, ALU.max), "y2")
                artanh_small(nc, then, small, y, t1, t2)
                answered()
                artanh_pick(nc, then, at, y, lnp, lnm, small, t1)
                then(nc.vector.reciprocal(t1, pn))
                then(nc.vector.tensor_tensor(t1, t1, at, ALU.mult))
                then(nc.vector.tensor_scalar(t1, t1, rc, None, ALU.mult))
                then(nc.vector.tensor_tensor(k["val"][:, :, 0:F], v[:, :, :], spread(t1), ALU.mult))
                then(nc.vector.memset(k["val"][:, :, F], 1.0))

            @block.scalar
            def _(act):
                at_ = steps["dve"]

                def root():
                    nc.scalar.sqrt(nr, ss).then_inc(asem, 1)

                act.wait_ge(loaded, 48)
                nc.scalar.sqrt(rc, c1).then_inc(asem, 1)
                act.wait_ge(dsem, at_["f_sq"])
                root()
                act.wait_ge(dsem, at_["fn_sq"])
                nc.scalar.sqrt(nr, ss).then_inc(amid, 1)
                act.wait_ge(amid, 1)
                nc.scalar.activation(th, nr, ACT.Tanh).then_inc(asem, 1)
                for name in ("p_sq", "pn_sq"):
                    act.wait_ge(dsem, at_[name])
                    root()
                act.wait_ge(dsem, at_["y1"])
                nc.scalar.activation(lnp, y, ACT.Ln, bias=1.0)
                nc.scalar.activation(lnm, y, ACT.Ln, scale=-1.0, bias=1.0).then_inc(asem, 1)
                act.wait_ge(turned, 1)
                for i, (a, w) in enumerate(SPANS):
                    last = nc.scalar.copy(vt[:, a:a + w], pt[0:F, i, 0:w])
                last.then_inc(evac, 1)
                act.wait_ge(dsem, at_["t_sq"])
                root()
                act.wait_ge(dsem, at_["tn_sq"])
                nc.scalar.sqrt(nr, ss).then_inc(amid, 1)
                act.wait_ge(amid, 2)
                nc.scalar.activation(th, nr, ACT.Tanh, scale=rc).then_inc(asem, 1)
                for name in ("g_sq", "gn_sq"):
                    act.wait_ge(dsem, at_[name])
                    root()
                act.wait_ge(dsem, at_["y2"])
                nc.scalar.activation(lnp, y, ACT.Ln, bias=1.0)
                nc.scalar.activation(lnm, y, ACT.Ln, scale=-1.0, bias=1.0).then_inc(asem, 1)
                for j in range(2):
                    act.wait_ge(aug_turned, j + 1)
                    for i, (a, w) in enumerate(SPANS):
                        last = nc.scalar.copy(k["hT"][0:W66, j, a:a + w], pt[0:W66, i, 0:w])
                    last.then_inc(aug_evac, 1)

            @block.tensor
            def _(pe):
                at_ = steps["dve"]
                pe.wait_ge(dsem, at_["y1"])
                turn_blocks(pe, nc, k, pt, v, F, turned)
                pe.wait_ge(evac, 1)
                for b in range(NBK):
                    last = nc.tensor.matmul(pt[:, b // 8, (b % 8) * F:(b % 8 + 1) * F], vt[:, b * P:(b + 1) * P],
                                            W[:, :], start=True, stop=True)
                last.then_inc(prod, 1)
                for j in range(2):
                    pe.wait_ge(dsem, at_["aug"])
                    if j:
                        pe.wait_ge(aug_evac, j)
                    turn_blocks(pe, nc, k, pt, aug[:, j], W66, aug_turned)


def pair_distances(nc, d, k):
    with ExitStack() as ctx:
        sb, ps, sem = tools(nc, ctx)
        m = sb("pd_m", [P, 2, NP])
        root1 = sb("pd_root1", [P, 2, NP])
        cnt = sb("pd_cnt", [P, 2, NP])
        out = sb("pd_out", [P, 2, NP])
        top = sb("pd_top", [P, NP])
        lhs = sb("pd_lhs", [W66, 2, P])
        dg = sb("pd_dg", [P, 2, P])
        topc = sb("pd_topc", [P, NBK])
        off = sb("pd_off", [P, P])
        dn = ps("pd_dn", [P, 7, BANK])
        tp = dn[:, 2:4, :]
        m_ready, off_diag, added, root, logs, not_diag = (
            sem(f"pd_{x}") for x in ("m_ready", "off_diag", "added", "root", "logs", "not_diag"))
        lhs_ready, loaded, stored, out_ready, masked_ = (
            [sem(f"pd_{x}{s}") for s in range(2)]
            for x in ("lhs_ready", "loaded", "stored", "out_ready", "masked"))
        prods, used = sem("pd_prods"), sem("pd_used")
        top_zero, top_turned, top_taken, diag, row, row_out = (
            sem(f"pd_{x}") for x in ("top_zero", "top_turned", "top_taken", "diag", "row", "row_out"))
        NS = len(SPANS)
        NSLOT = NS
        with nc.Block() as block:
            @block.sync
            def _(sp):
                def load(h, s):
                    sp.wait_ge(masked_[s], h)
                    sp.dma_start(cnt[:, s, :], d["counts"][bass.ds((2 * h + s) * P, P), :]).then_inc(loaded[s], 16)

                def store(h, s):
                    sp.wait_ge(masked_[s], h + 1)
                    sp.dma_start(d["near"][bass.ds((2 * h + s) * P, P), :], out[:, s, :]).then_inc(stored[s], 16)

                load(0, 0)
                with sp.Fori(0, NBK // 2) as h:
                    load(h, 1)
                    store(h, 0)
                    load(h + 1, 0)
                    store(h, 1)
                store(NBK // 2, 0)
                sp.wait_ge(stored[0], 16 * (NBK // 2 + 1))
                sp.wait_ge(stored[1], 16 * (NBK // 2))

            @block.gpsimd
            def _(pool):
                def columns(h, s):
                    pool.wait_ge(prods, 2 * NS * h)
                    nc.gpsimd.tensor_copy(lhs[:, s, :], k["hT"][0:W66, 1, bass.ds((2 * h + s) * P, P)])\
                      .then_inc(lhs_ready[s], 1)
                over_blocks(pool, columns)

            @block.tensor
            def _(pe):
                pe.wait_ge(top_zero, 1)

                def body(h, s):
                    pe.wait_ge(lhs_ready[s], h + 1)
                    for i, (a, w) in enumerate(SPANS):
                        pe.wait_ge(used, NS * (2 * h + s) + i + 1)
                        nc.tensor.matmul(dn[:, i, 0:w],
                                         lhs[:, s, :], k["hT"][0:W66, 0, a:a + w],
                                         start=True, stop=True).then_inc(prods, 1)
                over_blocks(pe, body)
                pe.wait_ge(out_ready[0], NBK // 2 + 1)
                for b in range(NBK):
                    if b >= 2:
                        pe.wait_ge(top_taken, b - 1)
                    nc.tensor.transpose(tp[:, b % 2, 0:P], top[:, b * P:(b + 1) * P],
                                        k["ident"][:, :]).then_inc(top_turned, 1)
                for b in range(NBK):
                    pe.wait_ge(diag, b + 1)
                    if b >= 2:
                        pe.wait_ge(row_out, b - 1)
                    nc.tensor.matmul(dn[:, b % 2, 0:P], k["ones"][:, :], dg[:, b % 2, :],
                                     start=True, stop=True).then_inc(row, 1)

            @block.scalar
            def _(act):
                def body(h, s):
                    b = 2 * h + s
                    act.wait_ge(m_ready, b + 1)
                    nc.scalar.activation(root1[:, s, :], m[:, s, :], ACT.Sqrt, bias=1.0).then_inc(root, 1)
                    act.wait_ge(root, 2 * b + 1)
                    nc.scalar.sqrt(m[:, s, :], m[:, s, :]).then_inc(root, 1)
                    act.wait_ge(added, b + 1)
                    nc.scalar.activation(m[:, s, :], m[:, s, :], ACT.Ln,
                                         scale=float(np.exp(-HALF_OFF))).then_inc(logs, 1)
                over_blocks(act, body)
                for b in range(NBK):
                    act.wait_ge(row, b + 1)
                    nc.scalar.copy(k["toprow"][:, b * P:(b + 1) * P], dn[:, b % 2, 0:P]).then_inc(row_out, 1)

            @block.vector
            def _(dve):
                def clipped(h, s):
                    b = 2 * h + s
                    dve.wait_ge(masked_[s], h)
                    for i, (a, w) in enumerate(SPANS):
                        dve.wait_ge(prods, NS * b + i + 1)
                        nc.vector.tensor_scalar(m[:, s, a:a + w], dn[:, i, 0:w], M_MIN, M_MAX,
                                                ALU.max, ALU.min).then_inc(used, 1)
                    dve.wait_ge(used, NS * b + NS + NSLOT)
                    dv = m[:, s, bass.ds(b * P, P)]
                    nc.vector.tensor_tensor(dv, dv, off[:, :], ALU.mult).then_inc(off_diag, 1)
                    dve.wait_ge(off_diag, b + 1)
                    nc.vector.tensor_scalar(dv, dv, M_MIN, None, ALU.max).then_inc(m_ready, 1)

                def masked(h, s):
                    b = 2 * h + s
                    dve.wait_ge(logs, b + 1)
                    dve.wait_ge(stored[s], 16 * h)
                    dve.wait_ge(loaded[s], 16 * h + 16)
                    dve.wait_ge(out_ready[s], h)
                    nc.vector.scalar_tensor_tensor(out=out[:, s, :], in0=cnt[:, s, :], scalar=1.0, in1=m[:, s, :],
                                                   op0=ALU.min, op1=ALU.mult).then_inc(masked_[s], 1)
                    dve.wait_ge(masked_[s], h + 1)
                    nc.vector.tensor_tensor(top[:, :], top[:, :], out[:, s, :], ALU.min).then_inc(out_ready[s], 1)
                    dve.wait_ge(out_ready[s], h + 1)

                def sums(h, s):
                    b = 2 * h + s
                    dve.wait_ge(root, 2 * b + 2)
                    nc.vector.tensor_tensor(m[:, s, :], m[:, s, :], root1[:, s, :], ALU.add).then_inc(added, 1)

                nc.vector.tensor_scalar(off[:, :], k["ident"][:, :], -1.0, 1.0, ALU.mult, ALU.add).then_inc(not_diag, 1)
                nc.vector.memset(topc[:, 0:1], 0.0).then_inc(used, NSLOT)
                nc.vector.memset(top[:, :], 0.0).then_inc(top_zero, 1)
                dve.wait_ge(top_zero, 1)
                dve.wait_ge(not_diag, 1)
                clipped(0, 0)
                sums(0, 0)
                with dve.Fori(0, NBK // 2) as h:
                    clipped(h, 1)
                    masked(h, 0)
                    sums(h, 1)
                    clipped(h + 1, 0)
                    masked(h, 1)
                    sums(h + 1, 0)
                masked(NBK // 2, 0)
                for b in range(NBK):
                    dve.wait_ge(top_turned, b + 1)
                    nc.vector.tensor_reduce(topc[:, b:b + 1], tp[:, b % 2, 0:P], AX.X, ALU.min).then_inc(top_taken, 1)
                for b in range(NBK):
                    dve.wait_ge(top_taken, b + 1)
                    if b >= 2:
                        dve.wait_ge(row, b - 1)
                    nc.vector.tensor_scalar(dg[:, b % 2, :], k["ident"][:, :], topc[:, b:b + 1], None,
                                            ALU.mult).then_inc(diag, 1)


def zero_sums(nc, k, acc, rows):
    for i, (a, w) in enumerate(SPANS):
        last = nc.tensor.matmul(acc[0:rows, i, 0:w], k["zeros"][:, 0:rows], k["zeros"][:, 0:w],
                                start=True, stop=False, skip_group_check=True)
    return last


def near_sums(nc, d, k):
    with ExitStack() as ctx:
        sb, ps, sem = tools(nc, ctx)
        near = sb("ns_near", [P, 2, NP])
        cnt = sb("ns_cnt", [P, 2, NP])
        z = sb("ns_z", [P, 2, NP])
        w_ = sb("ns_w", [P, 2, NP])
        val = sb("ns_val", [P, 2, W65])
        acc = ps("ns_acc", [P, 7, BANK])
        loaded, zed, exped, weighed, val_ready, summed = (
            [sem(f"ns_{x}{s}") for s in range(2)]
            for x in ("loaded", "zed", "exped", "weighed", "val_ready", "summed"))
        done, sums_out = sem("ns_done"), sem("ns_sums_out")
        with nc.Block() as block:
            @block.sync
            def _(sp):
                def load(h, s):
                    rows = bass.ds((2 * h + s) * P, P)
                    sp.wait_ge(zed[s], h)
                    sp.dma_start(near[:, s, :], d["near"][rows, :]).then_inc(loaded[s], 16)
                    sp.wait_ge(weighed[s], h)
                    sp.dma_start(cnt[:, s, :], d["counts"][rows, :]).then_inc(loaded[s], 16)
                over_blocks(sp, load)

            @block.gpsimd
            def _(pool):
                def body(h, s):
                    pool.wait_ge(summed[s], h)
                    nc.gpsimd.tensor_copy(val[:, s, :].unsqueeze(1), k["val"][:, bass.ds(2 * h + s, 1), 0:W65])\
                      .then_inc(val_ready[s], 1)
                over_blocks(pool, body)

            @block.vector
            def _(dve):
                def less_top(h, s):
                    dve.wait_ge(loaded[s], 32 * h + 32)
                    dve.wait_ge(exped[s], h)
                    nc.vector.tensor_tensor(z[:, s, :], near[:, s, :], k["toprow"][:, :],
                                            ALU.subtract).then_inc(zed[s], 1)

                def weigh(h, s):
                    dve.wait_ge(exped[s], h + 1)
                    dve.wait_ge(summed[s], h)
                    nc.vector.tensor_tensor(w_[:, s, :], z[:, s, :], cnt[:, s, :], ALU.mult).then_inc(weighed[s], 1)

                less_top(0, 0)
                with dve.Fori(0, NBK // 2) as h:
                    less_top(h, 1)
                    weigh(h, 0)
                    dve.wait_ge(weighed[0], h + 1)
                    less_top(h + 1, 0)
                    weigh(h, 1)
                    dve.wait_ge(weighed[1], h + 1)
                weigh(NBK // 2, 0)

            @block.scalar
            def _(act):
                def body(h, s):
                    act.wait_ge(zed[s], h + 1)
                    nc.scalar.activation(z[:, s, :], z[:, s, :], ACT.Exp, scale=k["cc"][:, 4:5]).then_inc(exped[s], 1)
                over_blocks(act, body)
                act.wait_ge(done, 1)
                for i, (a, w) in enumerate(SPANS):
                    nc.scalar.copy(k["sums"][0:W65, a:a + w], acc[0:W65, i, 0:w])

            @block.tensor
            def _(pe):
                zero_sums(nc, k, acc, W65)

                def body(h, s):
                    pe.wait_ge(weighed[s], h + 1)
                    pe.wait_ge(val_ready[s], h + 1)
                    for i, (a, w) in enumerate(SPANS):
                        last = nc.tensor.matmul(acc[0:W65, i, 0:w], val[:, s, :], w_[:, s, a:a + w],
                                                start=False, stop=False, skip_group_check=True)
                    last.then_inc(summed[s], 1)
                over_blocks(pe, body)
                nc.tensor.matmul(acc[0:1, 6, BANK - 1:BANK], k["zeros"][:, 0:1], k["zeros"][:, 0:1],
                                 start=False, stop=True, skip_group_check=True).then_inc(done, 1)
            del sums_out


def elu(nc, then, act_exp, v, t):
    then(nc.vector.tensor_scalar(t, v, 0.0, None, ALU.min), "elu")
    act_exp()
    then(nc.vector.tensor_scalar(v, v, 0.0, -1.0, ALU.max, ALU.add))
    then(nc.vector.tensor_tensor(v, v, t, ALU.add))


def end_hyperbolic(nc, d, k):
    with ExitStack() as ctx:
        sb, ps, sem = tools(nc, ctx)
        v = sb("eh_v", [P, NBK, F])
        t = sb("eh_t", [P, NBK, F])
        col = sb("eh_col", [P, 6, NBK])
        den, ss, nr, t1, th, t2 = (col[:, i, :] for i in range(6))
        pb = ps("eh_pb", [P, 4, BANK])
        back, dsem, asem, amid = sem("eh_back"), sem("eh_dve"), sem("eh_act"), sem("eh_act_mid")
        x = k["x"]
        rc, irc, c2lim = (k["cc"][:, i:i + 1] for i in (1, 2, 3))
        steps = {}
        with nc.Block() as block:
            @block.tensor
            def _(pe):
                back_blocks(pe, nc, k, pb, k["sums"], W65, back)

            @block.vector
            def _(dve):
                then = Count(dve, dsem)
                steps["dve"] = then.at
                a = [0]

                def answered():
                    a[0] += 1
                    dve.wait_ge(asem, a[0])

                dve.wait_ge(back, 1)
                for g in range(4):
                    lo, hi = 7 * g, min(NBK, 7 * g + 7)
                    rows = pb[:, g, 0:(hi - lo) * W65].rearrange("p (b f) -> p b f", f=W65)
                    then(nc.vector.tensor_scalar(den[:, lo:hi], rows[:, :, F], 1e-16, None, ALU.add))
                    then(nc.vector.reciprocal(den[:, lo:hi], den[:, lo:hi]))
                    then(nc.vector.tensor_tensor(v[:, lo:hi, :], rows[:, :, 0:F],
                                                 den[:, lo:hi].unsqueeze(2).to_broadcast([P, hi - lo, F]), ALU.mult))
                elu(nc, then, answered, v[:, :, :], t[:, :, :])
                then(nc.vector.tensor_scalar(v[:, :, :], v[:, :, :], EPS, None, ALU.add))
                norm_sq(nc, then, ss, v[:, :, :], t, "z_sq")
                answered()
                limit_norm(nc, then, v[:, :, :], nr, t1, c2lim)
                norm_sq(nc, then, ss, v[:, :, :], t, "zn_sq")
                answered()
                then(nc.vector.reciprocal(t1, nr))
                then(nc.vector.tensor_tensor(t1, t1, th, ALU.mult))
                then(nc.vector.tensor_scalar(t1, t1, irc, None, ALU.mult))
                then(nc.vector.tensor_tensor(v[:, :, :], v[:, :, :], spread(t1), ALU.mult))
                then(nc.vector.tensor_tensor(x[:, :, :], x[:, :, :], v[:, :, :], ALU.add))
                layernorm_stats(nc, then, x[:, :, :], t, t1, t2, "var")
                answered()
                then(nc.vector.reciprocal(t1, nr))
                then(nc.vector.tensor_tensor(x[:, :, :], x[:, :, :], spread(t1), ALU.mult))

            @block.scalar
            def _(act):
                at_ = steps["dve"]
                act.wait_ge(dsem, at_["elu"])
                nc.scalar.activation(t[:, :, :], t[:, :, :], ACT.Exp).then_inc(asem, 1)
                act.wait_ge(dsem, at_["z_sq"])
                nc.scalar.sqrt(nr, ss).then_inc(asem, 1)
                act.wait_ge(dsem, at_["zn_sq"])
                nc.scalar.sqrt(nr, ss).then_inc(amid, 1)
                act.wait_ge(amid, 1)
                nc.scalar.activation(th, nr, ACT.Tanh, scale=rc).then_inc(asem, 1)
                act.wait_ge(dsem, at_["var"])
                nc.scalar.sqrt(nr, t2).then_inc(asem, 1)
def take_edges(nc, d, k):
    with ExitStack() as ctx:
        sb, ps, sem = tools(nc, ctx)
        cur = sb("te_cur", [P, NT], I32)
        prev = sb("te_prev", [P, NT], I32)
        falls = sb("te_falls", [P, NT])
        fall = sb("te_fall", [P, 1])
        fp = ps("te_fp", [1, BANK])
        copied, loaded, compared, reduced, summed, kept = (
            sem(f"te_{x}") for x in ("copied", "loaded", "compared", "reduced", "summed", "kept"))
        with nc.Block() as block:
            @block.sync
            def _(sp):
                sp.dma_start(prev[:, :], d["dst_given"][0:EP].rearrange("(p e) -> p e", e=NT)).then_inc(loaded, 16)
                sp.dma_start(cur[:, :], d["dst_given"][1:EP + 1].rearrange("(p e) -> p e", e=NT)).then_inc(loaded, 16)
                sp.dma_start(d["src"].rearrange("(p e) -> p e", e=NT),
                             d["src_given"].rearrange("(p e) -> p e", e=NT)).then_inc(copied, 16)
                sp.dma_start(d["dst"][0:1].unsqueeze(0), d["dst_given"][0:1].unsqueeze(0)).then_inc(copied, 16)
                sp.dma_start(d["dst"][1:EP + 1].rearrange("(p e) -> p e", e=NT),
                             d["dst_given"][1:EP + 1].rearrange("(p e) -> p e", e=NT)).then_inc(copied, 16)
                sp.dma_start(d["attr8"].rearrange("r (p e) -> (r p) e", p=16),
                             d["attr_given"].rearrange("r (p e) -> (r p) e", p=16)).then_inc(copied, 16)
                sp.wait_ge(copied, 64)

            @block.vector
            def _(dve):
                dve.wait_ge(loaded, 32)
                nc.vector.tensor_tensor(falls[:, :], prev[:, :], cur[:, :], ALU.is_gt).then_inc(compared, 1)
                dve.wait_ge(compared, 1)
                nc.vector.tensor_reduce(fall[:, :], falls[:, :], AX.X, ALU.add).then_inc(reduced, 1)
                dve.wait_ge(summed, 1)
                nc.vector.tensor_copy(k["unsorted"][:, :], fp[:, 0:1]).then_inc(kept, 1)

            @block.tensor
            def _(pe):
                pe.wait_ge(reduced, 1)
                nc.tensor.matmul(fp[:, 0:1], fall[:, :], k["ones"][:, 0:1], start=True, stop=True).then_inc(summed, 1)


def sort_edges(nc, d, k):
    with ExitStack() as ctx:
        sb, ps, sem = tools(nc, ctx)
        srcs = sb("so2_src", [P, NT], I32)
        dsts = sb("so2_dst", [P, NT], I32)
        attr = sb("so2_attr", [P, 3, NT])
        dsh = sb("so2_dsh", [P, NT])
        hot = sb("so2_hot", [P, 2, NP], F16)
        base = sb("so2_base", [P, NP])
        tmp = sb("so2_tmp", [P, NP])
        place = sb("so2_place", [P, NT])
        half = sb("so2_half", [P, NT])
        aplace = sb("so2_aplace", [P, NT])
        before = sb("so2_before", [P, P], F16)
        rest = sb("so2_rest", [P, P], F16)
        all_ = sb("so2_all", [P, P], F16)
        val = sb("so2_val", [P, 5])
        vali = sb("so2_vali", [P, 2], I32)
        pl = sb("so2_pl", [P, 5], I32)
        acc = ps("so2_acc", [P, 7, BANK])
        loaded, made, made2, step, shifted = (sem(f"so2_{x}") for x in ("loaded", "made", "made2", "step", "shifted"))
        hots, used, ranked, hist, put, done1 = (sem(f"so2_{x}") for x in ("hots", "used", "ranked", "hist", "put", "done1"))
        opened = sem("so2_opened")
        sent = sem("so2_sent", pool_dma=True)
        accv = acc[:, :, :].rearrange("p a b -> p (a b)")[:, 0:NP]
        with nc.Block() as block:
            @block.sync
            def _(sp):
                falls = sp.value_load(k["unsorted"][0:1, 0:1], min_val=0, max_val=EP)
                with sp.If(falls > 0):
                    with nc.allow_non_contiguous_dma(reason="edge columns, on this path alone"):
                        sp.dma_start(srcs[:, :], d["src_given"].rearrange("(t p) -> p t", p=P)).then_inc(loaded, 16)
                        sp.dma_start(dsts[:, :], d["dst_given"][1:EP + 1].rearrange("(t p) -> p t", p=P)).then_inc(loaded, 16)
                        for h in range(2):
                            for j in range(3):
                                sp.dma_start(attr[:, j, h * HT:(h + 1) * HT],
                                             d["attr_given"][4 * h + j].rearrange("(t p) -> p t", p=P)).then_inc(loaded, 16)

            @block.tensor
            def _(pe):
                falls = pe.value_load(k["unsorted"][0:1, 0:1], min_val=0, max_val=EP)
                with pe.If(falls > 0):
                    def add(w, start):
                        for i, (a, n) in enumerate(SPANS):
                            last = nc.tensor.matmul(acc[:, i, 0:n], w, hot[:, 0, a:a + n], start=start, stop=False,
                                                    skip_group_check=True)
                        return last
                    pe.wait_ge(made2, 1)
                    pe.wait_ge(hots, 1)
                    add(all_[:, :], True).then_inc(used, 1)
                    with pe.Fori(1, NT) as t:
                        pe.wait_ge(hots, t + 1)
                        add(all_[:, :], False).then_inc(used, 1)
                    nc.tensor.matmul(acc[0:1, 6, BANK - 1:BANK], all_[:, 0:1], all_[:, 0:1], start=False, stop=True,
                                     skip_group_check=True).then_inc(hist, 1)
                    pe.wait_ge(done1, 1)
                    zero_sums(nc, k, acc, P)
                    with pe.Fori(0, NT) as t:
                        pe.wait_ge(hots, t + NT + 1)
                        add(before[:, :], False).then_inc(ranked, 1)
                        pe.wait_ge(put, t + 1)
                        add(rest[:, :], False).then_inc(used, 1)

            @block.gpsimd
            def _(pool):
                falls = pool.value_load(k["unsorted"][0:1, 0:1], min_val=0, max_val=EP)
                with pool.If(falls > 0):
                    G = nc.gpsimd
                    G.memset(all_[:, :], 1.0).then_inc(made, 1)
                    G.memset(before[:, :], 1.0).then_inc(made, 1)
                    G.memset(rest[:, :], 1.0).then_inc(made, 1)
                    pool.wait_ge(made, 3)
                    G.affine_select(out=before[:, :], in_=before[:, :], compare_op=ALU.is_gt, fill=0.0, base=0,
                                    pattern=[[1, P]], channel_multiplier=-1)
                    G.affine_select(out=rest[:, :], in_=rest[:, :], compare_op=ALU.is_ge, fill=0.0, base=0,
                                    pattern=[[-1, P]], channel_multiplier=1).then_inc(made2, 1)
                    with pool.Fori(0, NT) as t:
                        pool.wait_ge(shifted, t + 1)
                        pool.sem_inc(opened, 1)
                        for j, (to, off) in enumerate((("src", 0), ("dst", 0), ("attr8", 0), ("attr8", EP // 2),
                                                       ("attr8", 2 * (EP // 2)))):
                            flat = d[to].rearrange("r e -> (r e)") if to == "attr8" else d[to]
                            pool.indirect_dma_start(flat.unsqueeze(1), bass.IndirectOffsetOnAxis(ap=pl[:, j:j + 1], axis=0),
                                                    vali[:, j:j + 1] if j < 2 else val[:, j:j + 1], None).then_inc(sent, 16)

            @block.vector
            def _(dve):
                falls = dve.value_load(k["unsorted"][0:1, 0:1], min_val=0, max_val=EP)
                with dve.If(falls > 0):
                    V, TT, TS = nc.vector, nc.vector.tensor_tensor, nc.vector.tensor_scalar
                    then = Count(dve, step)
                    dve.wait_ge(loaded, 128)
                    then(V.tensor_copy(dsh[:, :], dsts[:, :]))
                    then(TS(dsh[:, :], dsh[:, :], -float(SHIFT), None, ALU.add))
                    with dve.Fori(0, NT) as t:
                        dve.wait_ge(used, t)
                        TS(hot[:, 0, :], k["iota16"][:, :], dsh[:, bass.ds(t, 1)], None, ALU.is_equal).then_inc(hots, 1)
                    dve.wait_ge(hist, 1)
                    then(V.memset(tmp[:, :], 0.0))
                    then(V.tensor_tensor_scan(base[:, :], accv, tmp[:, :], 0.0, ALU.add, ALU.add))
                    then(TT(base[:, :], base[:, :], accv, ALU.subtract))
                    V.memset(tmp[:, 0:1], 0.0).then_inc(done1, 1)
                    first = then.n
                    with dve.Fori(0, NT) as t:
                        dve.wait_ge(used, t + NT)
                        TS(hot[:, 0, :], k["iota16"][:, :], dsh[:, bass.ds(t, 1)], None, ALU.is_equal).then_inc(hots, 1)
                        dve.wait_ge(ranked, t + 1)
                        TT(tmp[:, :], base[:, :], accv, ALU.add).then_inc(put, 1)
                        dve.wait_ge(put, t + 1)
                        TT(tmp[:, :], tmp[:, :], hot[:, 0, :], ALU.mult).then_inc(step, 1)
                        dve.wait_ge(step, 2 * t + first + 1)
                        V.tensor_reduce(place[:, bass.ds(t, 1)], tmp[:, :], AX.X, ALU.add).then_inc(step, 1)
                        dve.wait_ge(step, 2 * t + first + 2)
                    then.n = first + 2 * NT
                    then(TS(half[:, :], place[:, :], float(EP // 2), 3.0 * (EP // 2), ALU.is_ge, ALU.mult))
                    then(TT(aplace[:, :], place[:, :], half[:, :], ALU.add))
                    first = then.n
                    with dve.Fori(0, NT) as t:
                        dve.wait_ge(sent, 80 * t)
                        one = bass.ds(t, 1)
                        V.tensor_copy(vali[:, 0:1], srcs[:, one])
                        V.tensor_copy(vali[:, 1:2], dsts[:, one])
                        for j in range(3):
                            V.tensor_copy(val[:, 2 + j:3 + j], attr[:, j, one])
                            TS(pl[:, 2 + j:3 + j], aplace[:, one], float(j * (EP // 2)), None, ALU.add)
                        V.tensor_copy(pl[:, 0:1], place[:, one])
                        TS(pl[:, 1:2], place[:, one], 1.0, None, ALU.add).then_inc(shifted, 1)
                    dve.wait_ge(sent, 80 * NT)
SUP = 2
WS = SUP * BANK
HALF = NP // 2
HSPANS = [(i * BANK, min(BANK, HALF - i * BANK)) for i in range(-(-HALF // BANK))]
REST = NCH % SUP * BANK
assert NCH // SUP == 2 * NBK


def counts_and_network(nc, d, k):
    with ExitStack() as ctx:
        sb, ps, sem = tools(nc, ctx)
        src_hot = sb("src_hot", [P, 4, HALF + 2], F16)
        dst_hot = sb("dst_hot", [P, 4, P], F16)
        cbuf = sb("cbuf", [P, 2, HALF])
        acc = ps("acc", [P, 4, BANK])
        hot = [sem("hot0"), sem("hot1")]
        used = [sem("hot_used0"), sem("hot_used1")]
        drained = [sem(f"bank_drained{i}") for i in range(4)]
        summed = sem("pass_summed")
        stored = [sem("counts_stored0"), sem("counts_stored1")]
        attr = sb("en_attr", [8, 2, WS])
        wd1 = sb("en_wd1", [4, F])
        wd2 = sb("en_wd2", [F, F])
        bd2 = sb("en_bd2", [1, F])
        mean1 = sb("en_mean1", [4, 1])
        mean2 = sb("en_mean2", [F, 1])
        meanb = sb("en_meanb", [1, 1])
        blk1 = sb("en_blk1", [8, P])
        blk2 = sb("en_blk2", [P, P])
        avg = sb("en_avg", [P, P])
        pc = sb("en_pc", [P, 5])
        eps = sb("en_eps", [P, 1])
        sq = sb("en_sq", [P, WS])
        rs = sb("en_rs", [P, WS])
        d1 = sb("en_d1", [P, WS])
        out = sb("en_out", [P, 2, WS])
        pa = ps("en_pa", [P, SUP, BANK])
        pv = ps("en_pv", [P, SUP, BANK])
        wl, dsem, placed = sem("en_wl"), sem("en_dve"), sem("en_placed")
        a_loaded = [sem(f"en_a_loaded{s}") for s in range(2)]
        d_stored = [sem(f"en_stored{s}", pool_dma=True) for s in range(2)]
        lin_a = [sem(f"en_lin_a{s}") for s in range(2)]
        lin_b, sqd, var, lned, rstd, normed, geld = (
            sem(f"en_{x}") for x in ("lin_b", "sqd", "var", "lned", "rstd", "normed", "geld"))
        steps = {}

        def pair_row(eng, row, b):
            return eng.value_load(k["pairs"][0:1, row, bass.ds(b, 1)], min_val=0, max_val=NPAIR)

        def before_passes(eng, b):
            return [eng.value_load(k["pairs"][0:1, row, bass.ds(b, 1)], min_val=0, max_val=4 * NPAIR)
                    for row in (2, 3)]

        def flat(t, w):
            return t[:, 0:w // BANK, :].rearrange("p a b -> p (a b)")

        with nc.Block() as block:
            @block.vector
            def _(dve):
                V, TT, TS = nc.vector, nc.vector.tensor_tensor, nc.vector.tensor_scalar
                then = Count(dve, dsem)
                for j in range(2):
                    V.memset(src_hot[:, 2 * j:2 * j + 2, HALF:HALF + 2], 1.0).then_inc(used[j], 1)
                for t, v in ((blk1, 0.0), (blk2, 0.0), (eps, LN_EPS), (avg, 0.0)):
                    then(V.memset(t[:, :], v))
                for h in range(2):
                    then(V.memset(avg[h * F:(h + 1) * F, h * F:(h + 1) * F], 1 / F))
                dve.wait_ge(wl, 16 * 12)
                for w, m in ((wd1, mean1), (wd2, mean2), (bd2, meanb)):
                    then(V.tensor_reduce(m[:, :], w[:, :], AX.X, ALU.add))
                    then(TS(m[:, :], m[:, :], 1 / F, None, ALU.mult))
                    then(TS(w[:, :], w[:, :], m[:, 0:1], None, ALU.subtract))
                steps["centred"] = then.n

                def hots(b, s, done, lo, hi):
                    with dve.Fori(lo, hi) as t:
                        for j in range(2):
                            slot = (done + t) % 2 * 2 + j
                            dve.wait_ge(used[j], done + t)
                            TS(dst_hot[:, bass.ds(slot, 1), :], k["iota_blk"][:, :].unsqueeze(1),
                               k["blk_first"][:, bass.ds(b, 1)], k["dst_col"][:, bass.ds(2 * t + j, 1)],
                               ALU.add, ALU.is_equal)
                            TS(src_hot[:, bass.ds(slot, 1), 0:HALF],
                               k["iota16"][:, s * HALF:(s + 1) * HALF].unsqueeze(1),
                               k["src_sh"][:, bass.ds(2 * t + j, 1)], None, ALU.is_equal).then_inc(hot[j], 1)

                def norm_a(b, s, w):
                    dve.wait_ge(rstd, 4 * b + 2 * s + 1)
                    TT(d1[:, 0:w], flat(pa, w), rs[:, 0:w], ALU.mult).then_inc(normed, 1)

                def norm_b(b, s, w):
                    dve.wait_ge(rstd, 4 * b + 2 * s + 2)
                    dve.wait_ge(d_stored[s], 16 * b)
                    V.scalar_tensor_tensor(out=out[:, s, 0:w], in0=flat(pa, w), scalar=pc[:, 4:5], in1=rs[:, 0:w],
                                           op0=ALU.add, op1=ALU.mult).then_inc(normed, 1)

                for j in range(2):
                    dve.wait_ge(used[j], 1)
                with dve.Fori(0, NBK) as b:
                    p0, p1, cut3, cut7 = (pair_row(dve, r, b) for r in (0, 1, 5, 8))
                    for s, done in enumerate(before_passes(dve, b)):
                        hots(b, s, done, p0, cut3)
                        norm_a(b, s, WS)
                        hots(b, s, done, cut3, cut7)
                        norm_b(b, s, WS)
                        hots(b, s, done, cut7, p1)
                norm_a(NBK, 0, REST)
                norm_b(NBK, 0, REST)

            @block.tensor
            def _(pe):
                def add(done, t, first):
                    for j in range(2):
                        slot = (done + t) % 2 * 2 + j
                        pe.wait_ge(hot[j], done + t + 1)
                        for i, (a, w) in enumerate(HSPANS):
                            if first is not None and j == 0:
                                pe.wait_ge(drained[i], first)
                            w += 1 if a + w == HALF else 0
                            last = nc.tensor.matmul(acc[:, i, 0:w], dst_hot[:, bass.ds(slot, 1), :],
                                                    src_hot[:, bass.ds(slot, 1), a:a + w],
                                                    start=first is not None and j == 0, stop=False,
                                                    skip_group_check=True)
                        last.then_inc(used[j], 1)

                def adds(done, lo, hi):
                    with pe.Fori(lo, hi) as t:
                        add(done, t, None)

                def linear_a(b, s, w):
                    pe.wait_ge(a_loaded[s], 16 * b + 16)
                    pe.wait_ge(normed, 4 * b + 2 * s)
                    for i in range(w // BANK):
                        last = nc.tensor.matmul(pa[:, i, :], blk1[:, :], attr[:, s, i * BANK:(i + 1) * BANK],
                                                start=True, stop=True)
                    last.then_inc(lin_a[s], 1)

                def linear_b(b, s, w):
                    pe.wait_ge(geld, 4 * b + 2 * s + 1)
                    for i in range(w // BANK):
                        last = nc.tensor.matmul(pa[:, i, :], blk2[:, :], d1[:, i * BANK:(i + 1) * BANK],
                                                start=True, stop=True)
                    last.then_inc(lin_b, 1)

                def variance(b, s, w, r):
                    pe.wait_ge(sqd, 4 * b + 2 * s + r + 1)
                    for i in range(w // BANK):
                        last = nc.tensor.matmul(pv[:, i, :], avg[:, :], sq[:, i * BANK:(i + 1) * BANK],
                                                start=True, stop=True)
                    last.then_inc(var, 1)

                for j in range(2):
                    pe.wait_ge(used[j], 1)
                pe.wait_ge(placed, 16 * 6)
                with pe.Fori(0, NBK) as b:
                    p0, p1, cut1, cut4, cut5 = (pair_row(pe, r, b) for r in (0, 1, 4, 6, 7))
                    for s, done in enumerate(before_passes(pe, b)):
                        linear_a(b, s, WS)
                        add(done, p0, 2 * b + s)
                        adds(done, p0 + 1, cut1)
                        variance(b, s, WS, 0)
                        adds(done, cut1, cut4)
                        linear_b(b, s, WS)
                        adds(done, cut4, cut5)
                        variance(b, s, WS, 1)
                        adds(done, cut5, p1)
                        nc.tensor.matmul(acc[0:1, 3, BANK - 1:BANK], k["ones16"][:, 0:1], k["ones16"][:, 0:1],
                                         start=False, stop=True, skip_group_check=True).then_inc(summed, 1)
                linear_a(NBK, 0, REST)
                variance(NBK, 0, REST, 0)
                linear_b(NBK, 0, REST)
                variance(NBK, 0, REST, 1)

            @block.scalar
            def _(act):
                def rsqrt(b, s, w, r):
                    nc.scalar.activation(sq[:, 0:w], flat(pa, w), ACT.Square,
                                         bias=pc[:, 4:5] if r else 0.0).then_inc(sqd, 1)
                    nc.scalar.preload_act_table_set("natural_log_exp_and_others")
                    act.wait_ge(var, 4 * b + 2 * s + r + 1)
                    nc.scalar.activation(rs[:, 0:w], flat(pv, w), ACT.Ln, bias=eps[:, 0:1]).then_inc(lned, 1)
                    act.wait_ge(lned, 4 * b + 2 * s + r + 1)
                    nc.scalar.activation(rs[:, 0:w], rs[:, 0:w], ACT.Exp, scale=-0.5).then_inc(rstd, 1)

                def gelu(b, s, r, t):
                    act.wait_ge(normed, 4 * b + 2 * s + r + 1)
                    nc.scalar.activation(t, t, ACT.Gelu, scale=pc[:, 2 * r:2 * r + 1],
                                         bias=pc[:, 2 * r + 1:2 * r + 2]).then_inc(geld, 1)

                def first_layer(b, s, w):
                    act.wait_ge(lin_a[s], b + 1)
                    rsqrt(b, s, w, 0)
                    gelu(b, s, 0, d1[:, 0:w])
                    act.wait_ge(lin_b, 2 * b + s + 1)
                    rsqrt(b, s, w, 1)

                act.wait_ge(placed, 16 * 6)
                with act.Fori(0, NBK) as b:
                    for s in range(2):
                        first_layer(b, s, WS)
                        act.wait_ge(summed, 2 * b + s + 1)
                        act.wait_ge(stored[s], 16 * b)
                        for i, (a, w) in enumerate(HSPANS):
                            if s and a + w == HALF:
                                nc.scalar.copy(k["deg"][:, bass.ds(b, 1)], acc[:, i, w:w + 1])
                            nc.scalar.copy(cbuf[:, s, a:a + w], acc[:, i, 0:w]).then_inc(drained[i], 1)
                        gelu(b, s, 1, out[:, s, :])
                first_layer(NBK, 0, REST)
                gelu(NBK, 0, 1, out[:, 0, 0:REST])

            @block.sync
            def _(sp):
                sp.dma_start(wd1[0:3, :], d["Wd1"]).then_inc(wl, 16)
                sp.dma_start(wd1[3:4, :], d["bd1"].unsqueeze(0)).then_inc(wl, 16)
                sp.dma_start(wd2[:, :], d["Wd2"]).then_inc(wl, 16)
                sp.dma_start(bd2[:, :], d["bd2"].unsqueeze(0)).then_inc(wl, 16)
                for h in range(2):
                    for i, n in enumerate(("g1", "b1", "g2", "b2")):
                        sp.dma_start(pc[h * F:(h + 1) * F, i:i + 1], d[n].unsqueeze(1)).then_inc(wl, 16)
                sp.wait_ge(dsem, steps["centred"])
                for h in range(2):
                    sp.dma_start(blk1[4 * h:4 * h + 4, h * F:(h + 1) * F], wd1[:, :]).then_inc(placed, 16)
                    sp.dma_start(blk2[h * F:(h + 1) * F, h * F:(h + 1) * F], wd2[:, :]).then_inc(placed, 16)
                    sp.dma_start(pc[h * F:(h + 1) * F, 4:5], bd2[:, :]).then_inc(placed, 16)

                def load(b, s, w):
                    sp.wait_ge(lin_a[s], b)
                    sp.dma_start(attr[:, s, 0:w], d["attr8"][:, bass.ds((2 * b + s) * WS, w)]).then_inc(a_loaded[s], 16)

                def store(b, s):
                    for i in range(4):
                        sp.wait_ge(drained[i], 2 * b + s + 1)
                    sp.dma_start(d["counts"][bass.ds(b * P, P), s * HALF:(s + 1) * HALF],
                                 cbuf[:, s, :]).then_inc(stored[s], 16)
                load(0, 0, WS)
                with sp.Fori(0, NBK - 1) as b:
                    load(b, 1, WS)
                    store(b, 0)
                    load(b + 1, 0, WS)
                    store(b, 1)
                load(NBK - 1, 1, WS)
                store(NBK - 1, 0)
                load(NBK, 0, REST)
                store(NBK - 1, 1)
                for s in range(2):
                    sp.wait_ge(stored[s], 16 * NBK)

            @block.gpsimd
            def _(pool):
                def store(b, s, w):
                    pool.wait_ge(geld, 4 * b + 2 * s + 2)
                    pool.dma_start(d["dnet"][:, bass.ds((2 * b + s) * WS, w)], out[:, s, 0:w]).then_inc(d_stored[s], 16)
                with pool.Fori(0, NBK) as b:
                    store(b, 0, WS)
                    store(b, 1, WS)
                store(NBK, 0, REST)
                pool.wait_ge(d_stored[0], 16 * (NBK + 1))
                pool.wait_ge(d_stored[1], 16 * NBK)


def finish_norm(nc, act, dsem, at_, asem, nr, var):
    act.wait_ge(dsem, at_["var"])
    nc.scalar.sqrt(nr, var).then_inc(asem, 1)


def attention_rows(nc, d, k):
    with ExitStack() as ctx:
        sb, ps, sem = tools(nc, ctx)
        wrow = sb("ar_wrow", [P, F])
        a2row = sb("ar_a2row", [P, F])
        a1 = sb("ar_a1", [F, 1])
        a1b = sb("ar_a1b", [F, P])
        sq = sb("ar_sq", [P, NBK, F])
        sd = sb("ar_sd", [P, NBK])
        hT = sb("ar_hT", [F, NP])
        pt = ps("ar_pt", [P, 7, BANK])
        loaded, dsem, turned, evac, prod = (sem(f"ar_{x}") for x in ("loaded", "dve", "turned", "evac", "prod"))
        steps = {}
        with nc.Block() as block:
            @block.sync
            def _(sp):
                sp.dma_start(wrow[:, :], d["W1"].unsqueeze(0).to_broadcast([P, F])).then_inc(loaded, 16)
                sp.dma_start(a2row[:, :], d["a1"][F:2 * F].unsqueeze(0).to_broadcast([P, F])).then_inc(loaded, 16)
                sp.dma_start(a1[:, :], d["a1"][0:F].unsqueeze(1)).then_inc(loaded, 16)

            @block.vector
            def _(dve):
                then = Count(dve, dsem)
                steps["dve"] = then.at
                dve.wait_ge(loaded, 48)
                then(nc.vector.tensor_copy(a1b[:, :], a1[:, :].to_broadcast([F, P])))
                then(nc.vector.tensor_tensor(k["val"][:, :, 0:F], k["x"][:, :, :],
                                             wrow[:, :].unsqueeze(1).to_broadcast([P, NBK, F]), ALU.mult), "h")
                then(nc.vector.tensor_tensor(sq[:, :, :], k["val"][:, :, 0:F],
                                             a2row[:, :].unsqueeze(1).to_broadcast([P, NBK, F]), ALU.mult))
                then(nc.vector.tensor_reduce(sd[:, :], sq[:, :, :], AX.X, ALU.add))
                then(nc.vector.tensor_scalar(k["sdst"][:, 0, :], sd[:, :], 0.8, None, ALU.mult))
                then(nc.vector.tensor_scalar(k["sdst"][:, 1, :], sd[:, :], 0.2, None, ALU.mult))

            @block.tensor
            def _(pe):
                pe.wait_ge(dsem, steps["dve"]["h"])
                turn_blocks(pe, nc, k, pt, k["val"], F, turned)
                pe.wait_ge(evac, 1)
                for i, (a, w) in enumerate(SPANS):
                    last = nc.tensor.matmul(pt[:, i, 0:w], a1b[:, :], hT[:, a:a + w], start=True, stop=True)
                last.then_inc(prod, 1)

            @block.scalar
            def _(act):
                act.wait_ge(turned, 1)
                for i, (a, w) in enumerate(SPANS):
                    last = nc.scalar.copy(hT[:, a:a + w], pt[0:F, i, 0:w])
                last.then_inc(evac, 1)
                act.wait_ge(prod, 1)
                for i, (a, w) in enumerate(SPANS):
                    nc.scalar.copy(k["toprow"][:, a:a + w], pt[:, i, 0:w])


def score_sums(nc, d, k):
    with ExitStack() as ctx:
        sb, ps, sem = tools(nc, ctx)
        cnt = sb("ss_cnt", [P, 2, NP])
        z = sb("ss_z", [P, 2, NP])
        w_ = sb("ss_w", [P, 2, NP])
        val = sb("ss_val", [P, 2, W65])
        acc = ps("ss_acc", [P, 7, BANK])
        loaded, relued, added, exped, weighed, val_ready, summed = (
            [sem(f"ss_{x}{s}") for s in range(2)]
            for x in ("loaded", "relued", "added", "exped", "weighed", "val_ready", "summed"))
        done = sem("ss_done")
        with nc.Block() as block:
            @block.sync
            def _(sp):
                def load(h, s):
                    sp.wait_ge(weighed[s], h)
                    sp.dma_start(cnt[:, s, :], d["counts"][bass.ds((2 * h + s) * P, P), :]).then_inc(loaded[s], 16)
                over_blocks(sp, load)

            @block.gpsimd
            def _(pool):
                def body(h, s):
                    pool.wait_ge(summed[s], h)
                    nc.gpsimd.tensor_copy(val[:, s, :].unsqueeze(1), k["val"][:, bass.ds(2 * h + s, 1), 0:W65])\
                      .then_inc(val_ready[s], 1)
                over_blocks(pool, body)

            @block.scalar
            def _(act):
                def relu(h, s):
                    act.wait_ge(weighed[s], h)
                    nc.scalar.activation(z[:, s, :], k["toprow"][:, :], ACT.Relu, scale=0.8,
                                         bias=k["sdst"][:, 0, bass.ds(2 * h + s, 1)]).then_inc(relued[s], 1)

                def exp(h, s):
                    act.wait_ge(added[s], h + 1)
                    nc.scalar.activation(z[:, s, :], z[:, s, :], ACT.Exp,
                                         bias=k["sdst"][:, 1, bass.ds(2 * h + s, 1)]).then_inc(exped[s], 1)
                relu(0, 0)
                with act.Fori(0, NBK // 2) as h:
                    relu(h, 1)
                    exp(h, 0)
                    relu(h + 1, 0)
                    exp(h, 1)
                exp(NBK // 2, 0)
                act.wait_ge(done, 1)
                for i, (a, w) in enumerate(SPANS):
                    nc.scalar.copy(k["sums"][0:W65, a:a + w], acc[0:W65, i, 0:w])

            @block.vector
            def _(dve):
                def add(h, s):
                    dve.wait_ge(relued[s], h + 1)
                    nc.vector.scalar_tensor_tensor(out=z[:, s, :], in0=k["toprow"][:, :], scalar=0.2, in1=z[:, s, :],
                                                   op0=ALU.mult, op1=ALU.add).then_inc(added[s], 1)

                def weigh(h, s):
                    dve.wait_ge(exped[s], h + 1)
                    dve.wait_ge(loaded[s], 16 * h + 16)
                    dve.wait_ge(summed[s], h)
                    nc.vector.scalar_tensor_tensor(out=w_[:, s, :], in0=z[:, s, :], scalar=3e38, in1=cnt[:, s, :],
                                                   op0=ALU.min, op1=ALU.mult).then_inc(weighed[s], 1)
                add(0, 0)
                with dve.Fori(0, NBK // 2) as h:
                    add(h, 1)
                    weigh(h, 0)
                    add(h + 1, 0)
                    weigh(h, 1)
                weigh(NBK // 2, 0)

            @block.tensor
            def _(pe):
                zero_sums(nc, k, acc, W65)

                def body(h, s):
                    pe.wait_ge(weighed[s], h + 1)
                    pe.wait_ge(val_ready[s], h + 1)
                    for i, (a, w) in enumerate(SPANS):
                        last = nc.tensor.matmul(acc[0:W65, i, 0:w], val[:, s, :], w_[:, s, a:a + w],
                                                start=False, stop=False, skip_group_check=True)
                    last.then_inc(summed[s], 1)
                over_blocks(pe, body)
                nc.tensor.matmul(acc[0:1, 6, BANK - 1:BANK], k["zeros"][:, 0:1], k["zeros"][:, 0:1],
                                 start=False, stop=True, skip_group_check=True).then_inc(done, 1)


def end_attention(nc, d, k):
    with ExitStack() as ctx:
        sb, ps, sem = tools(nc, ctx)
        v = sb("ea_v", [P, NBK, F])
        t = sb("ea_t", [P, NBK, F])
        xT = sb("ea_xT", [F, NP])
        w123 = sb("ea_w123", [F, 3 * F])
        w23 = sb("ea_w23", [P, NBK, 2 * F])
        col = sb("ea_col", [P, 4, NBK])
        den, nr, t1, t2 = (col[:, i, :] for i in range(4))
        pb = ps("ea_pb", [P, 7, BANK])
        back, dsem, asem, loaded, turned, evac, prod, kept, pb_free, stored = (
            sem(f"ea_{x}") for x in ("back", "dve", "act", "loaded", "turned", "evac", "prod", "kept", "pb_free",
                                     "stored"))
        x = k["x"]
        steps = {}
        NROUND = -(-NBK // 14)
        with nc.Block() as block:
            @block.sync
            def _(sp):
                for i, n in enumerate(("W2_1", "W2_2", "W2_3")):
                    sp.dma_start(w123[:, i * F:(i + 1) * F], d[n]).then_inc(loaded, 16)
                sp.wait_ge(kept, 4 * NROUND)
                sp.dma_start(d["w23"].rearrange("(b p) f -> p b f", p=P), w23[:, :, :]).then_inc(stored, 16)
                sp.wait_ge(stored, 16)

            @block.vector
            def _(dve):
                then = Count(dve, dsem)
                steps["dve"] = then.at
                dve.wait_ge(back, 1)
                for g in range(4):
                    lo, hi = 7 * g, min(NBK, 7 * g + 7)
                    rows = pb[:, g, 0:(hi - lo) * W65].rearrange("p (b f) -> p b f", f=W65)
                    then(nc.vector.tensor_tensor(den[:, lo:hi], rows[:, :, F], k["is_pad"][:, lo:hi], ALU.add))
                    then(nc.vector.reciprocal(den[:, lo:hi], den[:, lo:hi]))
                    then(nc.vector.tensor_tensor(v[:, lo:hi, :], rows[:, :, 0:F],
                                                 den[:, lo:hi].unsqueeze(2).to_broadcast([P, hi - lo, F]), ALU.mult))
                elu(nc, then, lambda: dve.wait_ge(asem, 1), v[:, :, :], t[:, :, :])
                then(nc.vector.tensor_tensor(x[:, :, :], x[:, :, :], v[:, :, :], ALU.add))
                layernorm_stats(nc, then, x[:, :, :], t, t1, t2, "var")
                dve.wait_ge(asem, 2)
                then(nc.vector.reciprocal(t1, nr))
                then(nc.vector.tensor_tensor(x[:, :, :], x[:, :, :], spread(t1), ALU.mult), "x")

            @block.scalar
            def _(act):
                at_ = steps["dve"]
                act.wait_ge(dsem, at_["elu"])
                nc.scalar.activation(t[:, :, :], t[:, :, :], ACT.Exp).then_inc(asem, 1)
                finish_norm(nc, act, dsem, at_, asem, nr, t2)
                act.wait_ge(turned, 1)
                for i, (a, w) in enumerate(SPANS):
                    last = nc.scalar.copy(xT[:, a:a + w], pb[0:F, i, 0:w])
                last.then_inc(evac, 1)
                for r in range(NROUND):
                    act.wait_ge(prod, r + 1)
                    for j in range(2):
                        b0, b1 = 14 * r, min(NBK, 14 * r + 14)
                        n2 = (b1 - b0 + 1) // 2
                        for q in range(2):
                            n = len(range(b0 + q, b1, 2))
                            src = pb[:, 0:n, q * 3 * F:(q + 1) * 3 * F]
                            if j == 0:
                                last = nc.scalar.copy(k["w1x"][:, b0 + q:b1:2, :], src[:, :, 0:F])
                            else:
                                last = nc.scalar.copy(w23[:, b0 + q:b1:2, :], src[:, :, F:3 * F])
                            last.then_inc(kept, 1)
                        del n2

            @block.tensor
            def _(pe):
                back_blocks(pe, nc, k, pb, k["sums"], W65, back)
                pe.wait_ge(dsem, steps["dve"]["x"])
                turn_blocks(pe, nc, k, pb, x, F, turned)
                pe.wait_ge(evac, 1)
                pe.wait_ge(loaded, 48)
                for r in range(NROUND):
                    if r:
                        pe.wait_ge(kept, 4 * r)
                    for b in range(14 * r, min(NBK, 14 * r + 14)):
                        i = b - 14 * r
                        last = nc.tensor.matmul(pb[:, i // 2, (i % 2) * 3 * F:(i % 2 + 1) * 3 * F],
                                                xT[:, b * P:(b + 1) * P], w123[:, :], start=True, stop=True)
                    last.then_inc(prod, 1)
            del pb_free


def over_pairs(eng, n, body):
    with eng.Fori(0, n // 2) as h:
        body(h, 0)
        body(h, 1)
    body(n // 2, 0)


ROW = 3 * F


def edge_softmax(nc, d, k):
    with ExitStack() as ctx:
        sb, ps, sem = tools(nc, ctx)
        idx = sb("es_idx", [P, 2, 2, CT], I32)
        opened = sem("es_opened")
        got = sb("es_got", [P, 2, CT, 2, 2 * F])
        dn = sb("es_dn", [P, 2, BANK])
        st = sb("es_st", [2, 2, BANK], BF16)
        sel = sb("es_sel", [2, P], BF16)
        lg = sb("es_lg", [P, 2, BANK])
        v3 = sb("es_v3", [P, 2, BANK])
        mx = sb("es_mx", [P, 2, BANK + 1])
        dec = sb("es_dec", [P, 2, BANK])
        e = sb("es_e", [P, 2, BANK])
        ev = sb("es_ev", [P, 2, BANK])
        s0 = sb("es_s0", [P, 2, BANK])
        s1 = sb("es_s1", [P, 2, BANK])
        rows = sb("es_rows", [P, 2, CT, 2, ROW])
        w2p = ps("es_w2p", [P, BANK])
        w3p = ps("es_w3p", [P, BANK])
        pen = ps("es_pen", [P, 2, BANK])
        rp = ps("es_rp", [P, 4, BANK])
        idx_ready, dn_loaded, stored, st_loaded = (
            [sem(f"es_{x}{s}") for s in range(2)] for x in ("idx_ready", "dn_loaded", "stored", "st_loaded"))
        gathered = [sem(f"es_gathered{s}", pool_dma=True) for s in range(2)]
        one = ("sel_made", "turned2", "turned3", "penned", "lg_ready", "v3_ready", "max_ready", "pen_used", "dec_in", "e_in",
               "dec_ready", "e_ready", "ev_ready", "s0_ready", "s1_ready", "rows_turned", "rows_out", "carry", "zeroed")
        (sel_made, turned2, turned3, penned, lg_ready, v3_ready, max_ready, pen_used, dec_in, e_in,
         dec_ready, e_ready, ev_ready, s0_ready, s1_ready, rows_turned, rows_out, carry, zeroed) = (
             sem(f"es_{x}") for x in one)
        with nc.Block() as block:
            @block.gpsimd
            def _(pool):
                def body(h, s):
                    pool.wait_ge(gathered[s], 16 * 2 * CT * h)
                    for half in range(2):
                        last = nc.gpsimd.tensor_copy(
                            idx[:, s, half, :], k["src_idx"][:, bass.ds(half * HT + (2 * h + s) * CT, CT)])
                    last.then_inc(idx_ready[s], 1)
                    pool.wait_ge(idx_ready[s], h + 1)
                    pool.wait_ge(turned3, 2 * h)
                    pool.sem_inc(opened, 1)
                    for t in range(CT):
                        for half in range(2):
                            pool.indirect_dma_start(
                                got[:, s, t, half, :], None, d["w23"],
                                bass.IndirectOffsetOnAxis(ap=idx[:, s, half, t:t + 1], axis=0)).then_inc(gathered[s], 16)
                over_pairs(pool, NCH, body)

            @block.sync
            def _(sp):
                def load(h, s):
                    c = 2 * h + s
                    sp.wait_ge(penned, 2 * h)
                    sp.wait_ge(v3_ready, 2 * h)
                    sp.dma_start(dn[:, s, :], d["dnet"][:, bass.ds(c * BANK, BANK)]).then_inc(dn_loaded[s], 16)
                    sp.dma_start(st[:, s, :], d["starts"][:, bass.ds(c * BANK, BANK)]).then_inc(st_loaded[s], 16)
                over_pairs(sp, NCH, load)

            @block.tensor
            def _(pe):
                pe.wait_ge(sel_made, 1)

                def turn_in(h, s):
                    c = 2 * h + s
                    pe.wait_ge(st_loaded[s], 16 * h + 16)
                    pe.wait_ge(pen_used, 2 * h)
                    nc.tensor.matmul(pen[:, s, :], sel[:, :], st[:, s, :], start=True, stop=True).then_inc(penned, 1)
                    pe.wait_ge(gathered[s], 16 * 2 * CT * (h + 1))
                    pe.wait_ge(lg_ready, c)
                    for t in range(CT):
                        for half in range(2):
                            last = nc.tensor.matmul(w2p[half * F:(half + 1) * F, t * P:(t + 1) * P],
                                                    got[:, s, t, half, 0:F], k["ident"][:, :], start=True, stop=True)
                    last.then_inc(turned2, 1)
                    pe.wait_ge(v3_ready, c)
                    for t in range(CT):
                        for half in range(2):
                            last = nc.tensor.matmul(w3p[half * F:(half + 1) * F, t * P:(t + 1) * P],
                                                    got[:, s, t, half, F:2 * F], k["ident"][:, :], start=True, stop=True)
                    last.then_inc(turned3, 1)

                def turn_out(h, s):
                    c = 2 * h + s
                    for i, (x, done) in enumerate(((mx, max_ready), (s0, s0_ready), (s1, s1_ready))):
                        pe.wait_ge(done, c + 1)
                    pe.wait_ge(rows_out, CT * c)
                    for t in range(CT):
                        for i, x in enumerate((mx, s0, s1)):
                            o = 1 if i == 0 else 0
                            last = nc.tensor.transpose(rp[:, t, i * P:(i + 1) * P],
                                                       x[:, s, o + t * P:o + (t + 1) * P], k["ident"][:, :])
                        last.then_inc(rows_turned, 1)
                turn_in(0, 0)
                with pe.Fori(0, NCH // 2) as h:
                    turn_in(h, 1)
                    turn_out(h, 0)
                    turn_in(h + 1, 0)
                    turn_out(h, 1)
                turn_out(NCH // 2, 0)

            @block.vector
            def _(dve):
                nc.vector.memset(mx[:, 1, BANK:BANK + 1], -BIG).then_inc(zeroed, 1)
                nc.vector.memset(s0[:, 1, BANK - 1:BANK], 0.0).then_inc(zeroed, 1)
                nc.vector.memset(s1[:, 1, BANK - 1:BANK], 0.0).then_inc(zeroed, 1)
                dve.wait_ge(zeroed, 3)

                def body(h, s):
                    c = 2 * h + s
                    o = 1 - s
                    dve.wait_ge(dn_loaded[s], 16 * h + 16)
                    dve.wait_ge(turned2, c + 1)
                    dve.wait_ge(e_in, 2 * h)
                    nc.vector.tensor_tensor(lg[:, s, :], dn[:, s, :], w2p[:, :], ALU.subtract).then_inc(lg_ready, 1)
                    dve.wait_ge(turned3, c + 1)
                    nc.vector.tensor_tensor(v3[:, s, :], dn[:, s, :], w3p[:, :], ALU.add).then_inc(v3_ready, 1)
                    dve.wait_ge(penned, c + 1)
                    dve.wait_ge(rows_turned, 2 * CT * h)
                    nc.vector.tensor_copy(mx[:, s, 0:1], mx[:, o, BANK:BANK + 1]).then_inc(carry, 1)
                    dve.wait_ge(lg_ready, c + 1)
                    nc.vector.tensor_tensor_scan(mx[:, s, 1:BANK + 1], pen[:, s, :], lg[:, s, :],
                                                 mx[:, o, BANK:BANK + 1], ALU.add, ALU.max).then_inc(max_ready, 1)
                    dve.wait_ge(carry, c + 1)
                    dve.wait_ge(max_ready, c + 1)
                    nc.vector.tensor_tensor(dec[:, s, :], pen[:, s, :], mx[:, s, 0:BANK], ALU.add).then_inc(pen_used, 1)
                    nc.vector.tensor_tensor(e[:, s, :], lg[:, s, :], mx[:, s, 1:BANK + 1], ALU.subtract).then_inc(e_in, 1)
                    dve.wait_ge(pen_used, c + 1)
                    nc.vector.tensor_tensor(dec[:, s, :], dec[:, s, :], mx[:, s, 1:BANK + 1],
                                            ALU.subtract).then_inc(dec_in, 1)
                    dve.wait_ge(e_ready, c + 1)
                    dve.wait_ge(v3_ready, c + 1)
                    nc.vector.tensor_tensor(ev[:, s, :], e[:, s, :], v3[:, s, :], ALU.mult).then_inc(ev_ready, 1)
                    dve.wait_ge(dec_ready, c + 1)
                    nc.vector.tensor_tensor_scan(s0[:, s, :], dec[:, s, :], e[:, s, :], s0[:, o, BANK - 1:BANK],
                                                 ALU.mult, ALU.add).then_inc(s0_ready, 1)
                    dve.wait_ge(ev_ready, c + 1)
                    nc.vector.tensor_tensor_scan(s1[:, s, :], dec[:, s, :], ev[:, s, :], s1[:, o, BANK - 1:BANK],
                                                 ALU.mult, ALU.add).then_inc(s1_ready, 1)
                    dve.wait_ge(s0_ready, c + 1)
                    dve.wait_ge(s1_ready, c + 1)
                over_pairs(dve, NCH, body)

            @block.scalar
            def _(act):
                nc.scalar.copy(sel[:, :], k["half_sel"][:, :]).then_inc(sel_made, 1)

                def exps(h, s):
                    c = 2 * h + s
                    act.wait_ge(e_in, c + 1)
                    nc.scalar.activation(e[:, s, :], e[:, s, :], ACT.Exp).then_inc(e_ready, 1)
                    act.wait_ge(dec_in, c + 1)
                    nc.scalar.activation(dec[:, s, :], dec[:, s, :], ACT.Exp).then_inc(dec_ready, 1)

                def rows_to(h, s):
                    c = 2 * h + s
                    act.wait_ge(stored[s], 16 * 2 * h)
                    for t in range(CT):
                        act.wait_ge(rows_turned, CT * c + t + 1)
                        nc.scalar.copy(rows[:, s, t, :, :].rearrange("p h (q f) -> p h q f", f=F),
                                       rp[:, t, 0:3 * P].rearrange("p (q h f) -> p h q f", q=3, h=2)).then_inc(rows_out, 1)
                    act.wait_ge(rows_out, CT * c + CT)
                    for half in range(2):
                        r = (half * HT + c * CT) * P
                        act.dma_start(d["rows"][bass.ds(r, CT * P), :].rearrange("(t p) w -> p t w", p=P),
                                      rows[:, s, :, half, :]).then_inc(stored[s], 16)
                exps(0, 0)
                with act.Fori(0, NCH // 2) as h:
                    exps(h, 1)
                    rows_to(h, 0)
                    exps(h + 1, 0)
                    rows_to(h, 1)
                rows_to(NCH // 2, 0)
                act.wait_ge(stored[0], 32 * (NCH // 2 + 1))
                act.wait_ge(stored[1], 32 * (NCH // 2))


def end_edges(nc, d, k):
    with ExitStack() as ctx:
        sb, ps, sem = tools(nc, ctx)
        col = sb("ee_col", [P, 12, NBK])
        cum, last_, first, stra, has, idf, t1, t2, nr, t3, deg1, tot = (col[:, i, :] for i in range(12))
        idx = sb("ee_idx", [P, NBK], I32)
        mid = sb("ee_mid", [P, ROW])
        r = sb("ee_r", [P, NBK, ROW])
        l2 = sb("ee_l2", [P, NBK, F])
        a = sb("ee_a", [P, NBK, F])
        b_ = sb("ee_b", [P, NBK, F])
        m = sb("ee_m", [P, NBK, F])
        zf = sb("ee_zf", [P, NBK])
        pp = ps("ee_pp", [P, 2, BANK])
        dsem, asem, loaded, prods = (sem(f"ee_{x}") for x in ("dve", "act", "loaded", "prods"))
        gathered = sem("ee_gathered", pool_dma=True)
        x, w1, deg = k["x"], k["w1x"], k["deg"]
        MID = float(EP // 2)
        steps = {}
        with nc.Block() as block:
            @block.sync
            def _(sp):
                sp.dma_start(mid[:, :], d["rows"][EP // 2 - 1:EP // 2, :].to_broadcast([P, ROW])).then_inc(loaded, 16)

            @block.tensor
            def _(pe):
                nc.tensor.matmul(pp[:, 0, 0:NBK], k["upper"][:, :], deg[:, :], start=True, stop=True)
                nc.tensor.matmul(pp[:, 1, 0:NBK], k["ones"][:, :], deg[:, :], start=True, stop=True).then_inc(prods, 1)

            @block.vector
            def _(dve):
                then = Count(dve, dsem)
                steps["dve"] = then.at
                V, TT, TS = nc.vector, nc.vector.tensor_tensor, nc.vector.tensor_scalar
                dve.wait_ge(prods, 1)
                then(V.memset(zf[:, :], 0.0))
                then(V.tensor_copy(tot, pp[:, 1, 0:NBK]))
                then(V.tensor_tensor_scan(t1, tot, zf[:, :], 0.0, ALU.add, ALU.add))
                then(TT(t1, t1, tot, ALU.subtract))
                then(TT(cum, t1, pp[:, 0, 0:NBK], ALU.add))
                then(TS(last_, cum, -1.0, None, ALU.add))
                then(TT(first, cum, deg[:, :], ALU.subtract))
                then(TS(has, deg[:, :], 1.0, None, ALU.min))
                then(TS(stra, first, MID, None, ALU.is_lt))
                then(TS(t2, last_, MID, None, ALU.is_ge))
                then(TT(stra, stra, t2, ALU.mult))
                then(TT(stra, stra, has, ALU.mult))
                then(TS(idf, last_, 0.0, None, ALU.max))
                then(V.tensor_copy(idx[:, :], idf), "idx")
                dve.wait_ge(loaded, 16)
                dve.wait_ge(gathered, 16 * NBK)
                m1, s0, s1 = (r[:, :, i * F:(i + 1) * F] for i in range(3))
                m2, z0, z1 = (mid[:, i * F:(i + 1) * F].unsqueeze(1).to_broadcast([P, NBK, F]) for i in range(3))
                then(TT(l2[:, :, :], w1[:, :, :], m2, ALU.add))
                then(TT(a[:, :, :], w1[:, :, :], m1, ALU.add))
                then(TT(m[:, :, :], l2[:, :, :], a[:, :, :], ALU.subtract))
                then(TS(m[:, :, :], m[:, :, :], 0.0, None, ALU.max))
                then(TT(m[:, :, :], m[:, :, :], spread(stra), ALU.mult))
                then(TT(m[:, :, :], m[:, :, :], a[:, :, :], ALU.add))
                then(TT(a[:, :, :], a[:, :, :], m[:, :, :], ALU.subtract))
                then(TT(b_[:, :, :], l2[:, :, :], m[:, :, :], ALU.subtract))
                then(TS(b_[:, :, :], b_[:, :, :], 0.0, None, ALU.min), "shifts")
                dve.wait_ge(asem, 2)
                then(TT(b_[:, :, :], b_[:, :, :], spread(stra), ALU.mult))
                then(TT(m[:, :, :], s0, a[:, :, :], ALU.mult))
                then(TT(l2[:, :, :], b_[:, :, :], z0, ALU.mult))
                then(TT(m[:, :, :], m[:, :, :], l2[:, :, :], ALU.add))
                then(V.reciprocal(m[:, :, :], m[:, :, :]))
                then(TT(m[:, :, :], m[:, :, :], spread(has), ALU.mult))
                then(TT(a[:, :, :], a[:, :, :], s1, ALU.mult))
                then(TT(b_[:, :, :], b_[:, :, :], z1, ALU.mult))
                then(TT(a[:, :, :], a[:, :, :], b_[:, :, :], ALU.add))
                then(TT(a[:, :, :], a[:, :, :], m[:, :, :], ALU.mult))
                then(TT(x[:, :, :], x[:, :, :], a[:, :, :], ALU.add))
                layernorm_stats(nc, then, x[:, :, :], a, t1, t2, "var")
                dve.wait_ge(asem, 3)
                then(V.reciprocal(t1, nr))
                then(TT(x[:, :, :], x[:, :, :], spread(t1), ALU.mult))

            @block.gpsimd
            def _(pool):
                pool.wait_ge(dsem, steps["dve"]["idx"])
                for b in range(NBK):
                    pool.indirect_dma_start(r[:, b, :], None, d["rows"],
                                            bass.IndirectOffsetOnAxis(ap=idx[:, b:b + 1], axis=0)).then_inc(gathered, 16)

            @block.scalar
            def _(act):
                at_ = steps["dve"]
                act.wait_ge(dsem, at_["shifts"])
                nc.scalar.activation(a[:, :, :], a[:, :, :], ACT.Exp).then_inc(asem, 1)
                nc.scalar.activation(b_[:, :, :], b_[:, :, :], ACT.Exp).then_inc(asem, 1)
                act.wait_ge(dsem, at_["var"])
                nc.scalar.sqrt(nr, t2).then_inc(asem, 1)
            del t3, deg1


HID = 2 * F


def sum_neighbours(nc, d, k, first, val, agg):
    tag = "n1" if first else "n2"
    with ExitStack() as ctx:
        sb, ps, sem = tools(nc, ctx)
        cnt = sb(f"{tag}_cnt", [P, 2, NP])
        ct = sb(f"{tag}_ct", [P, 2, NP]) if first else cnt
        tp = ps(f"{tag}_tp", [P, 4, BANK])
        acc = ps(f"{tag}_acc", [P, 2, BANK])
        loaded, turned, copied, summed, taken = (
            [sem(f"{tag}_{x}{s}") for s in range(2)] for x in ("loaded", "turned", "copied", "summed", "taken"))
        stored = [sem(f"{tag}_stored{s}", pool_dma=True) for s in range(2)] if first else None
        NS = len(SPANS)
        with nc.Block() as block:
            @block.sync
            def _(sp):
                def load(h, s):
                    if first:
                        sp.wait_ge(turned[s], NS * h)
                    else:
                        sp.wait_ge(summed[s], h)
                    sp.dma_start(cnt[:, s, :], (d["counts"] if first else d["turned"])[bass.ds((2 * h + s) * P, P), :])\
                      .then_inc(loaded[s], 16)
                over_blocks(sp, load)

            if first:
                @block.gpsimd
                def _(pool):
                    def store(h, s):
                        pool.wait_ge(copied[s], NS * h + NS)
                        pool.dma_start(d["turned"][bass.ds((2 * h + s) * P, P), :], ct[:, s, :]).then_inc(stored[s], 16)
                    over_blocks(pool, store)
                    pool.wait_ge(stored[0], 16 * (NBK // 2 + 1))
                    pool.wait_ge(stored[1], 16 * (NBK // 2))

                @block.scalar
                def _(act):
                    def body(h, s):
                        act.wait_ge(stored[s], 16 * h)
                        act.wait_ge(summed[s], h)
                        for i, (a, w) in enumerate(SPANS):
                            act.wait_ge(turned[s], NS * h + i + 1)
                            nc.scalar.copy(ct[:, s, a:a + w], tp[:, i % 4, 0:w]).then_inc(copied[s], 1)
                    over_blocks(act, body)

            @block.tensor
            def _(pe):
                def turn(h, s):
                    pe.wait_ge(loaded[s], 16 * h + 16)
                    pe.wait_ge(copied[1 - s], NS * (h + s))
                    for i, (a, w) in enumerate(SPANS):
                        if i >= 4:
                            pe.wait_ge(copied[s], NS * h + i - 3)
                        for j in range(w // P):
                            last = nc.tensor.transpose(tp[:, i % 4, j * P:(j + 1) * P],
                                                       cnt[:, s, a + j * P:a + (j + 1) * P], k["ident"][:, :])
                        last.then_inc(turned[s], 1)

                def add(h, s):
                    if first:
                        pe.wait_ge(copied[s], NS * h + NS)
                    else:
                        pe.wait_ge(loaded[s], 16 * h + 16)
                    pe.wait_ge(taken[s], h)
                    for b in range(NBK):
                        last = nc.tensor.matmul(acc[:, s, 0:F], ct[:, s, b * P:(b + 1) * P], val[:, b, 0:F],
                                                start=(b == 0), stop=(b == NBK - 1))
                    last.then_inc(summed[s], 1)

                if first:
                    turn(0, 0)
                    with pe.Fori(0, NBK // 2) as h:
                        turn(h, 1)
                        add(h, 0)
                        turn(h + 1, 0)
                        add(h, 1)
                    add(NBK // 2, 0)
                else:
                    over_blocks(pe, add)

            @block.vector
            def _(dve):
                def take(h, s):
                    dve.wait_ge(summed[s], h + 1)
                    nc.vector.tensor_copy(agg[:, bass.ds(2 * h + s, 1), :], acc[:, s, 0:F].unsqueeze(1))\
                       .then_inc(taken[s], 1)
                over_blocks(dve, take)


def sage_values(nc, d, k):
    with ExitStack() as ctx:
        _, _, sem = tools(nc, ctx)
        step = sem("sv_step")
        with nc.Block() as block:
            @block.vector
            def _(dve):
                then = Count(dve, step)
                then(nc.vector.tensor_scalar(k["safe"][:, :, :], k["x"][:, :, :], BIG, -BIG, ALU.min, ALU.max))
                then(nc.vector.tensor_scalar(k["inv_deg"][:, :], k["deg"][:, :], 1.0, None, ALU.max))
                then(nc.vector.reciprocal(k["inv_deg"][:, :], k["inv_deg"][:, :]))


def sage_hidden(nc, d, k):
    with ExitStack() as ctx:
        sb, ps, sem = tools(nc, ctx)
        mxn = sb("sh_mxn", [P, NBK, 2 * F])
        hid = sb("sh_hid", [P, NBK, HID])
        sq = sb("sh_sq", [P, NBK, HID])
        cols = sb("sh_cols", [P, NP])
        w1 = sb("sh_w1", [2 * F, HID])
        w3 = sb("sh_w3", [HID, 2 * F])
        b1 = sb("sh_b1", [P, HID])
        col = sb("sh_col", [P, 2, NBK])
        ss, nr = (col[:, i, :] for i in range(2))
        pt = ps("sh_pt", [P, 7, BANK])
        loaded, dsem, asem, turned, evac, prod, kept = (
            sem(f"sh_{x}") for x in ("loaded", "dve", "act", "turned", "evac", "prod", "kept"))
        steps = {}
        with nc.Block() as block:
            @block.sync
            def _(sp):
                sp.dma_start(w1[0:F, :], d["W1_l"]).then_inc(loaded, 16)
                sp.dma_start(w1[F:2 * F, :], d["W1_r"]).then_inc(loaded, 16)
                sp.dma_start(w3[:, 0:F], d["W3_l"]).then_inc(loaded, 16)
                sp.dma_start(w3[:, F:2 * F], d["W3_r"]).then_inc(loaded, 16)
                sp.dma_start(b1[:, :], d["sb1"].unsqueeze(0).to_broadcast([P, HID])).then_inc(loaded, 16)

            @block.vector
            def _(dve):
                then = Count(dve, dsem)
                steps["dve"] = then.at
                then(nc.vector.tensor_tensor(mxn[:, :, 0:F], k["agg"][:, :, :], spread(k["inv_deg"][:, :]), ALU.mult))
                then(nc.vector.tensor_copy(mxn[:, :, F:2 * F], k["x"][:, :, :]), "mxn")
                dve.wait_ge(loaded, 80)
                dve.wait_ge(prod, 1)
                for g in range(7):
                    lo, hi = 4 * g, min(NBK, 4 * g + 4)
                    then(nc.vector.tensor_tensor(
                        hid[:, lo:hi, :], pt[:, g, 0:(hi - lo) * HID].rearrange("p (b f) -> p b f", f=HID),
                        b1[:, :].unsqueeze(1).to_broadcast([P, hi - lo, HID]), ALU.add))
                then(nc.vector.tensor_tensor(sq[:, :, :], hid[:, :, :], hid[:, :, :], ALU.mult))
                then(nc.vector.tensor_reduce(ss, sq[:, :, :], AX.X, ALU.add), "sq")
                dve.wait_ge(asem, 1)
                then(nc.vector.tensor_scalar(nr, nr, 1e-12, None, ALU.max))
                then(nc.vector.reciprocal(nr, nr))
                then(nc.vector.tensor_tensor(hid[:, :, :], hid[:, :, :], spread(nr, HID), ALU.mult))
                then(nc.vector.tensor_scalar(hid[:, :, :], hid[:, :, :], 0.0, None, ALU.max), "hid")
                dve.wait_ge(kept, 1)
                then(nc.vector.tensor_scalar(k["safe"][:, :, :], k["safe"][:, :, :], BIG, -BIG, ALU.min, ALU.max))

            @block.scalar
            def _(act):
                at_ = steps["dve"]
                for r in range(2):
                    act.wait_ge(turned, r + 1)
                    for i, (a, w) in enumerate(SPANS):
                        last = nc.scalar.copy(cols[:, a:a + w], pt[:, i, 0:w])
                    last.then_inc(evac, 1)
                    if r == 0:
                        act.wait_ge(dsem, at_["sq"])
                        nc.scalar.sqrt(nr, ss).then_inc(asem, 1)
                act.wait_ge(prod, 2)
                for g in range(7):
                    lo, hi = 4 * g, min(NBK, 4 * g + 4)
                    v = pt[:, g, 0:(hi - lo) * 2 * F].rearrange("p (b f) -> p b f", f=2 * F)
                    nc.scalar.copy(k["safe"][:, lo:hi, :], v[:, :, 0:F])
                    last = nc.scalar.copy(k["hr"][:, lo:hi, :], v[:, :, F:2 * F])
                last.then_inc(kept, 1)

            @block.tensor
            def _(pe):
                at_ = steps["dve"]
                pe.wait_ge(loaded, 80)
                for r, (rows, w, name) in enumerate(((mxn, w1, "mxn"), (hid, w3, "hid"))):
                    pe.wait_ge(dsem, at_[name])
                    turn_blocks(pe, nc, k, pt, rows, P, turned)
                    pe.wait_ge(evac, r + 1)
                    for b in range(NBK):
                        last = nc.tensor.matmul(pt[:, b // 4, (b % 4) * P:(b % 4 + 1) * P], cols[:, b * P:(b + 1) * P],
                                                w[:, :], start=True, stop=True)
                    last.then_inc(prod, 1)


def sage_out(nc, d, k):
    with ExitStack() as ctx:
        sb, ps, sem = tools(nc, ctx)
        b3 = sb("so_b3", [P, F])
        t = sb("so_t", [P, NBK, F])
        col = sb("so_col", [P, 3, NBK])
        nr, t1, t2 = (col[:, i, :] for i in range(3))
        loaded, dsem, asem, stored = (sem(f"so_{x}") for x in ("loaded", "dve", "act", "stored"))
        x, agg = k["x"], k["agg"]
        steps = {}
        whole = N // P
        with nc.Block() as block:
            @block.vector
            def _(dve):
                then = Count(dve, dsem)
                steps["dve"] = then.at
                TT = nc.vector.tensor_tensor
                then(TT(agg[:, :, :], agg[:, :, :], spread(k["inv_deg"][:, :]), ALU.mult))
                then(TT(agg[:, :, :], agg[:, :, :], k["hr"][:, :, :], ALU.add))
                dve.wait_ge(loaded, 16)
                then(TT(agg[:, :, :], agg[:, :, :], b3[:, :].unsqueeze(1).to_broadcast([P, NBK, F]), ALU.add))
                then(TT(x[:, :, :], x[:, :, :], agg[:, :, :], ALU.add))
                layernorm_stats(nc, then, x[:, :, :], t, t1, t2, "var")
                dve.wait_ge(asem, 1)
                then(nc.vector.reciprocal(t1, nr))
                then(TT(x[:, :, :], x[:, :, :], spread(t1), ALU.mult), "x")

            @block.scalar
            def _(act):
                finish_norm(nc, act, dsem, steps["dve"], asem, nr, t2)

            @block.sync
            def _(sp):
                sp.dma_start(b3[:, :], d["sb3"].unsqueeze(0).to_broadcast([P, F])).then_inc(loaded, 16)
                sp.wait_ge(dsem, steps["dve"]["x"])
                sp.dma_start(d["out"][0:whole * P, :].rearrange("(b p) f -> p b f", p=P),
                             x[:, 0:whole, :]).then_inc(stored, 16)
                sp.dma_start(d["out"][whole * P:N, :], x[0:N - whole * P, whole, :]).then_inc(stored, 16)
                sp.wait_ge(stored, 32)


def graph_net_kernel(nc, d):
    for name, shape, dt in (("counts", (NP, NP), F32), ("near", (NP, NP), F32), ("turned", (NP, NP), F32),
                            ("starts", (2, EP // 2), BF16), ("w23", (NP, 2 * F), F32), ("dnet", (P, EP // 2), F32),
                            ("rows", (EP, ROW), F32), ("src", (EP,), I32), ("dst", (EP + 1,), I32),
                            ("attr8", (8, EP // 2), F32)):
        d[name] = nc.dram_tensor(name, shape, dt, kind="Internal").ap()
    k = {}
    with ExitStack() as ctx:
        def keep(stack, *what):
            for name, shape, dt in what:
                k[name] = stack.enter_context(nc.sbuf_tensor(name, shape, dt))

        keep(ctx, ("ident", [P, P], F32), ("ones", [P, P], F32), ("upper", [P, P], F32), ("zeros", [P, BANK], F32),
             ("ones16", [P, 2], F16), ("is_pad", [P, NBK], F32), ("half_sel", [2, P], F32), ("blk_first", [P, NBK], F32),
             ("src_idx", [P, NT], I32), ("deg", [P, NBK], F32), ("x", [P, NBK, F], F32), ("cc", [P, 5], F32), ("unsorted", [1, 1], I32),
             ("w1x", [P, NBK, F], F32))
        with ExitStack() as build:
            keep(build, ("iota16", [P, NP], F16), ("iota_blk", [P, P], F16))
            constants(nc, k)
            take_edges(nc, d, k)
            sort_edges(nc, d, k)
            keep(build, ("src_col", [P, NT], F32),
                 ("dst_col", [P, NT], F32), ("src_sh", [P, NT], F32), ("pairs", [1, 4 + len(CUTS), NBK], I32))
            edge_tables(nc, build, d, k)
            counts_and_network(nc, d, k)
        with ExitStack() as dense:
            keep(dense, ("val", [P, NBK, W65], F32), ("toprow", [P, NP], F32), ("sdst", [P, 2, NBK], F32),
                 ("hT", [W66, 2, NP], F32))
            k["sums"] = k["hT"][:, 0, :]
            hyperbolic_nodes(nc, d, k)
            pair_distances(nc, d, k)
            near_sums(nc, d, k)
            end_hyperbolic(nc, d, k)
            attention_rows(nc, d, k)
            score_sums(nc, d, k)
            end_attention(nc, d, k)
        edge_softmax(nc, d, k)
        end_edges(nc, d, k)
        keep(ctx, ("safe", [P, NBK, F], F32), ("inv_deg", [P, NBK], F32), ("agg", [P, NBK, F], F32),
             ("hr", [P, NBK, F], F32))
        sage_values(nc, d, k)
        sum_neighbours(nc, d, k, True, k["safe"], k["agg"])
        sage_hidden(nc, d, k)
        sum_neighbours(nc, d, k, False, k["safe"], k["agg"])
        sage_out(nc, d, k)


_NAMES = {"c": "L0_gnn_c", "W0": "L0_gnn_W", "W1": "L1_gnn_W", "a1": "L1_gnn_a", "Wd1": "L2_gnn_Wd1",
          "bd1": "L2_gnn_bd1", "g1": "L2_gnn_g1", "b1": "L2_gnn_b1", "Wd2": "L2_gnn_Wd2", "bd2": "L2_gnn_bd2",
          "g2": "L2_gnn_g2", "b2": "L2_gnn_b2", "W2_1": "L2_gnn_W1", "W2_2": "L2_gnn_W2", "W2_3": "L2_gnn_W3",
          "W1_l": "L3_gnn_W1_l", "W1_r": "L3_gnn_W1_r", "sb1": "L3_gnn_b1", "W3_l": "L3_gnn_W3_l",
          "W3_r": "L3_gnn_W3_r", "sb3": "L3_gnn_b3"}


def kernel(**inputs):
    import concourse.bacc as _bacc
    from concourse.bass_utils import run_bass_kernel_spmd as _run

    nc = _bacc.Bacc("TRN2", target_bir_lowering=False, num_devices=1)
    src = np.full((EP,), PADN, np.int32)
    src[0:E] = inputs["src"]
    dst = np.full((EP + 1,), PADN, np.int32)
    dst[0] = -1
    dst[1:E + 1] = inputs["dst"]
    x = np.ones((NP, F), np.float32)
    x[0:N] = inputs["x"]
    attr = np.zeros((2, 4, EP // 2), np.float32)
    attr[:, 3] = 1.0
    attr[0, 0:3] = inputs["edge_attr_3"][0:EP // 2].T
    attr[1, 0:3, 0:E - EP // 2] = inputs["edge_attr_3"][EP // 2:E].T
    arrays = {"src_given": src, "dst_given": dst, "x_in": x, "attr_given": attr.reshape(8, EP // 2)}
    for name, given in _NAMES.items():
        arrays[name + "_in"] = np.ascontiguousarray(inputs[given])
    d = {}
    for name, a in arrays.items():
        t = nc.dram_tensor(name, a.shape, mybir.dt.from_np(a.dtype), kind="ExternalInput").ap()
        d[name.removesuffix("_in")] = t
    d["out"] = nc.dram_tensor("out_0_dram", (N, F), F32, kind="ExternalOutput").ap()
    graph_net_kernel(nc, d)
    r = _run(nc, [arrays], core_ids=[0])
    return r.results[0]["out_0_dram"]
```

```python
from contextlib import ExitStack

import concourse.bass as bass
import numpy as np
from concourse import mybir

P = 128
N = 3125
E = 103125
F = 64
NBK = -(-N // P)
NP = NBK * P
PADN = NP - 1
CT = 4
NCH = -(-E // (2 * CT * P))
NT = 2 * CT * NCH
HT = NT // 2
EP = NT * P
NG = -(-NT // P)
NPAIR = NT // 2
BITS = (NPAIR + 1).bit_length()
LEAST = 9
BANK = 512
SPANS = [(k * BANK, min(BANK, NP - k * BANK)) for k in range(-(-NP // BANK))]
SHIFT = NP // 2
BIG = 1e30
ALU = mybir.AluOpType
ACT = mybir.ActivationFunctionType
AX = mybir.AxisListType
F32 = mybir.dt.float32
F16 = mybir.dt.float16
BF16 = mybir.dt.bfloat16
I32 = mybir.dt.int32


def tools(nc, ctx):
    used = []

    def clear():
        for handle in used:
            nc.gpsimd.sem_clear(handle)
    ctx.callback(clear)

    def sb(name, shape, dt=F32):
        return ctx.enter_context(nc.sbuf_tensor(name, shape, dt))

    def ps(name, shape):
        return ctx.enter_context(nc.psum_tensor(name, shape, F32))

    def sem(name, pool_dma=False):
        if pool_dma:
            return nc.alloc_semaphore(name)
        used.append(ctx.enter_context(nc.semaphore(name)))
        return used[-1]
    return sb, ps, sem


def network_weights(nc, d, k, sb, sem):
    wd1 = sb("en_wd1", [4, F])
    wd2 = sb("en_wd2", [F, F])
    bd2 = sb("en_bd2", [1, F])
    mean1 = sb("en_mean1", [4, 1])
    mean2 = sb("en_mean2", [F, 1])
    meanb = sb("en_meanb", [1, 1])
    wl, step, placed = sem("en_wl"), sem("en_step"), sem("en_placed")
    blk1, blk2, avg, pc, eps = (k[name] for name in ("blk1", "blk2", "avg", "pc", "eps"))
    steps = {}

    def load(sp):
        sp.dma_start(wd1[0:3, :], d["Wd1"]).then_inc(wl, 16)
        sp.dma_start(wd1[3:4, :], d["bd1"].unsqueeze(0)).then_inc(wl, 16)
        sp.dma_start(wd2[:, :], d["Wd2"]).then_inc(wl, 16)
        sp.dma_start(bd2[:, :], d["bd2"].unsqueeze(0)).then_inc(wl, 16)
        for h in range(2):
            for i, n in enumerate(("g1", "b1", "g2", "b2")):
                sp.dma_start(pc[h * F:(h + 1) * F, i:i + 1], d[n].unsqueeze(1)).then_inc(wl, 16)

    def centre(dve):
        then = Count(dve, step)
        V, TS = nc.vector, nc.vector.tensor_scalar
        for t, v in ((blk1, 0.0), (blk2, 0.0), (eps, LN_EPS), (avg, 0.0)):
            then(V.memset(t[:, :], v))
        for h in range(2):
            then(V.memset(avg[h * F:(h + 1) * F, h * F:(h + 1) * F], 1 / F))
        dve.wait_ge(wl, 16 * 12)
        for w, m in ((wd1, mean1), (wd2, mean2), (bd2, meanb)):
            then(V.tensor_reduce(m[:, :], w[:, :], AX.X, ALU.add))
            then(TS(m[:, :], m[:, :], 1 / F, None, ALU.mult))
            then(TS(w[:, :], w[:, :], m[:, 0:1], None, ALU.subtract))
        steps["centred"] = then.n

    def place(sp):
        sp.wait_ge(step, steps["centred"])
        for h in range(2):
            sp.dma_start(blk1[4 * h:4 * h + 4, h * F:(h + 1) * F], wd1[:, :]).then_inc(placed, 16)
            sp.dma_start(blk2[h * F:(h + 1) * F, h * F:(h + 1) * F], wd2[:, :]).then_inc(placed, 16)
            sp.dma_start(pc[h * F:(h + 1) * F, 4:5], bd2[:, :]).then_inc(placed, 16)
        sp.wait_ge(placed, 16 * 6)
    return load, centre, place


def edge_tables(nc, d, k):
    with ExitStack() as ctx:
        sb, ps, sem = tools(nc, ctx)

        raw = sb("raw_ends", [P, 2, NG, P], I32)
        rawf = sb("raw_ends_f", [P, 2, NG, P], F32)
        cur = sb("dst_cur", [P, NT], I32)
        prev = sb("dst_prev", [P, NT], I32)
        starts = sb("start_flags", [P, NT], BF16)
        below = sb("below", [P, NT], F32)
        cnt = sb("cnt", [P, NBK + 1], F32)
        tot = sb("tot", [1, NBK + 1], F32)
        toti = sb("toti", [1, NBK + 1], I32)
        lo = sb("lo", [1, NBK], I32)
        hi = sb("hi", [1, NBK], I32)
        lof = sb("lof", [1, NBK], F32)
        nf = sb("nf", [1, NBK], F32)
        zf = sb("zf", [1, NBK], F32)
        incl = sb("incl", [1, NBK], F32)
        tps = ctx.enter_context(nc.psum_tensor("tps", [P, 2, 4, BANK], F32))
        loaded = sem("ends_loaded")
        dl_loaded = sem("dst_loaded")
        stored = sem("starts_stored")
        ready_f = sem("ends_float")
        turned = sem("ends_turned")
        flags = sem("starts_ready")
        cnt_ready = sem("cnt_ready")
        tot_ready = sem("tot_ready")
        step = sem("table_step")
        load_weights, centre_weights, place_weights = network_weights(nc, d, k, sb, sem)
        full = NT // P
        rest = NT - full * P

        with nc.Block() as block:
            @block.tensor
            def _(pe):
                pe.wait_ge(ready_f, 2)
                for i in range(2):
                    for g in range(NG):
                        n = P if g < full else rest
                        last = nc.tensor.transpose(tps[:, i, g // 4, (g % 4) * P:(g % 4) * P + n],
                                                   rawf[0:n, i, g, :], k["ident"][0:n, 0:n])
                    last.then_inc(turned, 1)
                pe.wait_ge(cnt_ready, 1)
                nc.tensor.matmul(tps[0:1, 0, 3, 0:NBK + 1], k["ones"][:, 0:1], cnt[:, :],
                                 start=True, stop=True).then_inc(tot_ready, 1)

            @block.vector
            def _(dve):
                n = [0]

                def then(ins):
                    n[0] += 1
                    ins.then_inc(step, 1)
                    dve.wait_ge(step, n[0])

                dve.wait_ge(loaded, 64)
                for i in range(2):
                    nc.vector.tensor_copy(rawf[:, i, 0:full, :], raw[:, i, 0:full, :])
                    nc.vector.tensor_copy(rawf[0:rest, i, full, :], raw[0:rest, i, full, :]).then_inc(ready_f, 1)
                dve.wait_ge(dl_loaded, 32)
                nc.vector.tensor_tensor(starts[:, :], cur[:, :], prev[:, :], ALU.not_equal).then_inc(flags, 1)
                for i, t in enumerate((k["src_col"], k["dst_col"])):
                    dve.wait_ge(turned, i + 1)
                    for h in range(2):
                        a, b = h * BANK, min(NT, (h + 1) * BANK)
                        then(nc.vector.tensor_copy(t[:, a:b], tps[:, i, h, 0:b - a]))
                then(nc.vector.memset(k["src_idx"][:, NT:NT + 2 * CT], 0))
                then(nc.vector.tensor_copy(k["src_idx"][:, 0:NT], k["src_col"][:, :]))
                for b in range(NBK + 1):
                    then(nc.vector.tensor_scalar(below[:, :], k["dst_col"][:, :], float(b * P), None, ALU.is_lt))
                    then(nc.vector.tensor_reduce(cnt[:, b:b + 1], below[:, :], AX.X, ALU.add))
                nc.vector.memset(zf[:, :], 0.0).then_inc(cnt_ready, 1)
                centre_weights(dve)
                dve.wait_ge(tot_ready, 1)
                then(nc.vector.tensor_copy(tot[:, :], tps[0:1, 0, 3, 0:NBK + 1]))
                then(nc.vector.tensor_copy(toti[:, :], tot[:, :]))
                then(nc.vector.tensor_scalar(lo[:, :], toti[:, 0:NBK], 8, None, ALU.arith_shift_right))
                then(nc.vector.tensor_copy(lof[:, :], lo[:, :]))
                then(nc.vector.tensor_scalar(lof[:, :], lof[:, :], float(NPAIR - LEAST), None, ALU.min))
                then(nc.vector.tensor_scalar(nf[:, :], tot[:, 1:NBK + 1], 255.0, None, ALU.add))
                then(nc.vector.tensor_copy(hi[:, :], nf[:, :]))
                then(nc.vector.tensor_scalar(hi[:, :], hi[:, :], 8, None, ALU.arith_shift_right))
                then(nc.vector.tensor_copy(nf[:, :], hi[:, :]))
                then(nc.vector.scalar_tensor_tensor(out=nf[:, :], in0=lof[:, :], scalar=float(LEAST), in1=nf[:, :],
                                                    op0=ALU.add, op1=ALU.max))
                then(nc.vector.tensor_tensor(nf[:, :], nf[:, :], lof[:, :], ALU.subtract))
                then(nc.vector.tensor_tensor_scan(incl[:, :], nf[:, :], zf[:, :], 0.0, ALU.add, ALU.add))
                then(nc.vector.tensor_tensor(incl[:, :], incl[:, :], nf[:, :], ALU.subtract))
                then(nc.vector.scalar_tensor_tensor(out=incl[:, :], in0=incl[:, :], scalar=2.0, in1=lof[:, :],
                                                    op0=ALU.mult, op1=ALU.subtract))
                then(nc.vector.tensor_scalar(nf[:, :], nf[:, :], -1.0, None, ALU.add))
                V = nc.vector
                then(V.tensor_copy(k["pairs"][:, :], lof[:, :]))
                for value, shift in ((nf, BITS), (incl, 2 * BITS)):
                    then(V.tensor_copy(lo[:, :], value[:, :]))
                    then(V.tensor_scalar(lo[:, :], lo[:, :], shift, None, ALU.logical_shift_left))
                    then(V.tensor_tensor(k["pairs"][:, :], k["pairs"][:, :], lo[:, :], ALU.bitwise_or))
                then(nc.vector.tensor_scalar(k["src_sh"][:, :], k["src_col"][:, :], -float(SHIFT), None, ALU.add))

            @block.sync
            def _(sp):
                for i, t in enumerate((d["src"], d["dst"])):
                    v = t[1:EP + 1] if i else t[0:EP]
                    sp.dma_start(raw[:, i, 0:full, :],
                                 v[0:full * P * P].rearrange("(g p e) -> p g e", p=P, e=P)).then_inc(loaded, 16)
                    sp.dma_start(raw[0:rest, i, full, :],
                                 v[full * P * P:EP].rearrange("(p e) -> p e", e=P)).then_inc(loaded, 16)
                sp.dma_start(prev[:, :], d["dst"][0:EP].rearrange("(p e) -> p e", e=NT)).then_inc(dl_loaded, 16)
                sp.dma_start(cur[:, :], d["dst"][1:EP + 1].rearrange("(p e) -> p e", e=NT)).then_inc(dl_loaded, 16)
                load_weights(sp)
                sp.wait_ge(flags, 1)
                sp.dma_start(d["starts"].rearrange("h (p e) -> (h p) e", e=NT), starts[:, :]).then_inc(stored, 16)
                place_weights(sp)
                sp.wait_ge(stored, 16)


def constants(nc, k):
    with ExitStack() as ctx:
        _, _, sem = tools(nc, ctx)
        made, io_made = sem("consts_made"), sem("iota_made")
        ioi = ctx.enter_context(nc.sbuf_tensor("iota_i", [P, NP], I32))
        iop = ctx.enter_context(nc.sbuf_tensor("iota_p", [P, P], I32))
        iob = ctx.enter_context(nc.sbuf_tensor("iota_b", [P, NBK], I32))
        with nc.Block() as block:
            @block.gpsimd
            def _(pool):
                G = nc.gpsimd
                G.iota(ioi[:, :], pattern=[[1, NP]], base=-SHIFT, channel_multiplier=0).then_inc(io_made, 1)
                G.iota(iop[:, :], pattern=[[1, P]], base=0, channel_multiplier=0).then_inc(io_made, 1)
                G.iota(iob[:, :], pattern=[[P, NBK]], base=0, channel_multiplier=0).then_inc(io_made, 1)
                for name, v in (("ones", 1.0), ("ident", 0.0), ("upper", 1.0), ("is_pad", 0.0), ("half_sel", -BIG),
                                ("zeros", 0.0)):
                    G.memset(k[name][:, :], v).then_inc(made, 1)
                G.memset(k["ones16"][:, :], 1.0).then_inc(made, 1)
                pool.wait_ge(made, 7)

                def where(name, op, fill, base, pattern, mult):
                    return G.affine_select(out=k[name][:, :], in_=k[name][:, :], compare_op=op, fill=fill, base=base,
                                           pattern=pattern, channel_multiplier=mult)
                where("ident", ALU.not_equal, 1.0, 0, [[-1, P]], 1)
                where("upper", ALU.is_ge, 0.0, 0, [[1, P]], -1)
                where("is_pad", ALU.is_ge, 1.0, N - 1, [[-P, NBK]], -1)
                where("half_sel", ALU.is_ge, 0.0, 0, [[1, P]], -F).then_inc(made, 1)
                pool.wait_ge(made, 8)
                where("half_sel", ALU.is_ge, 0.0, F - 1, [[-1, P]], F)

            @block.vector
            def _(dve):
                dve.wait_ge(io_made, 3)
                nc.vector.tensor_copy(k["iota16"][:, :], ioi[:, :])
                nc.vector.tensor_copy(k["iota_blk"][:, :], iop[:, :])
                nc.vector.tensor_copy(k["blk_first"][:, :], iob[:, :])


EPS = 1e-15
CLIP = 0.98
LN_EPS = 1e-5
M_MIN = 1e-16
SELF_NEAR = float(np.arcsinh(np.sqrt(M_MIN)))
M_MAX = CLIP * CLIP / (1 - CLIP * CLIP)
HALF_OFF = 2.5
W65 = F + 1
W66 = F + 2


class Count:

    def __init__(self, eng, sem):
        self.eng, self.sem, self.n, self.at = eng, sem, 0, {}

    def __call__(self, ins, name=None):
        self.mark(ins, name)
        self.eng.wait_ge(self.sem, self.n)

    def mark(self, ins, name=None):
        self.n += 1
        ins.then_inc(self.sem, 1)
        if name:
            self.at[name] = self.n


def over_blocks(eng, body):
    with eng.Fori(0, NBK // 2) as h:
        body(h, 0)
        body(h, 1)
    body(NBK // 2, 0)


def spread(col, w=F):
    return col.unsqueeze(2).to_broadcast([P, NBK, w])


def turn_blocks(pe, nc, k, psum, nodes, width, last_sem):
    for b in range(NBK):
        last = nc.tensor.transpose(psum[0:width, b // 4, (b % 4) * P:(b % 4 + 1) * P], nodes[:, b, 0:width],
                                   k["ident"][:, :])
    last.then_inc(last_sem, 1)


def back_blocks(pe, nc, k, psum, cols, width, last_sem):
    for b in range(NBK):
        last = nc.tensor.transpose(psum[:, b // 7, (b % 7) * width:(b % 7 + 1) * width],
                                   cols[0:width, b * P:(b + 1) * P], k["ident"][0:width, 0:width])
    last.then_inc(last_sem, 1)


def norm_sq(nc, then, out, v, sq, name=None):
    then(nc.vector.tensor_tensor(sq[:, :, :], v, v, ALU.mult))
    then(nc.vector.tensor_reduce(out, sq[:, :, :], AX.X, ALU.add), name)


def limit_norm(nc, then, v, nrm, t, lim, c2=None):
    then(nc.vector.tensor_scalar(t, nrm, lim, None, ALU.max))
    then(nc.vector.reciprocal(t, t))
    then(nc.vector.tensor_scalar(t, t, lim, None, ALU.mult))
    then(nc.vector.tensor_tensor(v, v, spread(t), ALU.mult))


def artanh_small(nc, then, out, y, t1, t2):
    then(nc.vector.tensor_tensor(t1, y, y, ALU.mult))
    then(nc.vector.tensor_scalar(t2, t1, 1 / 7, 1 / 5, ALU.mult, ALU.add))
    then(nc.vector.tensor_tensor(t2, t2, t1, ALU.mult))
    then(nc.vector.tensor_scalar(t2, t2, 1 / 3, None, ALU.add))
    then(nc.vector.tensor_tensor(t2, t2, t1, ALU.mult))
    then(nc.vector.tensor_scalar(t2, t2, 1.0, None, ALU.add))
    then(nc.vector.tensor_tensor(out, t2, y, ALU.mult))


def artanh_pick(nc, then, out, y, lnp, lnm, small, t1):
    then(nc.vector.tensor_tensor(out, lnp, lnm, ALU.subtract))
    then(nc.vector.scalar_tensor_tensor(out=out, in0=out, scalar=0.5, in1=small, op0=ALU.mult, op1=ALU.subtract))
    then(nc.vector.tensor_scalar(t1, y, 0.15, None, ALU.is_ge))
    then(nc.vector.tensor_tensor(out, out, t1, ALU.mult))
    then(nc.vector.tensor_tensor(out, out, small, ALU.add))


def layernorm_stats(nc, then, v, sq, m, var, name):
    then(nc.vector.tensor_reduce(m, v, AX.X, ALU.add))
    then(nc.vector.tensor_scalar(m, m, 1 / F, None, ALU.mult))
    then(nc.vector.tensor_tensor(v, v, spread(m), ALU.subtract))
    then(nc.vector.tensor_tensor(sq[:, :, :], v, v, ALU.mult))
    then(nc.vector.tensor_reduce(var, sq[:, :, :], AX.X, ALU.add))
    then(nc.vector.tensor_scalar(var, var, 1 / F, LN_EPS, ALU.mult, ALU.add), name)


def hyperbolic_nodes(nc, d, k):
    with ExitStack() as ctx:
        sb, ps, sem = tools(nc, ctx)
        v = sb("n_v", [P, NBK, F])
        u = sb("n_u", [P, NBK, F])
        sq = sb("n_sq", [P, NBK, F])
        aug = sb("n_aug", [P, 2, NBK, W66])
        vt = sb("n_vt", [F, NP])
        W = sb("n_W", [F, F])
        col = sb("n_col", [P, 12, NBK])
        ss, nr, t1, t2, th, pn, at, small, lnp, lnm, y, nu = (col[:, i, :] for i in range(12))
        pt = ps("n_pt", [P, 7, BANK])
        loaded, dsem, asem, amid = sem("l0_loaded"), sem("l0_dve"), sem("l0_act"), sem("l0_act_mid")
        turned, evac, prod, aug_turned, aug_evac = (sem(f"l0_{x}") for x in
                                                    ("turned", "evac", "prod", "aug_turned", "aug_evac"))
        x, cc = k["x"], k["cc"]
        c1, rc, irc, c2lim = (cc[:, i:i + 1] for i in range(4))
        with nc.Block() as block:
            @block.sync
            def _(sp):
                sp.dma_start(x[:, :, :], d["x"].rearrange("(b p) f -> p b f", p=P)).then_inc(loaded, 16)
                sp.dma_start(c1, d["c"].unsqueeze(0).to_broadcast([P, 1])).then_inc(loaded, 16)
                sp.dma_start(W[:, :], d["W0"]).then_inc(loaded, 16)

            steps = {}

            @block.vector
            def _(dve):
                then = Count(dve, dsem)
                steps["dve"] = then.at
                a = [0]

                def answered():
                    a[0] += 1
                    dve.wait_ge(asem, a[0])

                dve.wait_ge(loaded, 48)
                then(nc.vector.tensor_scalar(v[:, :, :], x[:, :, :], EPS, None, ALU.add), "c")
                norm_sq(nc, then, ss, v[:, :, :], sq, "f_sq")
                answered()
                answered()
                then(nc.vector.reciprocal(irc, rc))
                then(nc.vector.tensor_scalar(c2lim, irc, CLIP, None, ALU.mult))
                then(nc.vector.tensor_scalar(cc[:, 4:5], irc, -2.0, None, ALU.mult))
                limit_norm(nc, then, v[:, :, :], nr, t1, CLIP)
                norm_sq(nc, then, ss, v[:, :, :], sq, "fn_sq")
                answered()
                then(nc.vector.reciprocal(t1, nr))
                then(nc.vector.tensor_tensor(t1, t1, th, ALU.mult))
                then(nc.vector.tensor_tensor(v[:, :, :], v[:, :, :], spread(t1), ALU.mult))
                then(nc.vector.tensor_scalar(v[:, :, :], v[:, :, :], EPS, None, ALU.add))
                norm_sq(nc, then, ss, v[:, :, :], sq, "p_sq")
                answered()
                limit_norm(nc, then, v[:, :, :], nr, t1, CLIP)
                norm_sq(nc, then, ss, v[:, :, :], sq, "pn_sq")
                answered()
                then(nc.vector.tensor_copy(pn, nr))
                then(nc.vector.tensor_scalar(y, pn, rc, None, ALU.mult))
                then(nc.vector.tensor_scalar(y, y, 0.9, -0.9, ALU.min, ALU.max), "y1")
                artanh_small(nc, then, small, y, t1, t2)
                answered()
                artanh_pick(nc, then, at, y, lnp, lnm, small, t1)
                then(nc.vector.reciprocal(t1, pn))
                then(nc.vector.tensor_tensor(t1, t1, at, ALU.mult))
                then(nc.vector.tensor_scalar(t1, t1, irc, None, ALU.mult))
                dve.wait_ge(prod, 1)
                for g in range(4):
                    lo, hi = 8 * g, min(NBK, 8 * g + 8)
                    then(nc.vector.tensor_tensor(
                        u[:, lo:hi, :], pt[:, g, 0:(hi - lo) * F].rearrange("p (b f) -> p b f", f=F),
                        t1[:, lo:hi].unsqueeze(2).to_broadcast([P, hi - lo, F]), ALU.mult))
                norm_sq(nc, then, ss, u[:, :, :], sq, "t_sq")
                answered()
                limit_norm(nc, then, u[:, :, :], nr, t1, c2lim)
                norm_sq(nc, then, ss, u[:, :, :], sq, "tn_sq")
                answered()
                then(nc.vector.reciprocal(t1, nr))
                then(nc.vector.tensor_tensor(t1, t1, th, ALU.mult))
                then(nc.vector.tensor_scalar(t1, t1, irc, None, ALU.mult))
                then(nc.vector.tensor_tensor(u[:, :, :], u[:, :, :], spread(t1), ALU.mult))
                norm_sq(nc, then, nu, u[:, :, :], sq)
                then(nc.vector.tensor_scalar(t1, nu, c1, -1.0, ALU.mult, ALU.mult))
                then(nc.vector.tensor_scalar(t1, t1, 1.0, None, ALU.add))
                then(nc.vector.reciprocal(aug[:, 0, :, F + 1], t1))
                s_ = aug[:, 0, :, F + 1]
                then(nc.vector.tensor_tensor(aug[:, 0, :, F], nu, s_, ALU.mult))
                then(nc.vector.tensor_tensor(aug[:, 0, :, 0:F], u[:, :, :], spread(s_), ALU.mult))
                then(nc.vector.tensor_scalar(aug[:, 1, :, 0:F], aug[:, 0, :, 0:F], c1, -2.0, ALU.mult, ALU.mult))
                then(nc.vector.tensor_scalar(aug[:, 1, :, F], s_, c1, None, ALU.mult))
                then(nc.vector.tensor_scalar(aug[:, 1, :, F + 1], aug[:, 0, :, F], c1, None, ALU.mult), "aug")
                then(nc.vector.tensor_scalar(v[:, :, :], u[:, :, :], EPS, None, ALU.add))
                norm_sq(nc, then, ss, v[:, :, :], sq, "g_sq")
                answered()
                limit_norm(nc, then, v[:, :, :], nr, t1, CLIP)
                norm_sq(nc, then, ss, v[:, :, :], sq, "gn_sq")
                answered()
                then(nc.vector.tensor_copy(pn, nr))
                then(nc.vector.tensor_scalar(y, pn, rc, None, ALU.mult))
                then(nc.vector.tensor_scalar(y, y, 0.9, -0.9, ALU.min, ALU.max), "y2")
                artanh_small(nc, then, small, y, t1, t2)
                answered()
                artanh_pick(nc, then, at, y, lnp, lnm, small, t1)
                then(nc.vector.reciprocal(t1, pn))
                then(nc.vector.tensor_tensor(t1, t1, at, ALU.mult))
                then(nc.vector.tensor_scalar(t1, t1, rc, None, ALU.mult))
                then(nc.vector.tensor_tensor(k["val"][:, :, 0:F], v[:, :, :], spread(t1), ALU.mult))
                then(nc.vector.memset(k["val"][:, :, F], 1.0))

            @block.scalar
            def _(act):
                at_ = steps["dve"]

                def root():
                    nc.scalar.sqrt(nr, ss).then_inc(asem, 1)

                act.wait_ge(loaded, 48)
                nc.scalar.sqrt(rc, c1).then_inc(asem, 1)
                act.wait_ge(dsem, at_["f_sq"])
                root()
                act.wait_ge(dsem, at_["fn_sq"])
                nc.scalar.sqrt(nr, ss).then_inc(amid, 1)
                act.wait_ge(amid, 1)
                nc.scalar.activation(th, nr, ACT.Tanh).then_inc(asem, 1)
                for name in ("p_sq", "pn_sq"):
                    act.wait_ge(dsem, at_[name])
                    root()
                act.wait_ge(dsem, at_["y1"])
                nc.scalar.activation(lnp, y, ACT.Ln, bias=1.0)
                nc.scalar.activation(lnm, y, ACT.Ln, scale=-1.0, bias=1.0).then_inc(asem, 1)
                act.wait_ge(turned, 1)
                for i, (a, w) in enumerate(SPANS):
                    last = nc.scalar.copy(vt[:, a:a + w], pt[0:F, i, 0:w])
                last.then_inc(evac, 1)
                act.wait_ge(dsem, at_["t_sq"])
                root()
                act.wait_ge(dsem, at_["tn_sq"])
                nc.scalar.sqrt(nr, ss).then_inc(amid, 1)
                act.wait_ge(amid, 2)
                nc.scalar.activation(th, nr, ACT.Tanh, scale=rc).then_inc(asem, 1)
                for name in ("g_sq", "gn_sq"):
                    act.wait_ge(dsem, at_[name])
                    root()
                act.wait_ge(dsem, at_["y2"])
                nc.scalar.activation(lnp, y, ACT.Ln, bias=1.0)
                nc.scalar.activation(lnm, y, ACT.Ln, scale=-1.0, bias=1.0).then_inc(asem, 1)
                for j in range(2):
                    act.wait_ge(aug_turned, j + 1)
                    for i, (a, w) in enumerate(SPANS):
                        last = nc.scalar.copy(k["hT"][0:W66, j, a:a + w], pt[0:W66, i, 0:w])
                    last.then_inc(aug_evac, 1)

            @block.tensor
            def _(pe):
                at_ = steps["dve"]
                pe.wait_ge(dsem, at_["y1"])
                turn_blocks(pe, nc, k, pt, v, F, turned)
                pe.wait_ge(evac, 1)
                for b in range(NBK):
                    last = nc.tensor.matmul(pt[:, b // 8, (b % 8) * F:(b % 8 + 1) * F], vt[:, b * P:(b + 1) * P],
                                            W[:, :], start=True, stop=True)
                last.then_inc(prod, 1)
                for j in range(2):
                    pe.wait_ge(dsem, at_["aug"])
                    if j:
                        pe.wait_ge(aug_evac, j)
                    turn_blocks(pe, nc, k, pt, aug[:, j], W66, aug_turned)


PARTS = ((0, 3), (3, len(SPANS)))


def columns(part):
    lo, hi = PARTS[part]
    return slice(SPANS[lo][0], SPANS[hi - 1][0] + SPANS[hi - 1][1])


def pair_distances(nc, d, k):
    with ExitStack() as ctx:
        sb, ps, sem = tools(nc, ctx)
        m = sb("pd_m", [P, 2, NP])
        root1 = sb("pd_root1", [P, 2, NP])
        cnt = sb("pd_cnt", [P, 2, NP])
        out = sb("pd_out", [P, 2, NP])
        top = sb("pd_top", [P, NP])
        lhs = sb("pd_lhs", [W66, 2, P])
        dg = sb("pd_dg", [P, 2, P])
        topc = sb("pd_topc", [P, NBK])
        off = sb("pd_off", [P, P])
        self_near = sb("pd_self_near", [P, P])
        dcnt = sb("pd_dcnt", [P, P])
        dn = ps("pd_dn", [P, 7, BANK])
        tp = dn[:, 2:4, :]
        not_diag, diag_fixed = sem("pd_not_diag"), sem("pd_diag_fixed")
        root, added, logs, masked_, lowered = (
            [sem(f"pd_{x}{c}") for c in range(2)] for x in ("root", "added", "logs", "masked", "lowered"))
        lhs_ready, loaded, stored, fixed = (
            [sem(f"pd_{x}{s}") for s in range(2)] for x in ("lhs_ready", "loaded", "stored", "fixed"))
        prods, used = sem("pd_prods"), sem("pd_used")
        top_zero, top_turned, top_taken, diag, row, row_out = (
            sem(f"pd_{x}") for x in ("top_zero", "top_turned", "top_taken", "diag", "row", "row_out"))
        NS = len(SPANS)
        NSLOT = NS
        with nc.Block() as block:
            @block.sync
            def _(sp):
                def load(h, s):
                    sp.wait_ge(fixed[s], h)
                    sp.dma_start(cnt[:, s, :], d["counts"][bass.ds((2 * h + s) * P, P), :]).then_inc(loaded[s], 16)

                def store(h, s):
                    sp.wait_ge(fixed[s], h + 1)
                    sp.dma_start(d["near"][bass.ds((2 * h + s) * P, P), :], out[:, s, :]).then_inc(stored[s], 16)

                load(0, 0)
                with sp.Fori(0, NBK // 2) as h:
                    load(h, 1)
                    store(h, 0)
                    load(h + 1, 0)
                    store(h, 1)
                store(NBK // 2, 0)
                sp.wait_ge(stored[0], 16 * (NBK // 2 + 1))
                sp.wait_ge(stored[1], 16 * (NBK // 2))

            @block.gpsimd
            def _(pool):
                def left(h, s):
                    pool.wait_ge(prods, 2 * NS * h)
                    nc.gpsimd.tensor_copy(lhs[:, s, :], k["hT"][0:W66, 1, bass.ds((2 * h + s) * P, P)])\
                      .then_inc(lhs_ready[s], 1)

                def sums(h, s):
                    for c in range(2):
                        cs = columns(c)
                        pool.wait_ge(root[c], 2 * (2 * h + s) + 2)
                        nc.gpsimd.tensor_tensor(m[:, s, cs], m[:, s, cs], root1[:, s, cs], ALU.add)\
                          .then_inc(added[c], 1)
                left(0, 0)
                with pool.Fori(0, NBK // 2) as h:
                    left(h, 1)
                    sums(h, 0)
                    left(h + 1, 0)
                    sums(h, 1)
                sums(NBK // 2, 0)

            @block.tensor
            def _(pe):
                pe.wait_ge(top_zero, 1)

                def body(h, s):
                    pe.wait_ge(lhs_ready[s], h + 1)
                    for i, (a, w) in enumerate(SPANS):
                        pe.wait_ge(used, NS * (2 * h + s) + i + 1)
                        nc.tensor.matmul(dn[:, i, 0:w],
                                         lhs[:, s, :], k["hT"][0:W66, 0, a:a + w],
                                         start=True, stop=True).then_inc(prods, 1)
                over_blocks(pe, body)
                for c in range(2):
                    pe.wait_ge(lowered[c], NBK)
                for b in range(NBK):
                    if b >= 2:
                        pe.wait_ge(top_taken, b - 1)
                    nc.tensor.transpose(tp[:, b % 2, 0:P], top[:, b * P:(b + 1) * P],
                                        k["ident"][:, :]).then_inc(top_turned, 1)
                for b in range(NBK):
                    pe.wait_ge(diag, b + 1)
                    if b >= 2:
                        pe.wait_ge(row_out, b - 1)
                    nc.tensor.matmul(dn[:, b % 2, 0:P], k["ones"][:, :], dg[:, b % 2, :],
                                     start=True, stop=True).then_inc(row, 1)

            @block.scalar
            def _(act):
                def roots(h, s):
                    b = 2 * h + s
                    for c in range(2):
                        cs = columns(c)
                        act.wait_ge(used, NS * b + PARTS[c][1] + NSLOT)
                        nc.scalar.activation(root1[:, s, cs], m[:, s, cs], ACT.Sqrt, bias=1.0).then_inc(root[c], 1)
                        act.wait_ge(root[c], 2 * b + 1)
                        nc.scalar.sqrt(m[:, s, cs], m[:, s, cs]).then_inc(root[c], 1)

                def logarithms(h, s):
                    b = 2 * h + s
                    for c in range(2):
                        cs = columns(c)
                        act.wait_ge(added[c], b + 1)
                        nc.scalar.activation(m[:, s, cs], m[:, s, cs], ACT.Ln,
                                             scale=float(np.exp(-HALF_OFF))).then_inc(logs[c], 1)
                roots(0, 0)
                with act.Fori(0, NBK // 2) as h:
                    roots(h, 1)
                    logarithms(h, 0)
                    roots(h + 1, 0)
                    logarithms(h, 1)
                logarithms(NBK // 2, 0)
                for b in range(NBK):
                    act.wait_ge(row, b + 1)
                    nc.scalar.copy(k["toprow"][:, b * P:(b + 1) * P], dn[:, b % 2, 0:P]).then_inc(row_out, 1)

            @block.vector
            def _(dve):
                def clipped(h, s, c):
                    b = 2 * h + s
                    for i in range(*PARTS[c]):
                        a, w = SPANS[i]
                        dve.wait_ge(prods, NS * b + i + 1)
                        nc.vector.tensor_scalar(m[:, s, a:a + w], dn[:, i, 0:w], M_MIN, M_MAX,
                                                ALU.max, ALU.min).then_inc(used, 1)

                def masked(h, s, c):
                    b = 2 * h + s
                    cs = columns(c)
                    dve.wait_ge(logs[c], b + 1)
                    dve.wait_ge(stored[s], 16 * h)
                    dve.wait_ge(loaded[s], 16 * h + 16)
                    nc.vector.scalar_tensor_tensor(out=out[:, s, cs], in0=cnt[:, s, cs], scalar=1.0, in1=m[:, s, cs],
                                                   op0=ALU.min, op1=ALU.mult).then_inc(masked_[c], 1)

                def own(h, s):
                    b = 2 * h + s
                    here = bass.ds(b * P, P)
                    for c in range(2):
                        dve.wait_ge(masked_[c], b + 1)
                    V = nc.vector
                    V.scalar_tensor_tensor(out=dcnt[:, :], in0=cnt[:, s, here], scalar=1.0, in1=self_near[:, :],
                                           op0=ALU.min, op1=ALU.mult).then_inc(diag_fixed, 1)
                    V.tensor_tensor(out[:, s, here], out[:, s, here], off[:, :], ALU.mult).then_inc(diag_fixed, 1)
                    dve.wait_ge(diag_fixed, 2 * b + 2)
                    V.tensor_tensor(out[:, s, here], out[:, s, here], dcnt[:, :], ALU.add).then_inc(fixed[s], 1)

                def lower(h, s):
                    dve.wait_ge(fixed[s], h + 1)
                    for c in range(2):
                        cs = columns(c)
                        nc.vector.tensor_tensor(top[:, cs], top[:, cs], out[:, s, cs], ALU.min).then_inc(lowered[c], 1)
                    for c in range(2):
                        dve.wait_ge(lowered[c], 2 * h + s + 1)

                nc.vector.tensor_scalar(off[:, :], k["ident"][:, :], -1.0, 1.0, ALU.mult, ALU.add).then_inc(not_diag, 1)
                nc.vector.tensor_scalar(self_near[:, :], k["ident"][:, :], SELF_NEAR - HALF_OFF, None,
                                        ALU.mult).then_inc(not_diag, 1)
                nc.vector.memset(topc[:, 0:1], 0.0).then_inc(used, NSLOT)
                nc.vector.memset(top[:, :], 0.0).then_inc(top_zero, 1)
                dve.wait_ge(top_zero, 1)
                dve.wait_ge(not_diag, 2)
                for s in range(2):
                    for c in range(2):
                        clipped(0, s, c)

                def step(h, s, more):
                    for c in range(2):
                        masked(h, s, c)
                        if more:
                            dve.wait_ge(masked_[c], 2 * h + s + 1)
                            clipped(h + 1, s, c)
                    own(h, s)
                    lower(h, s)
                with dve.Fori(0, NBK // 2 - 1) as h:
                    step(h, 0, True)
                    step(h, 1, True)
                step(NBK // 2 - 1, 0, True)
                step(NBK // 2 - 1, 1, False)
                step(NBK // 2, 0, False)
                for b in range(NBK):
                    dve.wait_ge(top_turned, b + 1)
                    nc.vector.tensor_reduce(topc[:, b:b + 1], tp[:, b % 2, 0:P], AX.X, ALU.min).then_inc(top_taken, 1)
                for b in range(NBK):
                    dve.wait_ge(top_taken, b + 1)
                    if b >= 2:
                        dve.wait_ge(row, b - 1)
                    nc.vector.tensor_scalar(dg[:, b % 2, :], k["ident"][:, :], topc[:, b:b + 1], None,
                                            ALU.mult).then_inc(diag, 1)


def zero_sums(nc, k, acc, rows):
    for i, (a, w) in enumerate(SPANS):
        last = nc.tensor.matmul(acc[0:rows, i, 0:w], k["zeros"][:, 0:rows], k["zeros"][:, 0:w],
                                start=True, stop=False, skip_group_check=True)
    return last


def near_sums(nc, d, k):
    with ExitStack() as ctx:
        sb, ps, sem = tools(nc, ctx)
        near = sb("ns_near", [P, 2, NP])
        cnt = sb("ns_cnt", [P, 2, NP])
        z = sb("ns_z", [P, 2, NP])
        w_ = sb("ns_w", [P, 2, NP])
        val = sb("ns_val", [P, 2, W65])
        acc = ps("ns_acc", [P, 7, BANK])
        near_loaded, cnt_loaded, zed, exped, val_ready, summed = (
            [sem(f"ns_{x}{s}") for s in range(2)]
            for x in ("near_loaded", "cnt_loaded", "zed", "exped", "val_ready", "summed"))
        weighed = [[sem(f"ns_weighed{s}_{c}") for c in range(2)] for s in range(2)]
        done = sem("ns_done")
        with nc.Block() as block:
            @block.sync
            def _(sp):
                def load(h, s):
                    rows = bass.ds((2 * h + s) * P, P)
                    sp.wait_ge(zed[s], 2 * h)
                    sp.dma_start(near[:, s, :], d["near"][rows, :]).then_inc(near_loaded[s], 16)
                    for c in range(2):
                        sp.wait_ge(weighed[s][c], h)
                    sp.dma_start(cnt[:, s, :], d["counts"][rows, :]).then_inc(cnt_loaded[s], 16)
                over_blocks(sp, load)

            @block.gpsimd
            def _(pool):
                def body(h, s):
                    pool.wait_ge(summed[s], 2 * h)
                    nc.gpsimd.tensor_copy(val[:, s, :].unsqueeze(1), k["val"][:, bass.ds(2 * h + s, 1), 0:W65])\
                      .then_inc(val_ready[s], 1)
                over_blocks(pool, body)

            @block.vector
            def _(dve):
                def less_top(h, s, c):
                    cs = columns(c)
                    dve.wait_ge(near_loaded[s], 16 * h + 16)
                    dve.wait_ge(weighed[s][c], h)
                    nc.vector.tensor_tensor(z[:, s, cs], near[:, s, cs], k["toprow"][:, cs],
                                            ALU.subtract).then_inc(zed[s], 1)

                def weigh(h, s, c):
                    cs = columns(c)
                    dve.wait_ge(cnt_loaded[s], 16 * h + 16)
                    dve.wait_ge(exped[s], 2 * h + c + 1)
                    dve.wait_ge(summed[s], 2 * h)
                    nc.vector.tensor_tensor(w_[:, s, cs], z[:, s, cs], cnt[:, s, cs],
                                            ALU.mult).then_inc(weighed[s][c], 1)

                for c in range(2):
                    less_top(0, 0, c)
                with dve.Fori(0, NBK // 2) as h:
                    for s in range(2):
                        for c in range(2):
                            less_top(h + s, 1 - s, c)
                            weigh(h, s, c)
                for c in range(2):
                    weigh(NBK // 2, 0, c)

            @block.scalar
            def _(act):
                def body(h, s):
                    for c in range(2):
                        cs = columns(c)
                        act.wait_ge(zed[s], 2 * h + c + 1)
                        nc.scalar.activation(z[:, s, cs], z[:, s, cs], ACT.Exp, scale=k["cc"][:, 4:5]).then_inc(exped[s], 1)
                over_blocks(act, body)
                act.wait_ge(done, 1)
                for i, (a, w) in enumerate(SPANS):
                    nc.scalar.copy(k["sums"][0:W65, a:a + w], acc[0:W65, i, 0:w])

            @block.tensor
            def _(pe):
                zero_sums(nc, k, acc, W65)
                over_blocks(pe, lambda h, s: add_weighed(nc, pe, h, s, acc, val, w_, weighed, val_ready, summed))
                nc.tensor.matmul(acc[0:1, 6, BANK - 1:BANK], k["zeros"][:, 0:1], k["zeros"][:, 0:1],
                                 start=False, stop=True, skip_group_check=True).then_inc(done, 1)


def add_weighed(nc, pe, h, s, acc, val, w_, weighed, val_ready, summed):
    pe.wait_ge(val_ready[s], h + 1)
    for c, (lo, hi) in enumerate(PARTS):
        pe.wait_ge(weighed[s][c], h + 1)
        for i in range(lo, hi):
            a, w = SPANS[i]
            last = nc.tensor.matmul(acc[0:W65, i, 0:w], val[:, s, :], w_[:, s, a:a + w],
                                    start=False, stop=False, skip_group_check=True)
        last.then_inc(summed[s], 1)


def elu(nc, then, act_exp, v, t):
    then(nc.vector.tensor_scalar(t, v, 0.0, None, ALU.min), "elu")
    act_exp()
    then(nc.vector.tensor_scalar(v, v, 0.0, -1.0, ALU.max, ALU.add))
    then(nc.vector.tensor_tensor(v, v, t, ALU.add))


def end_hyperbolic(nc, d, k):
    with ExitStack() as ctx:
        sb, ps, sem = tools(nc, ctx)
        v = sb("eh_v", [P, NBK, F])
        t = sb("eh_t", [P, NBK, F])
        col = sb("eh_col", [P, 6, NBK])
        den, ss, nr, t1, th, t2 = (col[:, i, :] for i in range(6))
        pb = ps("eh_pb", [P, 4, BANK])
        back, dsem, asem, amid = sem("eh_back"), sem("eh_dve"), sem("eh_act"), sem("eh_act_mid")
        x = k["x"]
        rc, irc, c2lim = (k["cc"][:, i:i + 1] for i in (1, 2, 3))
        steps = {}
        with nc.Block() as block:
            @block.tensor
            def _(pe):
                back_blocks(pe, nc, k, pb, k["sums"], W65, back)

            @block.vector
            def _(dve):
                then = Count(dve, dsem)
                steps["dve"] = then.at
                a = [0]

                def answered():
                    a[0] += 1
                    dve.wait_ge(asem, a[0])

                dve.wait_ge(back, 1)
                for g in range(4):
                    lo, hi = 7 * g, min(NBK, 7 * g + 7)
                    rows = pb[:, g, 0:(hi - lo) * W65].rearrange("p (b f) -> p b f", f=W65)
                    then(nc.vector.tensor_scalar(den[:, lo:hi], rows[:, :, F], 1e-16, None, ALU.add))
                    then(nc.vector.reciprocal(den[:, lo:hi], den[:, lo:hi]))
                    then(nc.vector.tensor_tensor(v[:, lo:hi, :], rows[:, :, 0:F],
                                                 den[:, lo:hi].unsqueeze(2).to_broadcast([P, hi - lo, F]), ALU.mult))
                elu(nc, then, answered, v[:, :, :], t[:, :, :])
                then(nc.vector.tensor_scalar(v[:, :, :], v[:, :, :], EPS, None, ALU.add))
                norm_sq(nc, then, ss, v[:, :, :], t, "z_sq")
                answered()
                limit_norm(nc, then, v[:, :, :], nr, t1, c2lim)
                norm_sq(nc, then, ss, v[:, :, :], t, "zn_sq")
                answered()
                then(nc.vector.reciprocal(t1, nr))
                then(nc.vector.tensor_tensor(t1, t1, th, ALU.mult))
                then(nc.vector.tensor_scalar(t1, t1, irc, None, ALU.mult))
                then(nc.vector.tensor_tensor(v[:, :, :], v[:, :, :], spread(t1), ALU.mult))
                then(nc.vector.tensor_tensor(x[:, :, :], x[:, :, :], v[:, :, :], ALU.add))
                layernorm_stats(nc, then, x[:, :, :], t, t1, t2, "var")
                answered()
                then(nc.vector.reciprocal(t1, nr))
                then(nc.vector.tensor_tensor(x[:, :, :], x[:, :, :], spread(t1), ALU.mult))

            @block.scalar
            def _(act):
                at_ = steps["dve"]
                act.wait_ge(dsem, at_["elu"])
                nc.scalar.activation(t[:, :, :], t[:, :, :], ACT.Exp).then_inc(asem, 1)
                act.wait_ge(dsem, at_["z_sq"])
                nc.scalar.sqrt(nr, ss).then_inc(asem, 1)
                act.wait_ge(dsem, at_["zn_sq"])
                nc.scalar.sqrt(nr, ss).then_inc(amid, 1)
                act.wait_ge(amid, 1)
                nc.scalar.activation(th, nr, ACT.Tanh, scale=rc).then_inc(asem, 1)
                act.wait_ge(dsem, at_["var"])
                nc.scalar.sqrt(nr, t2).then_inc(asem, 1)
def take_edges(nc, d, k):
    with ExitStack() as ctx:
        sb, ps, sem = tools(nc, ctx)
        cur = sb("te_cur", [P, NT], I32)
        prev = sb("te_prev", [P, NT], I32)
        falls = sb("te_falls", [P, NT])
        fall = sb("te_fall", [P, 1])
        fp = ps("te_fp", [1, BANK])
        copied, loaded, compared, reduced, summed, kept = (
            sem(f"te_{x}") for x in ("copied", "loaded", "compared", "reduced", "summed", "kept"))
        with nc.Block() as block:
            @block.sync
            def _(sp):
                sp.dma_start(prev[:, :], d["dst_given"][0:EP].rearrange("(p e) -> p e", e=NT)).then_inc(loaded, 16)
                sp.dma_start(cur[:, :], d["dst_given"][1:EP + 1].rearrange("(p e) -> p e", e=NT)).then_inc(loaded, 16)
                sp.dma_start(d["src"].rearrange("(p e) -> p e", e=NT),
                             d["src_given"].rearrange("(p e) -> p e", e=NT)).then_inc(copied, 16)
                sp.dma_start(d["dst"][0:1].unsqueeze(0), d["dst_given"][0:1].unsqueeze(0)).then_inc(copied, 16)
                sp.dma_start(d["dst"][1:EP + 1].rearrange("(p e) -> p e", e=NT),
                             d["dst_given"][1:EP + 1].rearrange("(p e) -> p e", e=NT)).then_inc(copied, 16)
                sp.dma_start(d["attr8"].rearrange("r (p e) -> (r p) e", p=16),
                             d["attr_given"].rearrange("r (p e) -> (r p) e", p=16)).then_inc(copied, 16)
                sp.wait_ge(copied, 64)

            @block.vector
            def _(dve):
                dve.wait_ge(loaded, 32)
                nc.vector.tensor_tensor(falls[:, :], prev[:, :], cur[:, :], ALU.is_gt).then_inc(compared, 1)
                dve.wait_ge(compared, 1)
                nc.vector.tensor_reduce(fall[:, :], falls[:, :], AX.X, ALU.add).then_inc(reduced, 1)
                dve.wait_ge(summed, 1)
                nc.vector.tensor_copy(k["unsorted"][:, :], fp[:, 0:1]).then_inc(kept, 1)

            @block.tensor
            def _(pe):
                pe.wait_ge(reduced, 1)
                nc.tensor.matmul(fp[:, 0:1], fall[:, :], k["ones"][:, 0:1], start=True, stop=True).then_inc(summed, 1)


def sort_edges(nc, d, k):
    with ExitStack() as ctx:
        sb, ps, sem = tools(nc, ctx)
        srcs = sb("so_src", [P, NT], I32)
        dsts = sb("so_dst", [P, NT], I32)
        attr = sb("so_attr", [P, 3, NT])
        dsh = sb("so_dsh", [P, NT])
        hot = sb("so_hot", [P, NP], F16)
        base = sb("so_base", [P, NP])
        tmp = sb("so_tmp", [P, NP])
        place = sb("so_place", [P, NT])
        half = sb("so_half", [P, NT])
        aplace = sb("so_aplace", [P, NT])
        before = sb("so_before", [P, P], F16)
        rest = sb("so_rest", [P, P], F16)
        all_ = sb("so_all", [P, P], F16)
        val = sb("so_val", [P, 5])
        vali = sb("so_vali", [P, 2], I32)
        pl = sb("so_pl", [P, 5], I32)
        acc = ps("so_acc", [P, 7, BANK])
        loaded, made, masks_ready, step, shifted = (
            sem(f"so_{x}") for x in ("loaded", "made", "masks_ready", "step", "shifted"))
        hots, used, ranked, counted, put, based = (
            sem(f"so_{x}") for x in ("hots", "used", "ranked", "counted", "put", "based"))
        opened = sem("so_opened")
        sent = sem("so_sent", pool_dma=True)
        accv = acc[:, :, :].rearrange("p a b -> p (a b)")[:, 0:NP]
        with nc.Block() as block:
            @block.sync
            def _(sp):
                falls = sp.value_load(k["unsorted"][0:1, 0:1], min_val=0, max_val=EP)
                with sp.If(falls > 0):
                    with nc.allow_non_contiguous_dma(reason="edge columns, on this path alone"):
                        sp.dma_start(srcs[:, :], d["src_given"].rearrange("(t p) -> p t", p=P)).then_inc(loaded, 16)
                        sp.dma_start(dsts[:, :],
                                     d["dst_given"][1:EP + 1].rearrange("(t p) -> p t", p=P)).then_inc(loaded, 16)
                        for h in range(2):
                            for j in range(3):
                                row = d["attr_given"][4 * h + j].rearrange("(t p) -> p t", p=P)
                                sp.dma_start(attr[:, j, h * HT:(h + 1) * HT], row).then_inc(loaded, 16)

            @block.tensor
            def _(pe):
                falls = pe.value_load(k["unsorted"][0:1, 0:1], min_val=0, max_val=EP)
                with pe.If(falls > 0):
                    def add(w, start):
                        for i, (a, n) in enumerate(SPANS):
                            last = nc.tensor.matmul(acc[:, i, 0:n], w, hot[:, a:a + n], start=start, stop=False,
                                                    skip_group_check=True)
                        return last
                    pe.wait_ge(masks_ready, 1)
                    pe.wait_ge(hots, 1)
                    add(all_[:, :], True).then_inc(used, 1)
                    with pe.Fori(1, NT) as t:
                        pe.wait_ge(hots, t + 1)
                        add(all_[:, :], False).then_inc(used, 1)
                    nc.tensor.matmul(acc[0:1, 6, BANK - 1:BANK], all_[:, 0:1], all_[:, 0:1], start=False, stop=True,
                                     skip_group_check=True).then_inc(counted, 1)
                    pe.wait_ge(based, 1)
                    zero_sums(nc, k, acc, P)
                    with pe.Fori(0, NT) as t:
                        pe.wait_ge(hots, t + NT + 1)
                        add(before[:, :], False).then_inc(ranked, 1)
                        pe.wait_ge(put, t + 1)
                        add(rest[:, :], False).then_inc(used, 1)

            @block.gpsimd
            def _(pool):
                falls = pool.value_load(k["unsorted"][0:1, 0:1], min_val=0, max_val=EP)
                with pool.If(falls > 0):
                    G = nc.gpsimd
                    G.memset(all_[:, :], 1.0).then_inc(made, 1)
                    G.memset(before[:, :], 1.0).then_inc(made, 1)
                    G.memset(rest[:, :], 1.0).then_inc(made, 1)
                    pool.wait_ge(made, 3)
                    G.affine_select(out=before[:, :], in_=before[:, :], compare_op=ALU.is_gt, fill=0.0, base=0,
                                    pattern=[[1, P]], channel_multiplier=-1)
                    G.affine_select(out=rest[:, :], in_=rest[:, :], compare_op=ALU.is_ge, fill=0.0, base=0,
                                    pattern=[[-1, P]], channel_multiplier=1).then_inc(masks_ready, 1)
                    attrs = d["attr8"].rearrange("r e -> (r e)")
                    with pool.Fori(0, NT) as t:
                        pool.wait_ge(shifted, t + 1)
                        pool.sem_inc(opened, 1)
                        for j, to in enumerate((d["src"], d["dst"], attrs, attrs, attrs)):
                            what = vali if j < 2 else val
                            pool.indirect_dma_start(to.unsqueeze(1),
                                                    bass.IndirectOffsetOnAxis(ap=pl[:, j:j + 1], axis=0),
                                                    what[:, j:j + 1], None).then_inc(sent, 16)

            @block.vector
            def _(dve):
                falls = dve.value_load(k["unsorted"][0:1, 0:1], min_val=0, max_val=EP)
                with dve.If(falls > 0):
                    V, TT, TS = nc.vector, nc.vector.tensor_tensor, nc.vector.tensor_scalar
                    then = Count(dve, step)
                    dve.wait_ge(loaded, 128)
                    then(V.tensor_copy(dsh[:, :], dsts[:, :]))
                    then(TS(dsh[:, :], dsh[:, :], -float(SHIFT), None, ALU.add))
                    with dve.Fori(0, NT) as t:
                        dve.wait_ge(used, t)
                        TS(hot[:, :], k["iota16"][:, :], dsh[:, bass.ds(t, 1)], None, ALU.is_equal).then_inc(hots, 1)
                    dve.wait_ge(counted, 1)
                    then(V.memset(tmp[:, :], 0.0))
                    then(V.tensor_tensor_scan(base[:, :], accv, tmp[:, :], 0.0, ALU.add, ALU.add))
                    then(TT(base[:, :], base[:, :], accv, ALU.subtract))
                    V.memset(tmp[:, 0:1], 0.0).then_inc(based, 1)
                    first = then.n
                    with dve.Fori(0, NT) as t:
                        dve.wait_ge(used, t + NT)
                        TS(hot[:, :], k["iota16"][:, :], dsh[:, bass.ds(t, 1)], None, ALU.is_equal).then_inc(hots, 1)
                        dve.wait_ge(ranked, t + 1)
                        TT(tmp[:, :], base[:, :], accv, ALU.add).then_inc(put, 1)
                        dve.wait_ge(put, t + 1)
                        TT(tmp[:, :], tmp[:, :], hot[:, :], ALU.mult).then_inc(step, 1)
                        dve.wait_ge(step, 2 * t + first + 1)
                        V.tensor_reduce(place[:, bass.ds(t, 1)], tmp[:, :], AX.X, ALU.add).then_inc(step, 1)
                        dve.wait_ge(step, 2 * t + first + 2)
                    then.n = first + 2 * NT
                    then(TS(half[:, :], place[:, :], float(EP // 2), 3.0 * (EP // 2), ALU.is_ge, ALU.mult))
                    then(TT(aplace[:, :], place[:, :], half[:, :], ALU.add))
                    first = then.n
                    with dve.Fori(0, NT) as t:
                        dve.wait_ge(sent, 80 * t)
                        one = bass.ds(t, 1)
                        V.tensor_copy(vali[:, 0:1], srcs[:, one])
                        V.tensor_copy(vali[:, 1:2], dsts[:, one])
                        for j in range(3):
                            V.tensor_copy(val[:, 2 + j:3 + j], attr[:, j, one])
                            TS(pl[:, 2 + j:3 + j], aplace[:, one], float(j * (EP // 2)), None, ALU.add)
                        V.tensor_copy(pl[:, 0:1], place[:, one])
                        TS(pl[:, 1:2], place[:, one], 1.0, None, ALU.add).then_inc(shifted, 1)
                    dve.wait_ge(sent, 80 * NT)
SUP = 2
WS = SUP * BANK
RING = 4
HALF = NP // 2
HSPANS = [(i * BANK, min(BANK, HALF - i * BANK)) for i in range(-(-HALF // BANK))]
REST = NCH % SUP * BANK
assert NCH // SUP == 2 * NBK


def counts_and_network(nc, d, k):
    with ExitStack() as ctx:
        sb, ps, sem = tools(nc, ctx)
        src_hot = sb("src_hot", [P, 2 * RING, HALF + 2], F16)
        dst_hot = sb("dst_hot", [P, 2 * RING, P], F16)
        cbuf = sb("cbuf", [P, 2, HALF])
        acc = ps("acc", [P, 4, BANK])
        hot = [sem("hot0"), sem("hot1")]
        used = [sem("hot_used0"), sem("hot_used1")]
        drained = [sem(f"bank_drained{i}") for i in range(4)]
        summed = sem("pass_summed")
        stored = [sem("counts_stored0"), sem("counts_stored1")]
        attr = sb("en_attr", [8, 2, WS])
        blk1, blk2, avg, pc, eps = (k[name] for name in ("blk1", "blk2", "avg", "pc", "eps"))
        sq = sb("en_sq", [P, WS])
        rs = sb("en_rs", [P, WS])
        d1 = sb("en_d1", [P, WS])
        out = sb("en_out", [P, 2, WS])
        pa = ps("en_pa", [P, SUP, BANK])
        pv = ps("en_pv", [P, SUP, BANK])
        a_loaded = [sem(f"en_a_loaded{s}") for s in range(2)]
        d_stored = [sem(f"en_stored{s}", pool_dma=True) for s in range(2)]
        lin_a = [sem(f"en_lin_a{s}") for s in range(2)]
        lin_b, sqd, var, lned, rstd, normed, geld = (
            sem(f"en_{x}") for x in ("lin_b", "sqd", "var", "lned", "rstd", "normed", "geld"))

        def block_pairs(eng, b):
            word = eng.value_load(k["pairs"][0:1, bass.ds(b, 1)], min_val=0, max_val=2**31 - 1)
            first = (word & 2**BITS - 1).with_bounds(min_val=0, max_val=NPAIR - LEAST)
            more = (word >> BITS & 2**BITS - 1).with_bounds(min_val=LEAST - 1, max_val=NPAIR - 1)
            done = (word >> 2 * BITS & 2**(BITS + 3) - 1).with_bounds(min_val=0, max_val=4 * NPAIR)
            return eng.snap(first), eng.snap(more), (eng.snap(done), eng.snap(done + more + 1))

        def cut(first, more, eighth):
            return (first + 1 + (more * eighth >> 3)).with_bounds(min_val=1, max_val=NPAIR)

        def flat(t, w):
            return t[:, 0:w // BANK, :].rearrange("p a b -> p (a b)")

        with nc.Block() as block:
            @block.vector
            def _(dve):
                V, TT, TS = nc.vector, nc.vector.tensor_tensor, nc.vector.tensor_scalar
                V.memset(src_hot[:, 0:2, HALF:HALF + 2], 1.0)
                for r in range(1, RING):
                    for j in range(2):
                        V.memset(src_hot[:, 2 * r + j, HALF:HALF + 2], 1.0).then_inc(used[j], 1)
                def hots(b, s, done, lo, hi):
                    with dve.Fori(lo, hi) as t:
                        pair = dve.snap((done + t) % RING * 2)
                        for j in range(2):
                            slot = pair + j
                            dve.wait_ge(used[j], done + t)
                            TS(dst_hot[:, bass.ds(slot, 1), :], k["iota_blk"][:, :].unsqueeze(1),
                               k["blk_first"][:, bass.ds(b, 1)], k["dst_col"][:, bass.ds(2 * t + j, 1)],
                               ALU.add, ALU.is_equal)
                            TS(src_hot[:, bass.ds(slot, 1), 0:HALF],
                               k["iota16"][:, s * HALF:(s + 1) * HALF].unsqueeze(1),
                               k["src_sh"][:, bass.ds(2 * t + j, 1)], None, ALU.is_equal).then_inc(hot[j], 1)

                def norm_a(b, s, w):
                    dve.wait_ge(rstd, 4 * b + 2 * s + 1)
                    TT(d1[:, 0:w], flat(pa, w), rs[:, 0:w], ALU.mult).then_inc(normed, 1)

                def norm_b(b, s, w):
                    dve.wait_ge(rstd, 4 * b + 2 * s + 2)
                    dve.wait_ge(d_stored[s], 16 * b)
                    V.scalar_tensor_tensor(out=out[:, s, 0:w], in0=flat(pa, w), scalar=pc[:, 4:5], in1=rs[:, 0:w],
                                           op0=ALU.add, op1=ALU.mult).then_inc(normed, 1)

                for j in range(2):
                    dve.wait_ge(used[j], RING - 1)
                with dve.Fori(0, NBK) as b:
                    p0, more, passes = block_pairs(dve, b)
                    cut3, cut7, p1 = (cut(p0, more, e) for e in (3, 7, 8))
                    for s, done in enumerate(passes):
                        hots(b, s, done, p0, cut3)
                        norm_a(b, s, WS)
                        hots(b, s, done, cut3, cut7)
                        norm_b(b, s, WS)
                        hots(b, s, done, cut7, p1)
                norm_a(NBK, 0, REST)
                norm_b(NBK, 0, REST)

            @block.tensor
            def _(pe):
                def add(done, t, first):
                    pair = pe.snap((done + t) % RING * 2)
                    for j in range(2):
                        slot = pair + j
                        pe.wait_ge(hot[j], done + t + 1)
                        for i, (a, w) in enumerate(HSPANS):
                            if first is not None and j == 0:
                                pe.wait_ge(drained[i], first)
                            w += 1 if a + w == HALF else 0
                            last = nc.tensor.matmul(acc[:, i, 0:w], dst_hot[:, bass.ds(slot, 1), :],
                                                    src_hot[:, bass.ds(slot, 1), a:a + w],
                                                    start=first is not None and j == 0, stop=False,
                                                    skip_group_check=True)
                        last.then_inc(used[j], 1)

                def adds(done, lo, hi):
                    with pe.Fori(lo, hi) as t:
                        add(done, t, None)

                def linear_a(b, s, w):
                    pe.wait_ge(a_loaded[s], 16 * b + 16)
                    pe.wait_ge(normed, 4 * b + 2 * s)
                    for i in range(w // BANK):
                        last = nc.tensor.matmul(pa[:, i, :], blk1[:, :], attr[:, s, i * BANK:(i + 1) * BANK],
                                                start=True, stop=True)
                    last.then_inc(lin_a[s], 1)

                def linear_b(b, s, w):
                    pe.wait_ge(geld, 4 * b + 2 * s + 1)
                    for i in range(w // BANK):
                        last = nc.tensor.matmul(pa[:, i, :], blk2[:, :], d1[:, i * BANK:(i + 1) * BANK],
                                                start=True, stop=True)
                    last.then_inc(lin_b, 1)

                def variance(b, s, w, r):
                    pe.wait_ge(sqd, 4 * b + 2 * s + r + 1)
                    for i in range(w // BANK):
                        last = nc.tensor.matmul(pv[:, i, :], avg[:, :], sq[:, i * BANK:(i + 1) * BANK],
                                                start=True, stop=True)
                    last.then_inc(var, 1)

                for j in range(2):
                    pe.wait_ge(used[j], RING - 1)
                with pe.Fori(0, NBK) as b:
                    p0, more, passes = block_pairs(pe, b)
                    cut1, cut4, cut5, p1 = (cut(p0, more, e) for e in (1, 4, 5, 8))
                    for s, done in enumerate(passes):
                        linear_a(b, s, WS)
                        add(done, p0, 2 * b + s)
                        adds(done, p0 + 1, cut1)
                        variance(b, s, WS, 0)
                        adds(done, cut1, cut4)
                        linear_b(b, s, WS)
                        adds(done, cut4, cut5)
                        variance(b, s, WS, 1)
                        adds(done, cut5, p1)
                        nc.tensor.matmul(acc[0:1, 3, BANK - 1:BANK], k["ones16"][:, 0:1], k["ones16"][:, 0:1],
                                         start=False, stop=True, skip_group_check=True).then_inc(summed, 1)
                linear_a(NBK, 0, REST)
                variance(NBK, 0, REST, 0)
                linear_b(NBK, 0, REST)
                variance(NBK, 0, REST, 1)

            @block.scalar
            def _(act):
                def rsqrt(b, s, w, r):
                    nc.scalar.activation(sq[:, 0:w], flat(pa, w), ACT.Square,
                                         bias=pc[:, 4:5] if r else 0.0).then_inc(sqd, 1)
                    nc.scalar.preload_act_table_set("natural_log_exp_and_others")
                    act.wait_ge(var, 4 * b + 2 * s + r + 1)
                    nc.scalar.activation(rs[:, 0:w], flat(pv, w), ACT.Ln, bias=eps[:, 0:1]).then_inc(lned, 1)
                    act.wait_ge(lned, 4 * b + 2 * s + r + 1)
                    nc.scalar.activation(rs[:, 0:w], rs[:, 0:w], ACT.Exp, scale=-0.5).then_inc(rstd, 1)

                def gelu(b, s, r, t):
                    act.wait_ge(normed, 4 * b + 2 * s + r + 1)
                    nc.scalar.activation(t, t, ACT.Gelu, scale=pc[:, 2 * r:2 * r + 1],
                                         bias=pc[:, 2 * r + 1:2 * r + 2]).then_inc(geld, 1)

                def first_layer(b, s, w):
                    act.wait_ge(lin_a[s], b + 1)
                    rsqrt(b, s, w, 0)
                    gelu(b, s, 0, d1[:, 0:w])
                    act.wait_ge(lin_b, 2 * b + s + 1)
                    rsqrt(b, s, w, 1)

                with act.Fori(0, NBK) as b:
                    for s in range(2):
                        first_layer(b, s, WS)
                        act.wait_ge(summed, 2 * b + s + 1)
                        act.wait_ge(stored[s], 16 * b)
                        for i, (a, w) in enumerate(HSPANS):
                            if s and a + w == HALF:
                                nc.scalar.copy(k["deg"][:, bass.ds(b, 1)], acc[:, i, w:w + 1])
                            nc.scalar.copy(cbuf[:, s, a:a + w], acc[:, i, 0:w]).then_inc(drained[i], 1)
                        gelu(b, s, 1, out[:, s, :])
                first_layer(NBK, 0, REST)
                gelu(NBK, 0, 1, out[:, 0, 0:REST])

            @block.sync
            def _(sp):
                def load(b, s, w):
                    sp.wait_ge(lin_a[s], b)
                    sp.dma_start(attr[:, s, 0:w], d["attr8"][:, bass.ds((2 * b + s) * WS, w)]).then_inc(a_loaded[s], 16)

                def store(b, s):
                    for i in range(4):
                        sp.wait_ge(drained[i], 2 * b + s + 1)
                    sp.dma_start(d["counts"][bass.ds(b * P, P), s * HALF:(s + 1) * HALF],
                                 cbuf[:, s, :]).then_inc(stored[s], 16)
                load(0, 0, WS)
                with sp.Fori(0, NBK - 1) as b:
                    load(b, 1, WS)
                    store(b, 0)
                    load(b + 1, 0, WS)
                    store(b, 1)
                load(NBK - 1, 1, WS)
                store(NBK - 1, 0)
                load(NBK, 0, REST)
                store(NBK - 1, 1)
                for s in range(2):
                    sp.wait_ge(stored[s], 16 * NBK)

            @block.gpsimd
            def _(pool):
                def store(b, s, w):
                    pool.wait_ge(geld, 4 * b + 2 * s + 2)
                    pool.dma_start(d["dnet"][:, bass.ds((2 * b + s) * WS, w)], out[:, s, 0:w]).then_inc(d_stored[s], 16)
                with pool.Fori(0, NBK) as b:
                    store(b, 0, WS)
                    store(b, 1, WS)
                store(NBK, 0, REST)
                pool.wait_ge(d_stored[0], 16 * (NBK + 1))
                pool.wait_ge(d_stored[1], 16 * NBK)


def finish_norm(nc, act, dsem, at_, asem, nr, var):
    act.wait_ge(dsem, at_["var"])
    nc.scalar.sqrt(nr, var).then_inc(asem, 1)


def attention_rows(nc, d, k):
    with ExitStack() as ctx:
        sb, ps, sem = tools(nc, ctx)
        wrow = sb("ar_wrow", [P, F])
        a2row = sb("ar_a2row", [P, F])
        a1 = sb("ar_a1", [F, 1])
        a1b = sb("ar_a1b", [F, P])
        sq = sb("ar_sq", [P, NBK, F])
        sd = sb("ar_sd", [P, NBK])
        hT = sb("ar_hT", [F, NP])
        pt = ps("ar_pt", [P, 7, BANK])
        loaded, dsem, turned, evac, prod = (sem(f"ar_{x}") for x in ("loaded", "dve", "turned", "evac", "prod"))
        steps = {}
        with nc.Block() as block:
            @block.sync
            def _(sp):
                sp.dma_start(wrow[:, :], d["W1"].unsqueeze(0).to_broadcast([P, F])).then_inc(loaded, 16)
                sp.dma_start(a2row[:, :], d["a1"][F:2 * F].unsqueeze(0).to_broadcast([P, F])).then_inc(loaded, 16)
                sp.dma_start(a1[:, :], d["a1"][0:F].unsqueeze(1)).then_inc(loaded, 16)

            @block.vector
            def _(dve):
                then = Count(dve, dsem)
                steps["dve"] = then.at
                dve.wait_ge(loaded, 48)
                then(nc.vector.tensor_copy(a1b[:, :], a1[:, :].to_broadcast([F, P])))
                then(nc.vector.tensor_tensor(k["val"][:, :, 0:F], k["x"][:, :, :],
                                             wrow[:, :].unsqueeze(1).to_broadcast([P, NBK, F]), ALU.mult), "h")
                then(nc.vector.tensor_tensor(sq[:, :, :], k["val"][:, :, 0:F],
                                             a2row[:, :].unsqueeze(1).to_broadcast([P, NBK, F]), ALU.mult))
                then(nc.vector.tensor_reduce(sd[:, :], sq[:, :, :], AX.X, ALU.add))
                then(nc.vector.tensor_scalar(k["sdst"][:, 0, :], sd[:, :], 0.8, None, ALU.mult))
                then(nc.vector.tensor_scalar(k["sdst"][:, 1, :], sd[:, :], 0.2, None, ALU.mult))

            @block.tensor
            def _(pe):
                pe.wait_ge(dsem, steps["dve"]["h"])
                turn_blocks(pe, nc, k, pt, k["val"], F, turned)
                pe.wait_ge(evac, 1)
                for i, (a, w) in enumerate(SPANS):
                    last = nc.tensor.matmul(pt[:, i, 0:w], a1b[:, :], hT[:, a:a + w], start=True, stop=True)
                last.then_inc(prod, 1)

            @block.scalar
            def _(act):
                act.wait_ge(turned, 1)
                for i, (a, w) in enumerate(SPANS):
                    last = nc.scalar.copy(hT[:, a:a + w], pt[0:F, i, 0:w])
                last.then_inc(evac, 1)
                act.wait_ge(prod, 1)
                for i, (a, w) in enumerate(SPANS):
                    nc.scalar.copy(k["toprow"][:, a:a + w], pt[:, i, 0:w])


def score_sums(nc, d, k):
    with ExitStack() as ctx:
        sb, ps, sem = tools(nc, ctx)
        cnt = sb("ss_cnt", [P, 2, NP])
        z = sb("ss_z", [P, 2, NP])
        w_ = sb("ss_w", [P, 2, NP])
        val = sb("ss_val", [P, 2, W65])
        acc = ps("ss_acc", [P, 7, BANK])
        loaded, relued, added, exped, val_ready, summed = (
            [sem(f"ss_{x}{s}") for s in range(2)]
            for x in ("loaded", "relued", "added", "exped", "val_ready", "summed"))
        weighed = [[sem(f"ss_weighed{s}_{c}") for c in range(2)] for s in range(2)]
        waited = sem("ss_waited")
        done = sem("ss_done")
        with nc.Block() as block:
            @block.sync
            def _(sp):
                def load(h, s):
                    for c in range(2):
                        sp.wait_ge(weighed[s][c], h)
                    sp.dma_start(cnt[:, s, :], d["counts"][bass.ds((2 * h + s) * P, P), :]).then_inc(loaded[s], 16)
                over_blocks(sp, load)

            @block.gpsimd
            def _(pool):
                def body(h, s):
                    pool.wait_ge(summed[s], 2 * h)
                    nc.gpsimd.tensor_copy(val[:, s, :].unsqueeze(1), k["val"][:, bass.ds(2 * h + s, 1), 0:W65])\
                      .then_inc(val_ready[s], 1)
                over_blocks(pool, body)

            @block.scalar
            def _(act):
                def relu(h, s, c):
                    cs = columns(c)
                    act.wait_ge(weighed[s][c], h)
                    act.sem_inc(waited, 1)
                    nc.scalar.activation(z[:, s, cs], k["toprow"][:, cs], ACT.Relu, scale=0.8,
                                         bias=k["sdst"][:, 0, bass.ds(2 * h + s, 1)]).then_inc(relued[s], 1)

                def exp(h, s, c):
                    cs = columns(c)
                    act.wait_ge(added[s], 2 * h + c + 1)
                    act.sem_inc(waited, 1)
                    nc.scalar.activation(z[:, s, cs], z[:, s, cs], ACT.Exp,
                                         bias=k["sdst"][:, 1, bass.ds(2 * h + s, 1)]).then_inc(exped[s], 1)
                for c in range(2):
                    relu(0, 0, c)
                with act.Fori(0, NBK // 2) as h:
                    for s in range(2):
                        for c in range(2):
                            relu(h + s, 1 - s, c)
                            exp(h, s, c)
                for c in range(2):
                    exp(NBK // 2, 0, c)
                act.wait_ge(done, 1)
                for i, (a, w) in enumerate(SPANS):
                    nc.scalar.copy(k["sums"][0:W65, a:a + w], acc[0:W65, i, 0:w])

            @block.vector
            def _(dve):
                def add(h, s, c):
                    cs = columns(c)
                    dve.wait_ge(relued[s], 2 * h + c + 1)
                    nc.vector.scalar_tensor_tensor(out=z[:, s, cs], in0=k["toprow"][:, cs], scalar=0.2, in1=z[:, s, cs],
                                                   op0=ALU.mult, op1=ALU.add).then_inc(added[s], 1)

                def weigh(h, s, c):
                    cs = columns(c)
                    dve.wait_ge(exped[s], 2 * h + c + 1)
                    dve.wait_ge(loaded[s], 16 * h + 16)
                    dve.wait_ge(summed[s], 2 * h)
                    nc.vector.scalar_tensor_tensor(out=w_[:, s, cs], in0=z[:, s, cs], scalar=3e38, in1=cnt[:, s, cs],
                                                   op0=ALU.min, op1=ALU.mult).then_inc(weighed[s][c], 1)
                for c in range(2):
                    add(0, 0, c)
                with dve.Fori(0, NBK // 2) as h:
                    for s in range(2):
                        for c in range(2):
                            add(h + s, 1 - s, c)
                            weigh(h, s, c)
                for c in range(2):
                    weigh(NBK // 2, 0, c)

            @block.tensor
            def _(pe):
                zero_sums(nc, k, acc, W65)
                over_blocks(pe, lambda h, s: add_weighed(nc, pe, h, s, acc, val, w_, weighed, val_ready, summed))
                nc.tensor.matmul(acc[0:1, 6, BANK - 1:BANK], k["zeros"][:, 0:1], k["zeros"][:, 0:1],
                                 start=False, stop=True, skip_group_check=True).then_inc(done, 1)


def end_attention(nc, d, k):
    with ExitStack() as ctx:
        sb, ps, sem = tools(nc, ctx)
        v = sb("ea_v", [P, NBK, F])
        t = sb("ea_t", [P, NBK, F])
        xT = sb("ea_xT", [F, NP])
        w123 = sb("ea_w123", [F, 3 * F])
        w23 = sb("ea_w23", [P, NBK, 2 * F])
        col = sb("ea_col", [P, 4, NBK])
        den, nr, t1, t2 = (col[:, i, :] for i in range(4))
        pb = ps("ea_pb", [P, 7, BANK])
        back, dsem, asem, loaded, turned, evac, prod, kept, stored = (
            sem(f"ea_{x}") for x in ("back", "dve", "act", "loaded", "turned", "evac", "prod", "kept",
                                     "stored"))
        x = k["x"]
        steps = {}
        NROUND = -(-NBK // 14)
        with nc.Block() as block:
            @block.sync
            def _(sp):
                for i, n in enumerate(("W2_1", "W2_2", "W2_3")):
                    sp.dma_start(w123[:, i * F:(i + 1) * F], d[n]).then_inc(loaded, 16)
                sp.wait_ge(kept, 4 * NROUND)
                sp.dma_start(d["w23"].rearrange("(b p) f -> p b f", p=P), w23[:, :, :]).then_inc(stored, 16)
                sp.wait_ge(stored, 16)

            @block.vector
            def _(dve):
                then = Count(dve, dsem)
                steps["dve"] = then.at
                dve.wait_ge(back, 1)
                for g in range(4):
                    lo, hi = 7 * g, min(NBK, 7 * g + 7)
                    rows = pb[:, g, 0:(hi - lo) * W65].rearrange("p (b f) -> p b f", f=W65)
                    then(nc.vector.tensor_tensor(den[:, lo:hi], rows[:, :, F], k["is_pad"][:, lo:hi], ALU.add))
                    then(nc.vector.reciprocal(den[:, lo:hi], den[:, lo:hi]))
                    then(nc.vector.tensor_tensor(v[:, lo:hi, :], rows[:, :, 0:F],
                                                 den[:, lo:hi].unsqueeze(2).to_broadcast([P, hi - lo, F]), ALU.mult))
                elu(nc, then, lambda: dve.wait_ge(asem, 1), v[:, :, :], t[:, :, :])
                then(nc.vector.tensor_tensor(x[:, :, :], x[:, :, :], v[:, :, :], ALU.add))
                layernorm_stats(nc, then, x[:, :, :], t, t1, t2, "var")
                dve.wait_ge(asem, 2)
                then(nc.vector.reciprocal(t1, nr))
                then(nc.vector.tensor_tensor(x[:, :, :], x[:, :, :], spread(t1), ALU.mult), "x")

            @block.scalar
            def _(act):
                at_ = steps["dve"]
                act.wait_ge(dsem, at_["elu"])
                nc.scalar.activation(t[:, :, :], t[:, :, :], ACT.Exp).then_inc(asem, 1)
                finish_norm(nc, act, dsem, at_, asem, nr, t2)
                act.wait_ge(turned, 1)
                for i, (a, w) in enumerate(SPANS):
                    last = nc.scalar.copy(xT[:, a:a + w], pb[0:F, i, 0:w])
                last.then_inc(evac, 1)
                for r in range(NROUND):
                    act.wait_ge(prod, r + 1)
                    for j in range(2):
                        b0, b1 = 14 * r, min(NBK, 14 * r + 14)
                        for q in range(2):
                            n = len(range(b0 + q, b1, 2))
                            src = pb[:, 0:n, q * 3 * F:(q + 1) * 3 * F]
                            if j == 0:
                                last = nc.scalar.copy(k["w1x"][:, b0 + q:b1:2, :], src[:, :, 0:F])
                            else:
                                last = nc.scalar.copy(w23[:, b0 + q:b1:2, :], src[:, :, F:3 * F])
                            last.then_inc(kept, 1)

            @block.tensor
            def _(pe):
                back_blocks(pe, nc, k, pb, k["sums"], W65, back)
                pe.wait_ge(dsem, steps["dve"]["x"])
                turn_blocks(pe, nc, k, pb, x, F, turned)
                pe.wait_ge(evac, 1)
                pe.wait_ge(loaded, 48)
                for r in range(NROUND):
                    if r:
                        pe.wait_ge(kept, 4 * r)
                    for b in range(14 * r, min(NBK, 14 * r + 14)):
                        i = b - 14 * r
                        last = nc.tensor.matmul(pb[:, i // 2, (i % 2) * 3 * F:(i % 2 + 1) * 3 * F],
                                                xT[:, b * P:(b + 1) * P], w123[:, :], start=True, stop=True)
                    last.then_inc(prod, 1)


def over_pairs(eng, n, body):
    with eng.Fori(0, n // 2) as h:
        body(h, 0)
        body(h, 1)
    body(n // 2, 0)


ROW = 3 * F


def edge_softmax(nc, d, k):
    with ExitStack() as ctx:
        sb, ps, sem = tools(nc, ctx)
        idx = sb("es_idx", [P, 2, 2, CT], I32)
        opened = sem("es_opened")
        got = sb("es_got", [P, 2, CT, 2, 2 * F])
        dn = sb("es_dn", [P, 2, BANK])
        st = sb("es_st", [2, 2, BANK], BF16)
        sel = sb("es_sel", [2, P], BF16)
        lg = sb("es_lg", [P, 2, BANK])
        v3 = sb("es_v3", [P, 2, BANK])
        mx = sb("es_mx", [P, 2, BANK + 1])
        dec = sb("es_dec", [P, 2, BANK])
        e = sb("es_e", [P, 2, BANK])
        ev = sb("es_ev", [P, 2, BANK])
        s0 = sb("es_s0", [P, 2, BANK])
        s1 = sb("es_s1", [P, 2, BANK])
        rows = sb("es_rows", [P, 2, CT, 2, ROW])
        w2p = ps("es_w2p", [P, BANK])
        w3p = ps("es_w3p", [P, BANK])
        pen = ps("es_pen", [P, 2, BANK])
        rp = ps("es_rp", [P, 4, BANK])
        idx_ready, dn_loaded, stored, st_loaded, turned3 = (
            [sem(f"es_{x}{s}") for s in range(2)]
            for x in ("idx_ready", "dn_loaded", "stored", "st_loaded", "turned3_"))
        gathered = [sem(f"es_gathered{s}", pool_dma=True) for s in range(2)]
        one = ("sel_made", "turned2", "penned", "lg_ready", "v3_ready", "max_ready", "pen_used", "dec_in", "e_in",
               "dec_ready", "e_ready", "ev_ready", "s0_ready", "s1_ready", "rows_turned", "rows_out", "carry", "zeroed")
        (sel_made, turned2, penned, lg_ready, v3_ready, max_ready, pen_used, dec_in, e_in,
         dec_ready, e_ready, ev_ready, s0_ready, s1_ready, rows_turned, rows_out, carry, zeroed) = (
             sem(f"es_{x}") for x in one)
        with nc.Block() as block:
            @block.gpsimd
            def _(pool):
                def body(h, s):
                    pool.wait_ge(idx_ready[s], 2 * h + 2)
                    pool.wait_ge(turned3[s], h)
                    pool.sem_inc(opened, 1)
                    for t in range(CT):
                        for half in range(2):
                            pool.indirect_dma_start(
                                got[:, s, t, half, :], None, d["w23"],
                                bass.IndirectOffsetOnAxis(ap=idx[:, s, half, t:t + 1], axis=0)).then_inc(gathered[s], 16)
                over_pairs(pool, NCH, body)

            @block.sync
            def _(sp):
                def load(h, s):
                    c = 2 * h + s
                    sp.wait_ge(penned, 2 * h)
                    sp.wait_ge(v3_ready, 2 * h)
                    sp.dma_start(dn[:, s, :], d["dnet"][:, bass.ds(c * BANK, BANK)]).then_inc(dn_loaded[s], 16)
                    sp.dma_start(st[:, s, :], d["starts"][:, bass.ds(c * BANK, BANK)]).then_inc(st_loaded[s], 16)
                over_pairs(sp, NCH, load)

            @block.tensor
            def _(pe):
                pe.wait_ge(sel_made, 1)

                def turn_in(h, s):
                    c = 2 * h + s
                    pe.wait_ge(st_loaded[s], 16 * h + 16)
                    pe.wait_ge(pen_used, 2 * h)
                    nc.tensor.matmul(pen[:, s, :], sel[:, :], st[:, s, :], start=True, stop=True).then_inc(penned, 1)
                    pe.wait_ge(gathered[s], 16 * 2 * CT * (h + 1))
                    pe.wait_ge(lg_ready, c)
                    for t in range(CT):
                        nc.tensor.matmul(w2p[F:2 * F, t * P:(t + 1) * P], got[:, s, t, 1, 0:F],
                                         k["ident"][:, :], start=True, stop=True)
                        last = nc.tensor.transpose(w2p[0:F, t * P:(t + 1) * P], got[:, s, t, 0, 0:F], k["ident"][:, :])
                    last.then_inc(turned2, 1)
                    pe.wait_ge(v3_ready, c)
                    for t in range(CT):
                        nc.tensor.matmul(w3p[F:2 * F, t * P:(t + 1) * P], got[:, s, t, 1, F:2 * F],
                                         k["ident"][:, :], start=True, stop=True)
                        last = nc.tensor.transpose(w3p[0:F, t * P:(t + 1) * P], got[:, s, t, 0, F:2 * F], k["ident"][:, :])
                    last.then_inc(turned3[s], 1)

                def turn_out(h, s):
                    c = 2 * h + s
                    for i, (x, done) in enumerate(((mx, max_ready), (s0, s0_ready), (s1, s1_ready))):
                        pe.wait_ge(done, c + 1)
                    pe.wait_ge(rows_out, CT * c)
                    for t in range(CT):
                        for i, x in enumerate((mx, s0, s1)):
                            o = 1 if i == 0 else 0
                            last = nc.tensor.transpose(rp[:, t, i * P:(i + 1) * P],
                                                       x[:, s, o + t * P:o + (t + 1) * P], k["ident"][:, :])
                        last.then_inc(rows_turned, 1)
                turn_in(0, 0)
                with pe.Fori(0, NCH // 2) as h:
                    turn_in(h, 1)
                    turn_out(h, 0)
                    turn_in(h + 1, 0)
                    turn_out(h, 1)
                turn_out(NCH // 2, 0)

            @block.vector
            def _(dve):
                nc.vector.memset(mx[:, 1, BANK:BANK + 1], -BIG).then_inc(zeroed, 1)
                nc.vector.memset(s0[:, 1, BANK - 1:BANK], 0.0).then_inc(zeroed, 1)
                nc.vector.memset(s1[:, 1, BANK - 1:BANK], 0.0).then_inc(zeroed, 1)
                dve.wait_ge(zeroed, 3)

                def indices(h, s):
                    for half in range(2):
                        nc.vector.tensor_copy(
                            idx[:, s, half, :],
                            k["src_idx"][:, bass.ds(half * HT + (2 * h + s) * CT, CT)]).then_inc(idx_ready[s], 1)

                indices(0, 0)
                indices(0, 1)

                def body(h, s):
                    c = 2 * h + s
                    o = 1 - s
                    dve.wait_ge(dn_loaded[s], 16 * h + 16)
                    dve.wait_ge(turned2, c + 1)
                    dve.wait_ge(gathered[s], 16 * 2 * CT * h + 16 * 2 * CT)
                    indices(h + 1, s)
                    dve.wait_ge(e_in, 2 * h)
                    nc.vector.tensor_tensor(lg[:, s, :], dn[:, s, :], w2p[:, :], ALU.subtract).then_inc(lg_ready, 1)
                    dve.wait_ge(turned3[s], h + 1)
                    nc.vector.tensor_tensor(v3[:, s, :], dn[:, s, :], w3p[:, :], ALU.add).then_inc(v3_ready, 1)
                    dve.wait_ge(penned, c + 1)
                    dve.wait_ge(rows_turned, 2 * CT * h)
                    nc.vector.tensor_copy(mx[:, s, 0:1], mx[:, o, BANK:BANK + 1]).then_inc(carry, 1)
                    dve.wait_ge(lg_ready, c + 1)
                    nc.vector.tensor_tensor_scan(mx[:, s, 1:BANK + 1], pen[:, s, :], lg[:, s, :],
                                                 mx[:, o, BANK:BANK + 1], ALU.add, ALU.max).then_inc(max_ready, 1)
                    dve.wait_ge(carry, c + 1)
                    dve.wait_ge(max_ready, c + 1)
                    nc.vector.tensor_tensor(dec[:, s, :], pen[:, s, :], mx[:, s, 0:BANK], ALU.add).then_inc(pen_used, 1)
                    nc.vector.tensor_tensor(e[:, s, :], lg[:, s, :], mx[:, s, 1:BANK + 1], ALU.subtract).then_inc(e_in, 1)
                    dve.wait_ge(pen_used, c + 1)
                    nc.vector.tensor_tensor(dec[:, s, :], dec[:, s, :], mx[:, s, 1:BANK + 1],
                                            ALU.subtract).then_inc(dec_in, 1)
                    dve.wait_ge(e_ready, c + 1)
                    dve.wait_ge(v3_ready, c + 1)
                    nc.vector.tensor_tensor(ev[:, s, :], e[:, s, :], v3[:, s, :], ALU.mult).then_inc(ev_ready, 1)
                    dve.wait_ge(dec_ready, c + 1)
                    nc.vector.tensor_tensor_scan(s0[:, s, :], dec[:, s, :], e[:, s, :], s0[:, o, BANK - 1:BANK],
                                                 ALU.mult, ALU.add).then_inc(s0_ready, 1)
                    dve.wait_ge(ev_ready, c + 1)
                    nc.vector.tensor_tensor_scan(s1[:, s, :], dec[:, s, :], ev[:, s, :], s1[:, o, BANK - 1:BANK],
                                                 ALU.mult, ALU.add).then_inc(s1_ready, 1)
                    dve.wait_ge(s0_ready, c + 1)
                    dve.wait_ge(s1_ready, c + 1)
                over_pairs(dve, NCH, body)

            @block.scalar
            def _(act):
                nc.scalar.copy(sel[:, :], k["half_sel"][:, :]).then_inc(sel_made, 1)

                def exps(h, s):
                    c = 2 * h + s
                    act.wait_ge(e_in, c + 1)
                    nc.scalar.activation(e[:, s, :], e[:, s, :], ACT.Exp).then_inc(e_ready, 1)
                    act.wait_ge(dec_in, c + 1)
                    nc.scalar.activation(dec[:, s, :], dec[:, s, :], ACT.Exp).then_inc(dec_ready, 1)

                def rows_to(h, s):
                    c = 2 * h + s
                    act.wait_ge(stored[s], 16 * 2 * h)
                    for t in range(CT):
                        act.wait_ge(rows_turned, CT * c + t + 1)
                        nc.scalar.copy(rows[:, s, t, :, :].rearrange("p h (q f) -> p h q f", f=F),
                                       rp[:, t, 0:3 * P].rearrange("p (q h f) -> p h q f", q=3, h=2)).then_inc(rows_out, 1)
                    act.wait_ge(rows_out, CT * c + CT)
                    for half in range(2):
                        r = (half * HT + c * CT) * P
                        act.dma_start(d["rows"][bass.ds(r, CT * P), :].rearrange("(t p) w -> p t w", p=P),
                                      rows[:, s, :, half, :]).then_inc(stored[s], 16)
                exps(0, 0)
                with act.Fori(0, NCH // 2) as h:
                    exps(h, 1)
                    rows_to(h, 0)
                    exps(h + 1, 0)
                    rows_to(h, 1)
                rows_to(NCH // 2, 0)
                act.wait_ge(stored[0], 32 * (NCH // 2 + 1))
                act.wait_ge(stored[1], 32 * (NCH // 2))


def end_edges(nc, d, k):
    with ExitStack() as ctx:
        sb, ps, sem = tools(nc, ctx)
        col = sb("ee_col", [P, 10, NBK])
        cum, last_, first, stra, has, idf, t1, t2, nr, tot = (col[:, i, :] for i in range(10))
        idx = sb("ee_idx", [P, NBK], I32)
        mid = sb("ee_mid", [P, ROW])
        r = sb("ee_r", [P, NBK, ROW])
        l2 = sb("ee_l2", [P, NBK, F])
        a = sb("ee_a", [P, NBK, F])
        b_ = sb("ee_b", [P, NBK, F])
        m = sb("ee_m", [P, NBK, F])
        zf = sb("ee_zf", [P, NBK])
        pp = ps("ee_pp", [P, 2, BANK])
        dsem, asem, loaded, prods = (sem(f"ee_{x}") for x in ("dve", "act", "loaded", "prods"))
        gathered = sem("ee_gathered", pool_dma=True)
        x, w1, deg = k["x"], k["w1x"], k["deg"]
        MID = float(EP // 2)
        steps = {}
        with nc.Block() as block:
            @block.sync
            def _(sp):
                sp.dma_start(mid[:, :], d["rows"][EP // 2 - 1:EP // 2, :].to_broadcast([P, ROW])).then_inc(loaded, 16)

            @block.tensor
            def _(pe):
                nc.tensor.matmul(pp[:, 0, 0:NBK], k["upper"][:, :], deg[:, :], start=True, stop=True)
                nc.tensor.matmul(pp[:, 1, 0:NBK], k["ones"][:, :], deg[:, :], start=True, stop=True).then_inc(prods, 1)

            @block.vector
            def _(dve):
                then = Count(dve, dsem)
                steps["dve"] = then.at
                V, TT, TS = nc.vector, nc.vector.tensor_tensor, nc.vector.tensor_scalar
                dve.wait_ge(prods, 1)
                then(V.memset(zf[:, :], 0.0))
                then(V.tensor_copy(tot, pp[:, 1, 0:NBK]))
                then(V.tensor_tensor_scan(t1, tot, zf[:, :], 0.0, ALU.add, ALU.add))
                then(TT(t1, t1, tot, ALU.subtract))
                then(TT(cum, t1, pp[:, 0, 0:NBK], ALU.add))
                then(TS(last_, cum, -1.0, None, ALU.add))
                then(TT(first, cum, deg[:, :], ALU.subtract))
                then(TS(has, deg[:, :], 1.0, None, ALU.min))
                then(TS(stra, first, MID, None, ALU.is_lt))
                then(TS(t2, last_, MID, None, ALU.is_ge))
                then(TT(stra, stra, t2, ALU.mult))
                then(TT(stra, stra, has, ALU.mult))
                then(TS(idf, last_, 0.0, None, ALU.max))
                then(V.tensor_copy(idx[:, :], idf), "idx")
                dve.wait_ge(loaded, 16)
                dve.wait_ge(gathered, 16 * NBK)
                m1, s0, s1 = (r[:, :, i * F:(i + 1) * F] for i in range(3))
                m2, z0, z1 = (mid[:, i * F:(i + 1) * F].unsqueeze(1).to_broadcast([P, NBK, F]) for i in range(3))
                then(TT(l2[:, :, :], w1[:, :, :], m2, ALU.add))
                then(TT(a[:, :, :], w1[:, :, :], m1, ALU.add))
                then(TT(m[:, :, :], l2[:, :, :], a[:, :, :], ALU.subtract))
                then(TS(m[:, :, :], m[:, :, :], 0.0, None, ALU.max))
                then(TT(m[:, :, :], m[:, :, :], spread(stra), ALU.mult))
                then(TT(m[:, :, :], m[:, :, :], a[:, :, :], ALU.add))
                then(TT(a[:, :, :], a[:, :, :], m[:, :, :], ALU.subtract))
                then(TT(b_[:, :, :], l2[:, :, :], m[:, :, :], ALU.subtract))
                then(TS(b_[:, :, :], b_[:, :, :], 0.0, None, ALU.min), "shifts")
                dve.wait_ge(asem, 2)
                then(TT(b_[:, :, :], b_[:, :, :], spread(stra), ALU.mult))
                then(TT(m[:, :, :], s0, a[:, :, :], ALU.mult))
                then(TT(l2[:, :, :], b_[:, :, :], z0, ALU.mult))
                then(TT(m[:, :, :], m[:, :, :], l2[:, :, :], ALU.add))
                then(V.reciprocal(m[:, :, :], m[:, :, :]))
                then(TT(m[:, :, :], m[:, :, :], spread(has), ALU.mult))
                then(TT(a[:, :, :], a[:, :, :], s1, ALU.mult))
                then(TT(b_[:, :, :], b_[:, :, :], z1, ALU.mult))
                then(TT(a[:, :, :], a[:, :, :], b_[:, :, :], ALU.add))
                then(TT(a[:, :, :], a[:, :, :], m[:, :, :], ALU.mult))
                then(TT(x[:, :, :], x[:, :, :], a[:, :, :], ALU.add))
                layernorm_stats(nc, then, x[:, :, :], a, t1, t2, "var")
                dve.wait_ge(asem, 3)
                then(V.reciprocal(t1, nr))
                then(TT(x[:, :, :], x[:, :, :], spread(t1), ALU.mult))

            @block.gpsimd
            def _(pool):
                pool.wait_ge(dsem, steps["dve"]["idx"])
                for b in range(NBK):
                    pool.indirect_dma_start(r[:, b, :], None, d["rows"],
                                            bass.IndirectOffsetOnAxis(ap=idx[:, b:b + 1], axis=0)).then_inc(gathered, 16)

            @block.scalar
            def _(act):
                at_ = steps["dve"]
                act.wait_ge(dsem, at_["shifts"])
                nc.scalar.activation(a[:, :, :], a[:, :, :], ACT.Exp).then_inc(asem, 1)
                nc.scalar.activation(b_[:, :, :], b_[:, :, :], ACT.Exp).then_inc(asem, 1)
                act.wait_ge(dsem, at_["var"])
                nc.scalar.sqrt(nr, t2).then_inc(asem, 1)


HID = 2 * F


FIVE = 5
assert NBK % FIVE == 0


def over_fives(eng, body):
    with eng.Fori(0, NBK // FIVE) as h:
        for s in range(FIVE):
            body(h, s)


def ahead_fives(eng, ahead, body):
    ahead(0, 0)
    with eng.Fori(0, NBK // FIVE - 1) as h:
        for s in range(FIVE):
            ahead(h + (s + 1) // FIVE, (s + 1) % FIVE)
            body(h, s)
    for s in range(FIVE):
        if s + 1 < FIVE:
            ahead(NBK // FIVE - 1, s + 1)
        body(NBK // FIVE - 1, s)


def sum_neighbours(nc, d, k, tag, val, agg):
    with ExitStack() as ctx:
        sb, ps, sem = tools(nc, ctx)
        cnt = sb(f"{tag}_cnt", [P, FIVE, NP])
        ct = sb(f"{tag}_ct", [P, FIVE, NP])
        ct16 = sb(f"{tag}_ct16", [P, FIVE, NP], BF16)
        parts = sb(f"{tag}_parts", [P, NBK, 3, F], BF16)
        tp = ps(f"{tag}_tp", [P, 3, BANK])
        acc = ps(f"{tag}_acc", [P, FIVE, BANK])
        loaded, turned, copied, summed, taken = (
            [sem(f"{tag}_{x}{s}") for s in range(FIVE)] for x in ("loaded", "turned", "copied", "summed", "taken"))
        rest = agg
        split, two = sem(f"{tag}_split"), sem(f"{tag}_two")
        NS = len(SPANS)

        def either(eng, program):
            many = eng.value_load(k["many"][0:1, 0:1], min_val=0, max_val=1)
            with eng.If(many < 1):
                program(True)
            with eng.If(many > 0):
                program(False)

        with nc.Block() as block:
            @block.sync
            def _(sp):
                def load(h, s):
                    sp.wait_ge(turned[s], NS * h)
                    sp.dma_start(cnt[:, s, :], d["counts"][bass.ds((FIVE * h + s) * P, P), :]).then_inc(loaded[s], 16)
                over_fives(sp, load)

            @block.scalar
            def _(act):
                def copies(small):
                    def copy(h, s):
                        act.wait_ge(summed[s], h)
                        for i, (a, w) in enumerate(SPANS):
                            act.wait_ge(turned[s], NS * h + i + 1)
                            nc.scalar.copy((ct16 if small else ct)[:, s, a:a + w],
                                           tp[:, i % 3, 0:w]).then_inc(copied[s], 1)
                    over_fives(act, copy)
                either(act, copies)

            @block.tensor
            def _(pe):
                def turn(h, s):
                    pe.wait_ge(loaded[s], 16 * h + 16)
                    for i, (a, w) in enumerate(SPANS):
                        if i >= 3:
                            pe.wait_ge(copied[s], NS * h + i - 2)
                        elif s:
                            pe.wait_ge(copied[s - 1], NS * h + (7, 5, 6)[i])
                        else:
                            pe.wait_ge(copied[FIVE - 1], NS * h)
                        for j in range(w // P):
                            last = nc.tensor.transpose(tp[:, i % 3, j * P:(j + 1) * P],
                                                       cnt[:, s, a + j * P:a + (j + 1) * P], k["ident"][:, :])
                        last.then_inc(turned[s], 1)

                def sums(small):
                    def add(h, s):
                        pe.wait_ge(copied[s], NS * h + NS)
                        pe.wait_ge(taken[s], h)
                        for b in range(NBK):
                            if small:
                                out, at, v = acc[:, s, 0:3 * F], ct16, parts[:, b, :, :].rearrange("p q f -> p (q f)")
                            else:
                                out, at, v = acc[:, s, 0:F], ct, val[:, b, 0:F]
                            last = nc.tensor.matmul(out, at[:, s, b * P:(b + 1) * P], v,
                                                    start=(b == 0), stop=(b == NBK - 1))
                        last.then_inc(summed[s], 1)
                    if small:
                        pe.wait_ge(split, 5)
                    ahead_fives(pe, turn, add)
                either(pe, sums)

            @block.vector
            def _(dve):
                V, TT = nc.vector, nc.vector.tensor_tensor

                def takes(small):
                    def take(h, s):
                        dve.wait_ge(summed[s], h + 1)
                        to = agg[:, bass.ds(FIVE * h + s, 1), :]
                        if not small:
                            V.tensor_copy(to, acc[:, s, 0:F].unsqueeze(1)).then_inc(taken[s], 1)
                            return
                        V.tensor_copy(to, acc[:, s, 2 * F:3 * F].unsqueeze(1)).then_inc(two, 1)
                        for q in (1, 0):
                            dve.wait_ge(two, 2 * (FIVE * h + s) + 2 - q)
                            TT(to, to, acc[:, s, q * F:(q + 1) * F].unsqueeze(1), ALU.add)\
                                .then_inc(two if q else taken[s], 1)
                    if small:
                        then = Count(dve, split)
                        then(V.tensor_copy(parts[:, :, 0, :], val[:, :, 0:F]))
                        then(TT(rest[:, :, :], val[:, :, 0:F], parts[:, :, 0, :], ALU.subtract))
                        then(V.tensor_copy(parts[:, :, 1, :], rest[:, :, :]))
                        then(TT(rest[:, :, :], rest[:, :, :], parts[:, :, 1, :], ALU.subtract))
                        then(V.tensor_copy(parts[:, :, 2, :], rest[:, :, :]))
                    over_fives(dve, take)
                either(dve, takes)


def sage_values(nc, d, k):
    with ExitStack() as ctx:
        sb, ps, sem = tools(nc, ctx)
        high = sb("sv_high", [P, NBK])
        most = sb("sv_most", [P, 1])
        row = ps("sv_row", [1, BANK])
        step, turned = sem("sv_step"), sem("sv_turned")
        steps = {}
        with nc.Block() as block:
            @block.vector
            def _(dve):
                then = Count(dve, step)
                steps["dve"] = then.at
                V, TS = nc.vector, nc.vector.tensor_scalar
                then(TS(high[:, :], k["is_pad"][:, :], -BIG, None, ALU.mult))
                then(V.tensor_tensor(high[:, :], high[:, :], k["deg"][:, :], ALU.add))
                then(V.tensor_reduce(most[:, :], high[:, :], AX.X, ALU.max), "most")
                then(TS(k["safe"][:, :, :], k["x"][:, :, :], BIG, -BIG, ALU.min, ALU.max))
                then(TS(k["inv_deg"][:, :], k["deg"][:, :], 1.0, None, ALU.max))
                then(V.reciprocal(k["inv_deg"][:, :], k["inv_deg"][:, :]))
                dve.wait_ge(turned, 1)
                then(V.tensor_reduce(high[0:1, 0:1], row[0:1, 0:P], AX.X, ALU.max))
                then(TS(k["many"][0:1, 0:1], high[0:1, 0:1], 256.0, None, ALU.is_gt))

            @block.tensor
            def _(pe):
                pe.wait_ge(step, steps["dve"]["most"])
                nc.tensor.matmul(row[0:1, 0:P], most[:, 0:1], k["ident"][:, :],
                                 start=True, stop=True).then_inc(turned, 1)


def sage_hidden(nc, d, k):
    with ExitStack() as ctx:
        sb, ps, sem = tools(nc, ctx)
        mxn = sb("sh_mxn", [P, NBK, 2 * F])
        hid = sb("sh_hid", [P, NBK, HID])
        sq = sb("sh_sq", [P, NBK, HID])
        cols = sb("sh_cols", [P, NP])
        w1 = sb("sh_w1", [2 * F, HID])
        w3 = sb("sh_w3", [HID, 2 * F])
        b1 = sb("sh_b1", [P, HID])
        col = sb("sh_col", [P, 2, NBK])
        ss, nr = (col[:, i, :] for i in range(2))
        pt = ps("sh_pt", [P, 7, BANK])
        loaded, dsem, asem, turned, evac, prod, kept = (
            sem(f"sh_{x}") for x in ("loaded", "dve", "act", "turned", "evac", "prod", "kept"))
        steps = {}
        with nc.Block() as block:
            @block.sync
            def _(sp):
                sp.dma_start(w1[0:F, :], d["W1_l"]).then_inc(loaded, 16)
                sp.dma_start(w1[F:2 * F, :], d["W1_r"]).then_inc(loaded, 16)
                sp.dma_start(w3[:, 0:F], d["W3_l"]).then_inc(loaded, 16)
                sp.dma_start(w3[:, F:2 * F], d["W3_r"]).then_inc(loaded, 16)
                sp.dma_start(b1[:, :], d["sb1"].unsqueeze(0).to_broadcast([P, HID])).then_inc(loaded, 16)

            @block.vector
            def _(dve):
                then = Count(dve, dsem)
                steps["dve"] = then.at
                then(nc.vector.tensor_tensor(mxn[:, :, 0:F], k["agg"][:, :, :], spread(k["inv_deg"][:, :]), ALU.mult))
                then(nc.vector.tensor_copy(mxn[:, :, F:2 * F], k["x"][:, :, :]), "mxn")
                dve.wait_ge(loaded, 80)
                dve.wait_ge(prod, 1)
                for g in range(7):
                    lo, hi = 4 * g, min(NBK, 4 * g + 4)
                    then(nc.vector.tensor_tensor(
                        hid[:, lo:hi, :], pt[:, g, 0:(hi - lo) * HID].rearrange("p (b f) -> p b f", f=HID),
                        b1[:, :].unsqueeze(1).to_broadcast([P, hi - lo, HID]), ALU.add))
                then(nc.vector.tensor_tensor(sq[:, :, :], hid[:, :, :], hid[:, :, :], ALU.mult))
                then(nc.vector.tensor_reduce(ss, sq[:, :, :], AX.X, ALU.add), "sq")
                dve.wait_ge(asem, 1)
                then(nc.vector.tensor_scalar(nr, nr, 1e-12, None, ALU.max))
                then(nc.vector.reciprocal(nr, nr))
                then(nc.vector.tensor_tensor(hid[:, :, :], hid[:, :, :], spread(nr, HID), ALU.mult))
                then(nc.vector.tensor_scalar(hid[:, :, :], hid[:, :, :], 0.0, None, ALU.max), "hid")
                dve.wait_ge(kept, 1)
                then(nc.vector.tensor_scalar(k["safe"][:, :, :], k["safe"][:, :, :], BIG, -BIG, ALU.min, ALU.max))

            @block.scalar
            def _(act):
                at_ = steps["dve"]
                for r in range(2):
                    act.wait_ge(turned, r + 1)
                    for i, (a, w) in enumerate(SPANS):
                        last = nc.scalar.copy(cols[:, a:a + w], pt[:, i, 0:w])
                    last.then_inc(evac, 1)
                    if r == 0:
                        act.wait_ge(dsem, at_["sq"])
                        nc.scalar.sqrt(nr, ss).then_inc(asem, 1)
                act.wait_ge(prod, 2)
                for g in range(7):
                    lo, hi = 4 * g, min(NBK, 4 * g + 4)
                    v = pt[:, g, 0:(hi - lo) * 2 * F].rearrange("p (b f) -> p b f", f=2 * F)
                    nc.scalar.copy(k["safe"][:, lo:hi, :], v[:, :, 0:F])
                    last = nc.scalar.copy(k["hr"][:, lo:hi, :], v[:, :, F:2 * F])
                last.then_inc(kept, 1)

            @block.tensor
            def _(pe):
                at_ = steps["dve"]
                pe.wait_ge(loaded, 80)
                for r, (rows, w, name) in enumerate(((mxn, w1, "mxn"), (hid, w3, "hid"))):
                    pe.wait_ge(dsem, at_[name])
                    turn_blocks(pe, nc, k, pt, rows, P, turned)
                    pe.wait_ge(evac, r + 1)
                    for b in range(NBK):
                        last = nc.tensor.matmul(pt[:, b // 4, (b % 4) * P:(b % 4 + 1) * P], cols[:, b * P:(b + 1) * P],
                                                w[:, :], start=True, stop=True)
                    last.then_inc(prod, 1)


def sage_out(nc, d, k):
    with ExitStack() as ctx:
        sb, ps, sem = tools(nc, ctx)
        b3 = sb("so_b3", [P, F])
        t = sb("so_t", [P, NBK, F])
        col = sb("so_col", [P, 3, NBK])
        nr, t1, t2 = (col[:, i, :] for i in range(3))
        loaded, dsem, asem, stored = (sem(f"so_{x}") for x in ("loaded", "dve", "act", "stored"))
        x, agg = k["x"], k["agg"]
        steps = {}
        whole = N // P
        with nc.Block() as block:
            @block.vector
            def _(dve):
                then = Count(dve, dsem)
                steps["dve"] = then.at
                TT = nc.vector.tensor_tensor
                then(TT(agg[:, :, :], agg[:, :, :], spread(k["inv_deg"][:, :]), ALU.mult))
                then(TT(agg[:, :, :], agg[:, :, :], k["hr"][:, :, :], ALU.add))
                dve.wait_ge(loaded, 16)
                then(TT(agg[:, :, :], agg[:, :, :], b3[:, :].unsqueeze(1).to_broadcast([P, NBK, F]), ALU.add))
                then(TT(x[:, :, :], x[:, :, :], agg[:, :, :], ALU.add))
                layernorm_stats(nc, then, x[:, :, :], t, t1, t2, "var")
                dve.wait_ge(asem, 1)
                then(nc.vector.reciprocal(t1, nr))
                then(TT(x[:, :, :], x[:, :, :], spread(t1), ALU.mult), "x")

            @block.scalar
            def _(act):
                finish_norm(nc, act, dsem, steps["dve"], asem, nr, t2)

            @block.sync
            def _(sp):
                sp.dma_start(b3[:, :], d["sb3"].unsqueeze(0).to_broadcast([P, F])).then_inc(loaded, 16)
                sp.wait_ge(dsem, steps["dve"]["x"])
                sp.dma_start(d["out"][0:whole * P, :].rearrange("(b p) f -> p b f", p=P),
                             x[:, 0:whole, :]).then_inc(stored, 16)
                sp.dma_start(d["out"][whole * P:N, :], x[0:N - whole * P, whole, :]).then_inc(stored, 16)
                sp.wait_ge(stored, 32)


def graph_net_kernel(nc, d):
    for name, shape, dt in (("counts", (NP, NP), F32), ("near", (NP, NP), F32),
                            ("starts", (2, EP // 2), BF16), ("w23", (NP, 2 * F), F32), ("dnet", (P, EP // 2), F32),
                            ("rows", (EP, ROW), F32), ("src", (EP,), I32), ("dst", (EP + 1,), I32),
                            ("attr8", (8, EP // 2), F32)):
        d[name] = nc.dram_tensor(name, shape, dt, kind="Internal").ap()
    k = {}
    with ExitStack() as ctx:
        def keep(stack, *what):
            for name, shape, dt in what:
                k[name] = stack.enter_context(nc.sbuf_tensor(name, shape, dt))

        keep(ctx, ("ident", [P, P], F32), ("ones", [P, P], F32), ("upper", [P, P], F32), ("zeros", [P, BANK], F32),
             ("ones16", [P, 2], F16), ("is_pad", [P, NBK], F32), ("half_sel", [2, P], F32), ("blk_first", [P, NBK], F32),
             ("src_idx", [P, NT + 2 * CT], I32), ("deg", [P, NBK], F32), ("x", [P, NBK, F], F32), ("cc", [P, 5], F32),
             ("unsorted", [1, 1], I32),
             ("many", [1, 1], I32), ("w1x", [P, NBK, F], F32))
        with ExitStack() as build:
            keep(build, ("iota16", [P, NP], F16), ("iota_blk", [P, P], F16),
                 ("blk1", [8, P], F32), ("blk2", [P, P], F32), ("avg", [P, P], F32),
                 ("pc", [P, 5], F32),
                 ("eps", [P, 1], F32))
            constants(nc, k)
            take_edges(nc, d, k)
            sort_edges(nc, d, k)
            keep(build, ("src_col", [P, NT], F32),
                 ("dst_col", [P, NT], F32), ("src_sh", [P, NT], F32), ("pairs", [1, NBK], I32))
            edge_tables(nc, d, k)
            counts_and_network(nc, d, k)
        with ExitStack() as dense:
            keep(dense, ("val", [P, NBK, W65], F32), ("toprow", [P, NP], F32), ("sdst", [P, 2, NBK], F32),
                 ("hT", [W66, 2, NP], F32))
            k["sums"] = k["hT"][:, 0, :]
            hyperbolic_nodes(nc, d, k)
            pair_distances(nc, d, k)
            near_sums(nc, d, k)
            end_hyperbolic(nc, d, k)
            attention_rows(nc, d, k)
            score_sums(nc, d, k)
            end_attention(nc, d, k)
        edge_softmax(nc, d, k)
        end_edges(nc, d, k)
        keep(ctx, ("safe", [P, NBK, F], F32), ("inv_deg", [P, NBK], F32), ("agg", [P, NBK, F], F32),
             ("hr", [P, NBK, F], F32))
        sage_values(nc, d, k)
        sum_neighbours(nc, d, k, "n1", k["safe"], k["agg"])
        sage_hidden(nc, d, k)
        sum_neighbours(nc, d, k, "n2", k["safe"], k["agg"])
        sage_out(nc, d, k)


_NAMES = {"c": "L0_gnn_c", "W0": "L0_gnn_W", "W1": "L1_gnn_W", "a1": "L1_gnn_a", "Wd1": "L2_gnn_Wd1",
          "bd1": "L2_gnn_bd1", "g1": "L2_gnn_g1", "b1": "L2_gnn_b1", "Wd2": "L2_gnn_Wd2", "bd2": "L2_gnn_bd2",
          "g2": "L2_gnn_g2", "b2": "L2_gnn_b2", "W2_1": "L2_gnn_W1", "W2_2": "L2_gnn_W2", "W2_3": "L2_gnn_W3",
          "W1_l": "L3_gnn_W1_l", "W1_r": "L3_gnn_W1_r", "sb1": "L3_gnn_b1", "W3_l": "L3_gnn_W3_l",
          "W3_r": "L3_gnn_W3_r", "sb3": "L3_gnn_b3"}


def kernel(**inputs):
    import concourse.bacc as _bacc
    from concourse.bass_utils import run_bass_kernel_spmd as _run

    nc = _bacc.Bacc("TRN2", target_bir_lowering=False, num_devices=1)
    src = np.full((EP,), PADN, np.int32)
    src[0:E] = inputs["src"]
    dst = np.full((EP + 1,), PADN, np.int32)
    dst[0] = -1
    dst[1:E + 1] = inputs["dst"]
    x = np.ones((NP, F), np.float32)
    x[0:N] = inputs["x"]
    attr = np.zeros((2, 4, EP // 2), np.float32)
    attr[:, 3] = 1.0
    attr[0, 0:3] = inputs["edge_attr_3"][0:EP // 2].T
    attr[1, 0:3, 0:E - EP // 2] = inputs["edge_attr_3"][EP // 2:E].T
    arrays = {"src_given": src, "dst_given": dst, "x_in": x, "attr_given": attr.reshape(8, EP // 2)}
    for name, given in _NAMES.items():
        arrays[name + "_in"] = np.ascontiguousarray(inputs[given])
    d = {}
    for name, a in arrays.items():
        t = nc.dram_tensor(name, a.shape, mybir.dt.from_np(a.dtype), kind="ExternalInput").ap()
        d[name.removesuffix("_in")] = t
    d["out"] = nc.dram_tensor("out_0_dram", (N, F), F32, kind="ExternalOutput").ap()
    graph_net_kernel(nc, d)
    r = _run(nc, [arrays], core_ids=[0])
    return r.results[0]["out_0_dram"]
```
